# Optimizing a Trainium2 kernel written in Bass

```python
import numpy as np
import jax
import jax.numpy as jnp

def _softmax(x, axis=-1):
    return jax.nn.softmax(x, axis=axis)

def _gelu(x):
    return jax.nn.gelu(x, approximate=True)

def _silu(x):
    return jax.nn.silu(x)

def _sigmoid(x):
    return jax.nn.sigmoid(x)

def _layernorm(x, axis=-1, eps=1e-05):
    m = jnp.mean(x, axis=axis, keepdims=True)
    v = jnp.var(x, axis=axis, keepdims=True)
    return (x - m) / jnp.sqrt(v + eps)

def _scatter_add(tgt, idx, src, axis=0):
    return tgt.at[idx].add(src)

def _segment_sum(src, seg, n):
    return jax.ops.segment_sum(src, seg, n)
kernel_name = 'mk_xattn_ffn_d2_seqx_r4_6cc0a0'

def setup_inputs(seed: int=0):
    np.random.seed(seed)
    _w = jnp.asarray

    def _rec_inputs():
        import jax
        import jax.numpy as jnp
        _rk = jax.random.key(seed)
        x = 7.22e-05 + 1 * jax.random.normal(jax.random.fold_in(_rk, 1), (4, 512, 256), jnp.float32)
        _lenS = 512 - jax.random.randint(jax.random.fold_in(_rk, 7), (4,), 0, max(1, 512 // 4) + 1, jnp.int32)
        _lenS2 = 1024 - jax.random.randint(jax.random.fold_in(_rk, 8), (4,), 0, max(1, 1024 // 4) + 1, jnp.int32)
        _ctx_768P = jax.random.normal(jax.random.fold_in(_rk, 11), (4, 16, 192), jnp.float32)
        _ctx_768c = jax.random.dirichlet(jax.random.fold_in(_rk, 511), 0.3 * jnp.ones((16,), jnp.float32), (4, 1024))
        _ctx_768t = jnp.einsum('bsk,bkd->bsd', _ctx_768c, _ctx_768P)
        _ctx_768t = _ctx_768t * jax.lax.rsqrt(jnp.mean(jnp.square(_ctx_768t)) + 1e-12) * 0.953939
        ctx_768 = -0.000191848 + 0.999787 * (_ctx_768t + 0.3 * jax.random.normal(jax.random.fold_in(_rk, 611), (4, 1024, 192), jnp.float32))
        return (x, ctx_768)
    x, ctx_768 = _rec_inputs()

    def _L0_xattn_setup():
        import jax, jax.numpy as jnp
        import numpy as np
        HEADS = 16
        DIM_HEAD = 64
        QUERY_DIM = 256
        CONTEXT_DIM = 192
        INNER = HEADS * DIM_HEAD
        SCALE = DIM_HEAD ** (-0.5)
        key = jax.random.key(seed)
        ks = jax.random.split(key, 7)
        B, Sq, Skv = (4, 512, 512)
        x = jax.random.normal(ks[0], (B, Sq, QUERY_DIM), dtype=jnp.float32)
        context = jax.random.normal(ks[1], (B, Skv, CONTEXT_DIM), dtype=jnp.float32)
        w_q = jax.random.normal(ks[2], (QUERY_DIM, INNER), dtype=jnp.float32) / np.sqrt(QUERY_DIM)
        w_k = jax.random.normal(ks[3], (CONTEXT_DIM, INNER), dtype=jnp.float32) / np.sqrt(CONTEXT_DIM)
        w_v = jax.random.normal(ks[4], (CONTEXT_DIM, INNER), dtype=jnp.float32) / np.sqrt(CONTEXT_DIM)
        w_o = jax.random.normal(ks[5], (INNER, QUERY_DIM), dtype=jnp.float32) / np.sqrt(INNER)
        b_o = jax.random.normal(ks[6], (QUERY_DIM,), dtype=jnp.float32) * 0.02
        return {'x': x, 'context': context, 'w_q': w_q, 'w_k': w_k, 'w_v': w_v, 'w_o': w_o, 'b_o': b_o}
    _L0_xattn_all = _L0_xattn_setup()
    _L0_xattn_in = {k: v for k, v in _L0_xattn_all.items() if k in ('w_q', 'w_k', 'w_v', 'w_o', 'b_o')}
    del _L0_xattn_all

    def _L0_ffn_setup():
        import jax, jax.numpy as jnp
        import numpy as np
        H = 256
        I = 128
        E = 32
        TOP_K = 6
        N_GROUP = 8
        TOPK_GROUP = 4
        SCALE = 2.5
        N_SHARED = 2
        SI = I * N_SHARED
        B, S = (2, 256)
        key = jax.random.key(seed)
        ks = jax.random.split(key, 8)
        x = jax.random.normal(ks[0], (B, S, H), jnp.float32)
        gate_weight = jax.random.normal(ks[1], (E, H), jnp.float32) * 0.02
        e_score_correction_bias = jax.random.normal(ks[2], (E,), jnp.float32) * 0.01
        experts_gate_up = jax.random.normal(ks[3], (E, 2 * I, H), jnp.float32) * 0.02
        experts_down = jax.random.normal(ks[4], (E, H, I), jnp.float32) * 0.02
        shared_gate_w = jax.random.normal(ks[5], (SI, H), jnp.float32) * 0.02
        shared_up_w = jax.random.normal(ks[6], (SI, H), jnp.float32) * 0.02
        shared_down_w = jax.random.normal(ks[7], (H, SI), jnp.float32) * 0.02
        return {'x': x, 'gate_weight': gate_weight, 'e_score_correction_bias': e_score_correction_bias, 'experts_gate_up': experts_gate_up, 'experts_down': experts_down, 'shared_gate_w': shared_gate_w, 'shared_up_w': shared_up_w, 'shared_down_w': shared_down_w}
    _L0_ffn_all = _L0_ffn_setup()
    _L0_ffn_in = {k: v for k, v in _L0_ffn_all.items() if k in ('gate_weight', 'e_score_correction_bias', 'experts_gate_up', 'experts_down', 'shared_gate_w', 'shared_up_w', 'shared_down_w')}
    del _L0_ffn_all

    def _L1_xattn_setup():
        import jax, jax.numpy as jnp
        import numpy as np
        HEADS = 16
        DIM_HEAD = 64
        SCALE = DIM_HEAD ** (-0.5)
        QUERY_DIM = 256
        CONTEXT_DIM = 192
        INNER_DIM = HEADS * DIM_HEAD
        key = jax.random.key(seed)
        ks = jax.random.split(key, 7)
        B, Nq, Nk = (8, 1024, 77)
        x = jax.random.normal(ks[0], (B, Nq, QUERY_DIM), dtype=jnp.float32)
        context = jax.random.normal(ks[1], (B, Nk, CONTEXT_DIM), dtype=jnp.float32)
        Wq = jax.random.normal(ks[2], (QUERY_DIM, INNER_DIM), dtype=jnp.float32) * QUERY_DIM ** (-0.5)
        Wk = jax.random.normal(ks[3], (CONTEXT_DIM, INNER_DIM), dtype=jnp.float32) * CONTEXT_DIM ** (-0.5)
        Wv = jax.random.normal(ks[4], (CONTEXT_DIM, INNER_DIM), dtype=jnp.float32) * CONTEXT_DIM ** (-0.5)
        Wo = jax.random.normal(ks[5], (INNER_DIM, QUERY_DIM), dtype=jnp.float32) * INNER_DIM ** (-0.5)
        bo = jnp.zeros((QUERY_DIM,), dtype=jnp.float32)
        return {'x': x, 'context': context, 'Wq': Wq, 'Wk': Wk, 'Wv': Wv, 'Wo': Wo, 'bo': bo}
    _L1_xattn_all = _L1_xattn_setup()
    _L1_xattn_in = {k: v for k, v in _L1_xattn_all.items() if k in ('Wq', 'Wk', 'Wv', 'Wo', 'bo')}
    del _L1_xattn_all

    def _L1_ffn_setup():
        import jax, jax.numpy as jnp
        import numpy as np
        B, T, C, H, E = (1, 64, 256, 512, 8)
        STD = 0.02
        key = jax.random.key(seed)
        ks = jax.random.split(key, 8)
        f32 = jnp.float32
        return {'x': jax.random.normal(ks[0], (B, T, C), f32), 'up': jax.random.normal(ks[1], (E, H, C), f32) * STD, 'gate': jax.random.normal(ks[2], (E, H, C), f32) * STD, 'down': jax.random.normal(ks[3], (E, C, H), f32) * STD, 'router': jax.random.normal(ks[4], (E, C), f32) * STD, 'w_up_s': jax.random.normal(ks[5], (H, C), f32) * STD, 'w_gate_s': jax.random.normal(ks[6], (H, C), f32) * STD, 'w_down_s': jax.random.normal(ks[7], (C, H), f32) * STD}
    _L1_ffn_all = _L1_ffn_setup()
    _L1_ffn_in = {k: v for k, v in _L1_ffn_all.items() if k in ('up', 'gate', 'down', 'router', 'w_up_s', 'w_gate_s', 'w_down_s')}
    del _L1_ffn_all
    return {'x': x, 'ctx_768': ctx_768, 'L0_xattn_w_q': _L0_xattn_in['w_q'], 'L0_xattn_w_k': _L0_xattn_in['w_k'], 'L0_xattn_w_v': _L0_xattn_in['w_v'], 'L0_xattn_w_o': _L0_xattn_in['w_o'], 'L0_xattn_b_o': _L0_xattn_in['b_o'], 'L0_ffn_gate_weight': _L0_ffn_in['gate_weight'], 'L0_ffn_e_score_correction_bias': _L0_ffn_in['e_score_correction_bias'], 'L0_ffn_experts_gate_up': _L0_ffn_in['experts_gate_up'], 'L0_ffn_experts_down': _L0_ffn_in['experts_down'], 'L0_ffn_shared_gate_w': _L0_ffn_in['shared_gate_w'], 'L0_ffn_shared_up_w': _L0_ffn_in['shared_up_w'], 'L0_ffn_shared_down_w': _L0_ffn_in['shared_down_w'], 'L1_xattn_Wq': _L1_xattn_in['Wq'], 'L1_xattn_Wk': _L1_xattn_in['Wk'], 'L1_xattn_Wv': _L1_xattn_in['Wv'], 'L1_xattn_Wo': _L1_xattn_in['Wo'], 'L1_xattn_bo': _L1_xattn_in['bo'], 'L1_ffn_up': _L1_ffn_in['up'], 'L1_ffn_gate': _L1_ffn_in['gate'], 'L1_ffn_down': _L1_ffn_in['down'], 'L1_ffn_router': _L1_ffn_in['router'], 'L1_ffn_w_up_s': _L1_ffn_in['w_up_s'], 'L1_ffn_w_gate_s': _L1_ffn_in['w_gate_s'], 'L1_ffn_w_down_s': _L1_ffn_in['w_down_s']}

def reference(x, ctx_768, L0_xattn_w_q, L0_xattn_w_k, L0_xattn_w_v, L0_xattn_w_o, L0_xattn_b_o, L0_ffn_gate_weight, L0_ffn_e_score_correction_bias, L0_ffn_experts_gate_up, L0_ffn_experts_down, L0_ffn_shared_gate_w, L0_ffn_shared_up_w, L0_ffn_shared_down_w, L1_xattn_Wq, L1_xattn_Wk, L1_xattn_Wv, L1_xattn_Wo, L1_xattn_bo, L1_ffn_up, L1_ffn_gate, L1_ffn_down, L1_ffn_router, L1_ffn_w_up_s, L1_ffn_w_gate_s, L1_ffn_w_down_s):
    import jax
    import jax.numpy as jnp

    def _L0_xattn_ref(x, context, w_q, w_k, w_v, w_o, b_o):
        import jax, jax.numpy as jnp
        import numpy as np
        HEADS = 16
        DIM_HEAD = 64
        QUERY_DIM = 256
        CONTEXT_DIM = 192
        INNER = HEADS * DIM_HEAD
        SCALE = DIM_HEAD ** (-0.5)
        B, Sq, _ = x.shape
        Skv = context.shape[1]
        q = (x @ w_q).reshape(B, Sq, HEADS, DIM_HEAD).transpose(0, 2, 1, 3)
        k = (context @ w_k).reshape(B, Skv, HEADS, DIM_HEAD).transpose(0, 2, 1, 3)
        v = (context @ w_v).reshape(B, Skv, HEADS, DIM_HEAD).transpose(0, 2, 1, 3)
        sim = jnp.einsum('bhid,bhjd->bhij', q, k) * SCALE
        attn = jax.nn.softmax(sim, axis=-1)
        out = jnp.einsum('bhij,bhjd->bhid', attn, v)
        out = out.transpose(0, 2, 1, 3).reshape(B, Sq, INNER)
        return out @ w_o + b_o

    def _L0_ffn_ref(x, gate_weight, e_score_correction_bias, experts_gate_up, experts_down, shared_gate_w, shared_up_w, shared_down_w):
        import jax, jax.numpy as jnp
        import numpy as np
        H = 256
        I = 128
        E = 32
        TOP_K = 6
        N_GROUP = 8
        TOPK_GROUP = 4
        SCALE = 2.5
        N_SHARED = 2
        SI = I * N_SHARED
        B, S = (2, 256)
        b, s, h = x.shape
        xf = x.reshape(-1, h)
        T = xf.shape[0]
        logits = xf.astype(jnp.float32) @ gate_weight.astype(jnp.float32).T
        scores = jax.nn.sigmoid(logits)
        sfc = scores + e_score_correction_bias[None, :]
        gs = E // N_GROUP
        group_scores = sfc.reshape(T, N_GROUP, gs).max(axis=-1)
        _, gidx = jax.lax.top_k(group_scores, TOPK_GROUP)
        gmask = jnp.zeros((T, N_GROUP), bool).at[jnp.arange(T)[:, None], gidx].set(True)
        smask = jnp.repeat(gmask, gs, axis=1)
        masked = jnp.where(smask, sfc, 0.0)
        _, topk_idx = jax.lax.top_k(masked, TOP_K)
        tw = jnp.take_along_axis(scores, topk_idx, axis=1)
        tw = tw / (tw.sum(-1, keepdims=True) + 1e-20)
        tw = (tw * SCALE).astype(xf.dtype)
        combine = jnp.zeros((T, E), xf.dtype).at[jnp.arange(T)[:, None], topk_idx].add(tw)

        def expert_step(acc, inp):
            gu, dn, c = inp
            g = xf @ gu[:I].T
            u = xf @ gu[I:].T
            o = jax.nn.silu(g) * u @ dn.T
            return (acc + c[:, None] * o, None)
        routed, _ = jax.lax.scan(expert_step, jnp.zeros_like(xf), (experts_gate_up, experts_down, combine.T))
        sh = jax.nn.silu(xf @ shared_gate_w.T) * (xf @ shared_up_w.T)
        shared_out = sh @ shared_down_w.T
        return (routed + shared_out).reshape(b, s, h)

    def _L1_xattn_ref(x, context, Wq, Wk, Wv, Wo, bo):
        import jax, jax.numpy as jnp
        import numpy as np
        HEADS = 16
        DIM_HEAD = 64
        SCALE = DIM_HEAD ** (-0.5)
        QUERY_DIM = 256
        CONTEXT_DIM = 192
        INNER_DIM = HEADS * DIM_HEAD
        B, Nq, _ = x.shape
        Nk = context.shape[1]
        q = x @ Wq
        k = context @ Wk
        v = context @ Wv
        q = q.reshape(B, Nq, HEADS, DIM_HEAD).transpose(0, 2, 1, 3)
        k = k.reshape(B, Nk, HEADS, DIM_HEAD).transpose(0, 2, 1, 3)
        v = v.reshape(B, Nk, HEADS, DIM_HEAD).transpose(0, 2, 1, 3)
        sim = jnp.einsum('bhid,bhjd->bhij', q, k) * SCALE
        attn = jax.nn.softmax(sim, axis=-1)
        out = jnp.einsum('bhij,bhjd->bhid', attn, v)
        out = out.transpose(0, 2, 1, 3).reshape(B, Nq, INNER_DIM)
        return out @ Wo + bo

    def _L1_ffn_ref(x, up, gate, down, router, w_up_s, w_gate_s, w_down_s):
        import jax, jax.numpy as jnp
        import numpy as np
        B, T, C, H, E = (1, 64, 256, 512, 8)
        STD = 0.02
        b, t, c = x.shape
        x_ = x.reshape(b * t, c)
        logits = x_ @ router.T
        idx = jnp.argmax(logits, axis=-1)
        onehot = jax.nn.one_hot(idx, router.shape[0], dtype=x.dtype)
        u = jnp.einsum('bc,ehc->ebh', x_, up)
        g = jnp.einsum('bc,ehc->ebh', x_, gate)
        h = jax.nn.silu(g) * u
        ye = jnp.einsum('ebh,ech->ebc', h, down)
        y = jnp.einsum('ebc,be->bc', ye, onehot)
        ys = jax.nn.silu(x_ @ w_gate_s.T) * (x_ @ w_up_s.T) @ w_down_s.T
        return (y + ys).reshape(b, t, c)
    x = x + _L0_xattn_ref(_layernorm(x, axis=-1), ctx_768, L0_xattn_w_q, L0_xattn_w_k, L0_xattn_w_v, L0_xattn_w_o, L0_xattn_b_o)
    x = x + _L0_ffn_ref(_layernorm(x, axis=-1), L0_ffn_gate_weight, L0_ffn_e_score_correction_bias, L0_ffn_experts_gate_up, L0_ffn_experts_down, L0_ffn_shared_gate_w, L0_ffn_shared_up_w, L0_ffn_shared_down_w)
    x = x + _L1_xattn_ref(_layernorm(x, axis=-1), ctx_768, L1_xattn_Wq, L1_xattn_Wk, L1_xattn_Wv, L1_xattn_Wo, L1_xattn_bo)
    x = x + _L1_ffn_ref(_layernorm(x, axis=-1), L1_ffn_up, L1_ffn_gate, L1_ffn_down, L1_ffn_router, L1_ffn_w_up_s, L1_ffn_w_gate_s, L1_ffn_w_down_s)
    return x

_drawn_inputs = setup_inputs


def setup_inputs(seed=0):
    import zlib

    import numpy as np

    out = dict(_drawn_inputs(seed))
    spreads = {'L1_xattn_bo': (0.0, 0.1)}
    factors = {'L0_xattn_b_o': 3.829,
     'L0_ffn_gate_weight': 7.188,
     'L0_ffn_e_score_correction_bias': 8.0,
     'L0_ffn_experts_gate_up': 6.471,
     'L0_ffn_experts_down': 6.431,
     'L0_ffn_shared_gate_w': 4.672,
     'L0_ffn_shared_up_w': 4.646,
     'L0_ffn_shared_down_w': 4.629,
     'L1_ffn_up': 3.446,
     'L1_ffn_gate': 3.465,
     'L1_ffn_down': 3.426,
     'L1_ffn_router': 3.673,
     'L1_ffn_w_up_s': 3.297,
     'L1_ffn_w_gate_s': 3.302,
     'L1_ffn_w_down_s': 3.291}
    for name, (base, spread) in spreads.items():
        noise = np.random.default_rng([zlib.crc32(name.encode()), seed]).standard_normal(out[name].shape)
        drawn = base * np.exp(spread * noise) if base else spread * noise
        out[name] = jnp.asarray(drawn.astype(out[name].dtype))
    for name, factor in factors.items():
        out[name] = (out[name] * factor).astype(out[name].dtype)
    return out
```

```python
import concourse.bass as bass
from concourse import mybir
from contextlib import ExitStack

F32 = mybir.dt.float32
F32R = mybir.dt.float32r
ALU = mybir.AluOpType
ACT = mybir.ActivationFunctionType
AX = mybir.AxisListType
ds = bass.ds

P = 128
BATCH, SEQ, DIM = 4, 512, 256
SKV, CTXD = 1024, 192
HEADS, DH = 16, 64
TOK = BATCH * SEQ
NT = TOK // P
KD = DIM // P
HP = HEADS // 2
QT = SEQ // P
KVT = SKV // P
WCOL = (KD + 4) * P
MCOL = 2 * KD * P + DIM
BANK = 512
BLK = TOK // BANK
SCALE = DH ** -0.5
EPS = 1e-5

LAYERS = [
    dict(experts=32, per=1, shared=2, groups=8, top_groups=4, top=6, scale=2.5),
    dict(experts=8, per=4, shared=4, groups=0, top_groups=0, top=1, scale=1.0),
]


def build(nc, x, ctx_top, ctx_bot, layer_in, out):
    stack = ExitStack()

    def scope():
        return ExitStack()

    with stack:
        def sb(where, name, shape, dt=F32):
            return where.enter_context(nc.sbuf_tensor(name, shape, dt))

        def sems(where, prefix, names):
            return {n: where.enter_context(nc.semaphore(f"{prefix}_{n}")) for n in names.split()}

        ident = sb(stack, "ident", [P, P])
        nident = sb(stack, "nident", [P, P])
        ones = sb(stack, "ones", [P, DH])
        ctx_hi = sb(stack, "ctx_hi", [P, BATCH * SKV], F32R)
        ctx_lo = sb(stack, "ctx_lo", [P, BATCH * SKV], F32R)
        ctx_hl = sb(stack, "ctx_hl", [P, BATCH * SKV], F32R)
        xnT_hi = sb(stack, "xnT_hi", [P, KD, TOK], F32R)
        xnT_lo = sb(stack, "xnT_lo", [P, KD, TOK], F32R)
        psum = stack.enter_context(nc.psum_tensor("psum", [P, 8 * BANK], F32))
        heads_out = nc.dram_tensor("heads_out", (HP, P, TOK), F32, kind="Internal").ap()
        x_mid = nc.dram_tensor("x_mid", (TOK, DIM), F32, kind="Internal").ap()
        x_tiles = x.rearrange("(t p) d -> p t d", p=P)
        mid_tiles = x_mid.rearrange("(t p) d -> p t d", p=P)
        out_tiles = out.rearrange("(t p) d -> p t d", p=P)

        def bank(n, width=BANK):
            return psum[:, n * BANK:n * BANK + width]

        with scope() as s:
            stage = sb(s, "ctx_stage", [P, 2, SKV])
            sem = sems(s, "c", "id staged0 staged1 hi lo")
            with nc.Block() as block:
                NCH = 2 * BATCH

                @block.gpsimd
                def _(pool):
                    nc.gpsimd.memset(ident[:, :], 0.0).then_inc(sem["id"], 1)
                    nc.gpsimd.memset(nident[:, :], 0.0).then_inc(sem["id"], 1)
                    nc.gpsimd.memset(ones[:, :], 1.0).then_inc(sem["id"], 1)
                    pool.wait_ge(sem["id"], 3)
                    for m, v in ((ident, 1.0), (nident, -1.0)):
                        nc.gpsimd.affine_select(out=m[:, :], in_=m[:, :], compare_op=ALU.not_equal, fill=v, base=0,
                                                pattern=[[-1, P]], channel_multiplier=1).then_inc(sem["id"], 1)

                @block.sync
                def _(sp):
                    for n in range(NCH):
                        if n >= 2:
                            sp.wait_ge(sem["lo"], n - 1)
                        src = ctx_top if n < BATCH else ctx_bot
                        cols = slice((n % BATCH) * SKV, (n % BATCH + 1) * SKV)
                        sp.dma_start(stage[:, n % 2, :], src[:, cols]).then_inc(sem[f"staged{n % 2}"], 16)

                @block.scalar
                def _(act):
                    for n in range(NCH):
                        cols = slice((n % BATCH) * SKV, (n % BATCH + 1) * SKV)
                        act.wait_ge(sem[f"staged{n % 2}"], 16 * (n // 2 + 1))
                        dst = ctx_hi if n < BATCH else ctx_hl
                        nc.scalar.activation(dst[:, cols], stage[:, n % 2, :], ACT.Copy).then_inc(sem["hi"], 1)

                @block.vector
                def _(dve):
                    for n in range(NCH):
                        cols = slice((n % BATCH) * SKV, (n % BATCH + 1) * SKV)
                        dve.wait_ge(sem["hi"], n + 1)
                        if n < BATCH:
                            nc.vector.tensor_tensor(ctx_lo[:, cols], stage[:, n % 2, :], ctx_hi[:, cols],
                                                    ALU.subtract).then_inc(sem["lo"], 1)
                        else:
                            nc.vector.tensor_tensor(ctx_hl[DH:P, cols], stage[DH:P, n % 2, :], ctx_hl[DH:P, cols],
                                                    ALU.subtract).then_inc(sem["lo"], 1)

        def norm_phase(tag, xres, source, proj):
            with scope() as s:
                stats = sb(s, tag + "stats", [P, NT, 6])
                mean = sb(s, tag + "mean", [P, NT])
                var = sb(s, tag + "var", [P, NT])
                dif = sb(s, tag + "dif", [P, NT])
                std = sb(s, tag + "std", [P, NT])
                rstd = sb(s, tag + "rstd", [P, NT])
                xn = sb(s, tag + "xn", [P, 2, DIM])
                if proj:
                    wo, bias = proj
                    wo_sb = sb(s, tag + "wo", [P, HP, DIM])
                    bias_sb = sb(s, tag + "bias", [P, DIM])
                    heads = sb(s, tag + "heads", [P, 2, HP, P])
                sem = sems(s, tag, "x w heads0 heads1 biased proj added stat batch sqrt xn tr hi lo")
                with nc.Block() as block:

                    @block.sync
                    def _(sp):
                        if source is not None:
                            sp.dma_start(xres[:, :, :], source).then_inc(sem["x"], 16)
                        if proj:
                            sp.dma_start(wo_sb[:, :, :], wo).then_inc(sem["w"], 16)
                            sp.dma_start(bias_sb[:, :], bias.partition_broadcast(P)).then_inc(sem["w"], 16)
                            with sp.Fori(0, NT // 2) as j:
                                for par in range(2):
                                    t = j * 2 + par
                                    sp.wait_ge(sem["proj"], t + 1)
                                    sp.dma_start(heads[:, par, :, :], heads_out[:, :, ds(t * P, P)].rearrange("h p t -> p h t"))\
                                        .then_inc(sem[f"heads{par}"], 16)

                    @block.gpsimd
                    def _(pool):
                        if proj:
                            pool.wait_ge(sem["w"], 32)
                            pool.wait_ge(sem["x"], 16)
                            with pool.Fori(0, NT) as t:
                                nc.gpsimd.tensor_tensor(xres[:, ds(t, 1), :].rearrange("p a d -> p (a d)"),
                                                        xres[:, ds(t, 1), :].rearrange("p a d -> p (a d)"),
                                                        bias_sb[:, :], ALU.add).then_inc(sem["biased"], 1)

                    @block.scalar
                    def _(act):
                        act.wait_ge(sem["batch"], 8)
                        nc.scalar.activation(std[:, :], var[:, :], ACT.Sqrt).then_inc(sem["sqrt"], 1)
                        with act.Fori(0, NT // 2) as j:
                            for par in range(2):
                                t = j * 2 + par
                                act.wait_ge(sem["tr"], t + 1)
                                nc.scalar.activation(xnT_hi[:, :, ds(t * P, P)],
                                                     bank(2 + par, DIM).rearrange("p (k t) -> p k t", k=KD),
                                                     ACT.Copy).then_inc(sem["hi"], 1)

                    @block.tensor
                    def _(pe):
                        if proj:
                            pe.sem_inc(sem["proj"], 2)
                            pe.wait_ge(sem["w"], 32)
                            with pe.Fori(0, NT // 2) as j:
                                for par in range(2):
                                    t = j * 2 + par
                                    pe.wait_ge(sem[f"heads{par}"], j * 16 + 16)
                                    pe.wait_ge(sem["added"], t + 1)
                                    for h in range(HP):
                                        last = nc.tensor.matmul(bank(par, DIM), heads[:, par, h, :], wo_sb[:, h, :],
                                                                start=h == 0, stop=h == HP - 1)
                                    last.then_inc(sem["proj"], 1)
                        with pe.Fori(0, NT // 2) as j:
                            for par in range(2):
                                t = j * 2 + par
                                pe.wait_ge(sem["xn"], t + 1)
                                pe.wait_ge(sem["lo"], t + 1)
                                for k in range(KD):
                                    last = nc.tensor.transpose(bank(2 + par)[:, k * P:(k + 1) * P],
                                                               xn[:, par, k * P:(k + 1) * P], ident[:, :])
                                last.then_inc(sem["tr"], 1)

                    @block.vector
                    def _(dve):
                        dve.sem_inc(sem["added"], 2)
                        dve.sem_inc(sem["lo"], 2)
                        if source is not None:
                            dve.wait_ge(sem["x"], 16)
                        with dve.Fori(0, NT // 2) as j:
                            for par in range(2):
                                t = j * 2 + par
                                row = xres[:, ds(t, 1), :].rearrange("p a d -> p (a d)")
                                if proj:
                                    dve.wait_ge(sem["biased"], t + 1)
                                    dve.wait_ge(sem["proj"], t + 3)
                                    nc.vector.tensor_tensor(row, bank(par, DIM), row, ALU.add).then_inc(sem["added"], 1)
                                    dve.wait_ge(sem["added"], t + 3)
                                nc.vector.bn_stats(stats[:, ds(t, 1), :].rearrange("p a d -> p (a d)"), row)\
                                    .then_inc(sem["stat"], 1)
                        dve.wait_ge(sem["stat"], NT)
                        n = 0

                        def link(ins):
                            nonlocal n
                            n += 1
                            ins.then_inc(sem["batch"], 1)
                            dve.wait_ge(sem["batch"], n)

                        me, se, mo, so = (stats[:, :, i] for i in (1, 2, 4, 5))
                        link(nc.vector.tensor_tensor(mean[:, :], me, mo, ALU.add))
                        link(nc.vector.tensor_scalar(mean[:, :], mean[:, :], 0.5, None, ALU.mult))
                        link(nc.vector.tensor_tensor(dif[:, :], me, mo, ALU.subtract))
                        link(nc.vector.tensor_tensor(dif[:, :], dif[:, :], dif[:, :], ALU.mult))
                        link(nc.vector.tensor_scalar(dif[:, :], dif[:, :], DIM / 4.0, None, ALU.mult))
                        link(nc.vector.tensor_tensor(var[:, :], se, so, ALU.add))
                        link(nc.vector.tensor_tensor(var[:, :], var[:, :], dif[:, :], ALU.add))
                        link(nc.vector.tensor_scalar(var[:, :], var[:, :], 1.0 / DIM, EPS, ALU.mult, ALU.add))
                        dve.wait_ge(sem["sqrt"], 1)
                        link(nc.vector.reciprocal(rstd[:, :], std[:, :]))
                        link(nc.vector.tensor_tensor(dif[:, :], var[:, :], rstd[:, :], ALU.mult))
                        link(nc.vector.tensor_tensor(dif[:, :], dif[:, :], rstd[:, :], ALU.mult))
                        link(nc.vector.tensor_scalar(dif[:, :], dif[:, :], -0.5, 1.5, ALU.mult, ALU.add))
                        link(nc.vector.tensor_tensor(rstd[:, :], rstd[:, :], dif[:, :], ALU.mult))

                        def normalise(t, par):
                            nc.vector.tensor_scalar(xn[:, par, :], xres[:, ds(t, 1), :].rearrange("p a d -> p (a d)"),
                                                    mean[:, ds(t, 1)], rstd[:, ds(t, 1)], ALU.subtract, ALU.mult)\
                                .then_inc(sem["xn"], 1)

                        with dve.Fori(0, NT // 2) as j:
                            for par in range(2):
                                t = j * 2 + par
                                normalise(t, par)
                                dve.wait_ge(sem["hi"], t + 1)
                                nc.vector.tensor_tensor(xnT_lo[:, :, ds(t * P, P)],
                                                        bank(2 + par, DIM).rearrange("p (k t) -> p k t", k=KD),
                                                        xnT_hi[:, :, ds(t * P, P)], ALU.subtract).then_inc(sem["lo"], 1)

        def attention_phase(tag, weights):
            with scope() as s:
                raw = sb(s, tag + "raw", [P, WCOL])
                w_hi = sb(s, tag + "w_hi", [P, WCOL], F32R)
                w_lo = sb(s, tag + "w_lo", [P, WCOL], F32R)
                k_hl = sb(s, tag + "k_hl", [P, 2, 2, SKV], F32R)
                k_hs = sb(s, tag + "k_hs", [P, 2, 2, SKV], F32R)
                q_hh = sb(s, tag + "q_hh", [P, 2, 2, SEQ], F32R)
                q_lm = sb(s, tag + "q_lm", [P, 2, 2, SEQ], F32R)
                vT = sb(s, tag + "vT", [P, SKV])
                v = sb(s, tag + "v", [P, 2, KVT, P])
                probs = sb(s, tag + "probs", [P, 2, KVT, SEQ])
                psums = sb(s, tag + "psums", [P, 2, 2, SEQ])
                row_max = sb(s, tag + "row_max", [P, QT, 2])
                inv = sb(s, tag + "inv", [P, SEQ])
                o_sb = sb(s, tag + "o_sb", [P, 2, SEQ])
                sem = sems(s, tag, "raw whi wlo one proj hi lo vt v score max mt mrow qk exp acc total inv norm ostored0 ostored1")
                with nc.Block() as block:
                    O, TOTAL = bank(4), bank(5)
                    RING = dict(K0=7, K1=6, Q=7, VT0=6, VT1=7, VX0=6, VX1=7, MT=6)

                    def slot(n):
                        return psum[:, (n % 2) * 2 * BANK:(n % 2) * 2 * BANK + 2 * BANK]

                    WQ = [slice(k * P, (k + 1) * P) for k in range(KD)]
                    WK = [slice((KD + k) * P, (KD + k + 1) * P) for k in range(2)]
                    WV = [slice((KD + 2 + k) * P, (KD + 3 + k) * P) for k in range(2)]

                    @block.sync
                    def _(sp):
                        sp.dma_start(raw[:, :], weights[0, :, :]).then_inc(sem["raw"], 16)

                        def store(hp, b):
                            sp.wait_ge(sem["norm"], hp * BATCH + (b + 2))
                            sp.dma_start(heads_out[ds(hp, 1), :, b * SEQ:(b + 1) * SEQ].rearrange("a p t -> (a p) t"),
                                         o_sb[:, b % 2, :]).then_inc(sem[f"ostored{b % 2}"], 16)

                        with sp.Fori(0, HP - 1) as hp:
                            sp.wait_ge(sem["wlo"], hp + 1)
                            sp.dma_start(raw[:, :], weights[ds(hp + 1, 1), :, :].rearrange("a p c -> (a p) c"))\
                                .then_inc(sem["raw"], 16)
                            for b in range(BATCH):
                                store(hp, b)
                        for b in range(BATCH):
                            store(HP - 1, b)
                        for par in range(2):
                            sp.wait_ge(sem[f"ostored{par}"], 16 * (HP * BATCH // 2 + 1))

                    @block.gpsimd
                    def _(pool):
                        for par in range(2):
                            for h in range(2):
                                nc.gpsimd.memset(k_hs[DH:DH + 1, par, h, :].bitcast(F32), 1.0).then_inc(sem["one"], 1)

                        def accumulate(hp, b):
                            i = hp * BATCH
                            n = 0
                            for kp in range(1, KVT // 2):
                                for h in range(2):
                                    pool.wait_ge(sem["exp"], i * 8 + (8 * b + 2 * kp + h + 1))
                                    if kp > 1:
                                        pool.wait_ge(sem["acc"], i * 8 + (8 * b + n - 1))
                                    a = probs[:, h, 0:2, :] if kp == 1 else psums[:, h, :, :]
                                    nc.gpsimd.tensor_tensor(psums[:, h, :, :], a, probs[:, h, 2 * kp:2 * kp + 2, :], ALU.add)\
                                        .then_inc(sem["acc"], 1)
                                    n += 1
                            for h in range(2):
                                pool.wait_ge(sem["acc"], i * 8 + (8 * b + n - 1))
                                nc.gpsimd.tensor_tensor(psums[:, h, 0, :], psums[:, h, 0, :], psums[:, h, 1, :], ALU.add)\
                                    .then_inc(sem["acc"], 1)
                                n += 1

                        with pool.Fori(0, HP) as hp:
                            for b in range(BATCH):
                                accumulate(hp, b)

                    HEAD = [slice(0, DH), slice(DH, P)]
                    PIECES = ["K0", "K1", "Q", "VT0", "VT1", "VX0", "VX1"]

                    @block.scalar
                    def _(act):
                        def split_weights(hp):
                            act.wait_ge(sem["raw"], hp * 16 + 16)
                            nc.scalar.activation(w_hi[:, :], raw[:, :], ACT.Copy).then_inc(sem["whi"], 1)

                        def evacuate(piece, hp, b):
                            i, par = hp * BATCH, b % 2
                            src = bank(RING[piece])
                            act.wait_ge(sem["proj"], i * 7 + (7 * b + PIECES.index(piece) + 1))
                            if piece in ("K0", "K1"):
                                cols = slice(int(piece[1]) * BANK, (int(piece[1]) + 1) * BANK)
                                for h in range(2):
                                    last = nc.scalar.activation(k_hl[0:DH, par, h, cols], src[HEAD[h], :], ACT.Copy)
                                last.then_inc(sem["hi"], 1)
                            elif piece == "Q":
                                for h in range(2):
                                    nc.scalar.activation(q_hh[0:DH, par, h, :], src[HEAD[h], :], ACT.Copy)
                                    last = nc.scalar.activation(q_hh[DH:P, par, h, :], src[HEAD[h], :], ACT.Copy)
                                last.then_inc(sem["hi"], 1)
                            elif piece in ("VT0", "VT1"):
                                cols = slice(int(piece[2]) * BANK, (int(piece[2]) + 1) * BANK)
                                nc.scalar.activation(vT[:, cols], src, ACT.Copy).then_inc(sem["vt"], 1)
                            else:
                                kv = slice(int(piece[2]) * 4, (int(piece[2]) + 1) * 4)
                                nc.scalar.activation(v[:, par, kv, :], src.rearrange("p (n d) -> p n d", d=P), ACT.Copy)\
                                    .then_inc(sem["v"], 1)

                        def max_rows(hp, b):
                            i, par = hp * BATCH, b % 2
                            act.wait_ge(sem["mt"], i + (b + 1))
                            for h in range(2):
                                nc.scalar.activation(q_lm[DH:DH + 1, par, h, :], bank(RING["MT"])[32 * h:32 * h + 1, :],
                                                     ACT.Copy).then_inc(sem["mrow"], 1)

                        def exps(hp, b, p):
                            i, h, kp = hp * BATCH, p % 2, p // 2
                            act.wait_ge(sem["qk"], i * 8 + (8 * b + p + 1))
                            nc.scalar.activation(probs[:, h, 2 * kp:2 * kp + 2, :],
                                                 slot(p).rearrange("p (n q) -> p n q", n=2), ACT.Exp, scale=SCALE)\
                                .then_inc(sem["exp"], 1)

                        def segment(hp, b, ahead=True, more=True):
                            for p in range(8):
                                if ahead and p < 7:
                                    evacuate(PIECES[p], hp + (b + 1) // BATCH, (b + 1) % BATCH)
                                exps(hp, b, p)
                            if more and b == 2:
                                act.wait_ge(sem["proj"], hp * (7 * BATCH) + 7 * BATCH)
                                split_weights(hp + 1)
                            if ahead:
                                max_rows(hp + (b + 1) // BATCH, (b + 1) % BATCH)

                        split_weights(0)
                        for piece in PIECES:
                            evacuate(piece, 0, 0)
                        max_rows(0, 0)
                        with act.Fori(0, HP - 1) as hp:
                            for b in range(BATCH):
                                segment(hp, b)
                        for b in range(BATCH):
                            segment(HP - 1, b, ahead=b < BATCH - 1, more=False)

                    @block.vector
                    def _(dve):
                        dve.sem_inc(sem["norm"], 1)
                        dve.sem_inc(sem["inv"], 1)
                        dve.sem_inc(sem["ostored0"], 16)
                        dve.sem_inc(sem["ostored1"], 16)

                        def split_weights(hp):
                            dve.wait_ge(sem["whi"], hp + 1)
                            nc.vector.tensor_tensor(w_lo[:, :], raw[:, :], w_hi[:, :], ALU.subtract).then_inc(sem["wlo"], 1)

                        def low_parts(piece, hp, b):
                            i, par = hp * BATCH, b % 2
                            src = bank(RING[piece])
                            dve.wait_ge(sem["hi"], i * 3 + (3 * b + PIECES.index(piece) + 1))
                            for h in range(2):
                                if piece == "Q":
                                    last = nc.vector.tensor_tensor(q_lm[0:DH, par, h, :], src[HEAD[h], :],
                                                                   q_hh[0:DH, par, h, :], ALU.subtract)
                                else:
                                    cols = slice(int(piece[1]) * BANK, (int(piece[1]) + 1) * BANK)
                                    nc.vector.tensor_tensor(k_hl[DH:P, par, h, cols], src[HEAD[h], :],
                                                            k_hl[0:DH, par, h, cols], ALU.subtract)
                                    last = nc.vector.tensor_copy(k_hs[0:DH, par, h, cols], k_hl[0:DH, par, h, cols])
                            last.then_inc(sem["lo"], 1)

                        def maxima(hp, b):
                            i = hp * BATCH
                            for t in range(8):
                                dve.wait_ge(sem["score"], i * 8 + (8 * b + t + 1))
                                nc.vector.reduce_max(row_max[:, t // 2, t % 2:t % 2 + 1], slot(t), axis=AX.X)\
                                    .then_inc(sem["max"], 1)

                        def normalise(hp, b):
                            i = hp * BATCH
                            dve.wait_ge(sem["total"], i + (b + 1))
                            nc.vector.reciprocal(inv[:, :], TOTAL).then_inc(sem["inv"], 1)
                            dve.wait_ge(sem["inv"], i + (b + 2))
                            dve.wait_ge(sem[f"ostored{b % 2}"], hp * (8 * BATCH) + 16 * (b // 2 + 1))
                            nc.vector.tensor_tensor(o_sb[:, b % 2, :], O, inv[:, :], ALU.mult).then_inc(sem["norm"], 1)

                        def segment(hp, b, ahead=True, more=True):
                            if ahead:
                                for piece in ("K0", "K1", "Q"):
                                    low_parts(piece, hp + (b + 1) // BATCH, (b + 1) % BATCH)
                            if b > 0:
                                normalise(hp, b - 1)
                            if more and b == 2:
                                split_weights(hp + 1)
                            if ahead:
                                maxima(hp + (b + 1) // BATCH, (b + 1) % BATCH)
                            if b == BATCH - 1:
                                normalise(hp, b)

                        split_weights(0)
                        for piece in ("K0", "K1", "Q"):
                            low_parts(piece, 0, 0)
                        maxima(0, 0)
                        with dve.Fori(0, HP - 1) as hp:
                            for b in range(BATCH):
                                segment(hp, b)
                        for b in range(BATCH):
                            segment(HP - 1, b, ahead=b < BATCH - 1, more=False)

                    @block.tensor
                    def _(pe):
                        def split_product(dst, terms):
                            for n, (w, m) in enumerate(terms):
                                last = nc.tensor.matmul(dst, w, m, start=n == 0, stop=n == len(terms) - 1)
                            return last

                        def ctx_product(dst, W, b, half):
                            cols = slice(b * SKV + half * BANK, b * SKV + (half + 1) * BANK)
                            return split_product(dst, [(w_hi[:, W[0]], ctx_hi[:, cols]), (w_hi[:, W[0]], ctx_lo[:, cols]),
                                                       (w_lo[:, W[0]], ctx_hi[:, cols]), (w_hi[:, W[1]], ctx_hl[:, cols]),
                                                       (w_lo[:, W[1]], ctx_hl[:, cols])])

                        def project(piece, hp, b, first=False):
                            i = hp * BATCH
                            dst = bank(RING[piece])
                            if piece == "K0":
                                if not first:
                                    pe.wait_ge(sem["v"], i * 2 + 2 * b)
                                if b == 0:
                                    pe.wait_ge(sem["wlo"], hp + 1)
                                last = ctx_product(dst, WK, b, 0)
                            elif piece == "K1":
                                if not first:
                                    pe.wait_ge(sem["mrow"], i * 2 + 2 * b)
                                last = ctx_product(dst, WK, b, 1)
                            elif piece == "Q":
                                pe.wait_ge(sem["lo"], i * 3 + (3 * b + 1))
                                rows = slice(b * SEQ, (b + 1) * SEQ)
                                terms = []
                                for k in range(KD):
                                    terms += [(w_hi[:, WQ[k]], xnT_hi[:, k, rows]), (w_hi[:, WQ[k]], xnT_lo[:, k, rows]),
                                              (w_lo[:, WQ[k]], xnT_hi[:, k, rows])]
                                last = split_product(dst, terms)
                            elif piece == "VT0":
                                pe.wait_ge(sem["lo"], i * 3 + (3 * b + 2))
                                last = ctx_product(dst, WV, b, 0)
                            elif piece == "VT1":
                                pe.wait_ge(sem["lo"], i * 3 + (3 * b + 3))
                                last = ctx_product(dst, WV, b, 1)
                            else:
                                half = int(piece[2])
                                pe.wait_ge(sem["vt"], i * 2 + (2 * b + half + 1))
                                for n in range(4):
                                    col = half * BANK + n * P
                                    last = nc.tensor.transpose(dst[:, n * P:(n + 1) * P], vT[:, col:col + P], ident[:, :])
                            last.then_inc(sem["proj"], 1)

                        def score(hp, b, t, first=False):
                            i, par, h, qt = hp * BATCH, b % 2, t % 2, t // 2
                            if t == 0:
                                pe.wait_ge(sem["lo"], i * 3 + (3 * b + 3))
                            if t >= 2:
                                pe.wait_ge(sem["max"], i * 8 + (8 * b + t - 1))
                            elif not first:
                                pe.wait_ge(sem["exp"], i * 8 + (8 * b + t - 1))
                            for half in range(2):
                                last = nc.tensor.matmul(slot(t)[:, half * BANK:(half + 1) * BANK],
                                                        q_hh[:, par, h, qt * P:(qt + 1) * P],
                                                        k_hl[:, par, h, half * BANK:(half + 1) * BANK], start=True, stop=True)
                            last.then_inc(sem["score"], 1)

                        def transpose_max(hp, b):
                            i = hp * BATCH
                            pe.wait_ge(sem["v"], i * 2 + (2 * b + 1))
                            pe.wait_ge(sem["max"], i * 8 + (8 * b + 8))
                            for h in range(2):
                                for qt in range(QT):
                                    last = nc.tensor.matmul(bank(RING["MT"])[32 * h:32 * h + 1, qt * P:(qt + 1) * P],
                                                            row_max[:, qt, h:h + 1], nident[:, :], start=True, stop=True)
                            last.then_inc(sem["mt"], 1)

                        def qk(hp, b, p):
                            i, par, h, kp = hp * BATCH, b % 2, p % 2, p // 2
                            if p == 0:
                                pe.wait_ge(sem["mrow"], i * 2 + (2 * b + 2))
                            if p < 2:
                                pe.wait_ge(sem["max"], i * 8 + (8 * b + 7 + p))
                            else:
                                pe.wait_ge(sem["exp"], i * 8 + (8 * b + p - 1))
                            for n in range(2):
                                keys = slice((2 * kp + n) * P, (2 * kp + n + 1) * P)
                                dst = slot(p)[:, n * BANK:(n + 1) * BANK]
                                nc.tensor.matmul(dst, k_hl[:, par, h, keys], q_hh[:, par, h, :], start=True, stop=False)
                                last = nc.tensor.matmul(dst, k_hs[0:DH + 1, par, h, keys], q_lm[0:DH + 1, par, h, :],
                                                        start=False, stop=True)
                            last.then_inc(sem["qk"], 1)

                        def pv(hp, b, kv):
                            i, par = hp * BATCH, b % 2
                            if kv == 0:
                                pe.wait_ge(sem["v"], i * 2 + (2 * b + 2))
                                pe.wait_ge(sem["norm"], i + (b + 1))
                            if kv % 2 == 0:
                                pe.wait_ge(sem["exp"], i * 8 + (8 * b + kv + 2))
                            for h in range(2):
                                nc.tensor.matmul(O[HEAD[h], :], v[:, par, kv, HEAD[h]], probs[:, h, kv, :],
                                                 start=kv == 0, stop=kv == KVT - 1)

                        def total(hp, b):
                            i = hp * BATCH
                            pe.wait_ge(sem["acc"], i * 8 + (8 * b + 8))
                            pe.wait_ge(sem["inv"], i + (b + 1))
                            for h in range(2):
                                last = nc.tensor.matmul(TOTAL[HEAD[h], :], ones[:, :], psums[:, h, 0, :], start=True, stop=True)
                            last.then_inc(sem["total"], 1)

                        def segment(hp, b, ahead=True):
                            nhp, nb = hp + (b + 1) // BATCH, (b + 1) % BATCH
                            for p in range(8):
                                if ahead and p < 7:
                                    project(PIECES[p], nhp, nb)
                                qk(hp, b, p)
                            if ahead:
                                score(nhp, nb, 0)
                                for t in range(1, 8):
                                    score(nhp, nb, t)
                                    pv(hp, b, t - 1)
                                pv(hp, b, 7)
                                transpose_max(nhp, nb)
                            else:
                                for kv in range(KVT):
                                    pv(hp, b, kv)
                            total(hp, b)

                        pe.wait_ge(sem["one"], 4)
                        for piece in PIECES:
                            project(piece, 0, 0, first=True)
                        for t in range(8):
                            score(0, 0, t, first=True)
                        transpose_max(0, 0)
                        with pe.Fori(0, HP - 1) as hp:
                            for b in range(BATCH):
                                segment(hp, b)
                        for b in range(BATCH):
                            segment(HP - 1, b, ahead=b < BATCH - 1)

        def route_phase(tag, cfg, router, bias, weights_of):
            E, per = cfg["experts"], cfg["per"]
            G = cfg["groups"]
            with scope() as s:
                rt = sb(s, tag + "rt", [P, KD, E])
                rt_hi = sb(s, tag + "rt_hi", [P, KD, E], F32R)
                rt_lo = sb(s, tag + "rt_lo", [P, KD, E], F32R)
                scores = sb(s, tag + "scores", [P, NT, E])
                choice = sb(s, tag + "choice", [P, NT, E])
                eq, gt, sel, start = (sb(s, tag + n, [P, NT, E]) for n in ("eq", "gt", "sel", "start"))
                top = sb(s, tag + "top", [P, NT, 8])
                need = sb(s, tag + "need", [P, NT])
                if G:
                    bias_sb = sb(s, tag + "rbias", [P, E])
                    gmax, geq, ggt, gsel, gstart = (sb(s, tag + n, [P, NT, G]) for n in ("gmax", "geq", "ggt", "gsel", "gstart"))
                sem = sems(s, tag, "rt bias hi lo logits scores step")
                with nc.Block() as block:

                    @block.sync
                    def _(sp):
                        sp.dma_start(rt[:, :, :], router).then_inc(sem["rt"], 16)
                        if G:
                            sp.dma_start(bias_sb[:, :], bias.partition_broadcast(P)).then_inc(sem["bias"], 16)

                    @block.scalar
                    def _(act):
                        act.wait_ge(sem["rt"], 16)
                        nc.scalar.activation(rt_hi[:, :, :], rt[:, :, :], ACT.Copy).then_inc(sem["hi"], 1)
                        act.wait_ge(sem["logits"], 1)
                        nc.scalar.activation(scores[:, :, :], bank(0, NT * E).rearrange("p (t e) -> p t e", e=E),
                                             ACT.Sigmoid if G else ACT.Copy).then_inc(sem["scores"], 1)

                    @block.tensor
                    def _(pe):
                        pe.wait_ge(sem["lo"], 1)
                        for t in range(NT):
                            rows = slice(t * P, (t + 1) * P)
                            n = 0
                            for k in range(KD):
                                for a, w in ((xnT_hi, rt_hi), (xnT_lo, rt_hi), (xnT_hi, rt_lo)):
                                    last = nc.tensor.matmul(bank(0)[:, t * E:(t + 1) * E], a[:, k, rows], w[:, k, :],
                                                            start=n == 0, stop=n == 3 * KD - 1)
                                    n += 1
                        last.then_inc(sem["logits"], 1)

                    @block.vector
                    def _(dve):
                        dve.wait_ge(sem["hi"], 1)
                        nc.vector.tensor_tensor(rt_lo[:, :, :], rt[:, :, :], rt_hi[:, :, :], ALU.subtract).then_inc(sem["lo"], 1)
                        n = 0

                        def link(ins):
                            nonlocal n
                            n += 1
                            ins.then_inc(sem["step"], 1)
                            dve.wait_ge(sem["step"], n)

                        def flat(a):
                            return a.rearrange("p t n -> p (t n)")

                        def wide(a, n):
                            return a.unsqueeze(2).broadcast_to([P, NT, n])

                        def pick(v, k, n, eq, gt, sel, start):
                            link(nc.vector.memset(start[:, :, :], 1.0))
                            link(nc.vector.memset(start[:, :, 0:1], 0.0))
                            for t in range(NT):
                                last = nc.vector.max(top[:, t, :], v[:, t, :])
                            link(last)
                            kth = top[:, :, k - 1:k].broadcast_to([P, NT, n])
                            link(nc.vector.tensor_tensor(gt[:, :, :], v[:, :, :], kth, ALU.is_gt))
                            link(nc.vector.tensor_tensor(eq[:, :, :], v[:, :, :], kth, ALU.is_equal))
                            link(nc.vector.reduce_sum(need[:, :], gt[:, :, :], axis=AX.X))
                            link(nc.vector.tensor_scalar(need[:, :], need[:, :], -1.0, float(k), ALU.mult, ALU.add))
                            link(nc.vector.tensor_tensor_scan(flat(sel[:, :, :]), flat(start[:, :, :]), flat(eq[:, :, :]), 0.0,
                                                              ALU.mult, ALU.add))
                            link(nc.vector.tensor_tensor(sel[:, :, :], sel[:, :, :], wide(need[:, :], n), ALU.is_le))
                            link(nc.vector.tensor_tensor(eq[:, :, :], eq[:, :, :], sel[:, :, :], ALU.mult))
                            link(nc.vector.tensor_tensor(sel[:, :, :], gt[:, :, :], eq[:, :, :], ALU.add))

                        dve.wait_ge(sem["scores"], 1)
                        if G:
                            dve.wait_ge(sem["bias"], 16)
                            link(nc.vector.tensor_tensor(choice[:, :, :], scores[:, :, :],
                                                         bias_sb[:, :].unsqueeze(1).broadcast_to([P, NT, E]), ALU.add))
                            link(nc.vector.reduce_max(flat(gmax[:, :, :]), flat(choice[:, :, :])
                                                      .rearrange("p (g m) -> p g m", m=E // G), axis=AX.X))
                            pick(gmax, cfg["top_groups"], G, geq, ggt, gsel, gstart)
                            link(nc.vector.tensor_tensor(
                                flat(choice[:, :, :]).rearrange("p (g m) -> p g m", m=E // G),
                                flat(choice[:, :, :]).rearrange("p (g m) -> p g m", m=E // G),
                                flat(gsel[:, :, :]).unsqueeze(2).broadcast_to([P, NT * G, E // G]), ALU.mult))
                            pick(choice, cfg["top"], E, eq, gt, sel, start)
                            link(nc.vector.tensor_tensor(sel[:, :, :], sel[:, :, :], scores[:, :, :], ALU.mult))
                            link(nc.vector.reduce_sum(need[:, :], sel[:, :, :], axis=AX.X))
                            link(nc.vector.tensor_scalar(need[:, :], need[:, :], 1e-20, None, ALU.add))
                            link(nc.vector.reciprocal(need[:, :], need[:, :]))
                            link(nc.vector.tensor_scalar(need[:, :], need[:, :], cfg["scale"], None, ALU.mult))
                            link(nc.vector.tensor_tensor(sel[:, :, :], sel[:, :, :], wide(need[:, :], E), ALU.mult))
                        else:
                            pick(scores, cfg["top"], E, eq, gt, sel, start)
                        first = cfg["shared"] * NT
                        link(nc.vector.memset(weights_of[:, 0:first], 1.0))
                        for c in range(per):
                            link(nc.vector.tensor_copy(
                                weights_of[:, first:].rearrange("p (e c t) -> p c t e", c=per, t=NT)[:, c, :, :], sel[:, :, :]))

        def expert_phase(tag, chunks, packed, weights_of, xres, store):
            with scope() as s:
                raw = sb(s, tag + "raw", [P, 2, MCOL])
                w_hi = sb(s, tag + "w_hi", [P, 2, MCOL], F32R)
                w_lo = sb(s, tag + "w_lo", [P, 2, MCOL], F32R)
                act_g = sb(s, tag + "act_g", [P, 2, BANK])
                hid = sb(s, tag + "hid", [P, 2, BANK])
                hid_hi = sb(s, tag + "hid_hi", [P, 4, BANK], F32R)
                hid_lo = sb(s, tag + "hid_lo", [P, 4, BANK], F32R)
                sem = sems(s, tag, "raw0 raw1 whi wlo gu silu mul hhi hlo down fma out")
                UNITS = chunks * BLK
                ROUND = 2 * BLK
                ROUNDS = UNITS // ROUND
                TB = NT // BLK
                with nc.Block() as block:

                    def run(eng, unit):
                        unit(0, 0)
                        unit(0, 1)
                        with eng.Fori(0, ROUNDS - 1) as j:
                            for u in range(2, ROUND + 2):
                                unit(j, u)
                        for u in range(2, ROUND):
                            unit(ROUNDS - 1, u)

                    @block.sync
                    def _(sp):
                        with sp.Fori(0, chunks // 2) as j:
                            for par in range(2):
                                sp.wait_ge(sem["wlo"], j * 2 + (par + 1))
                                sp.dma_start(raw[:, par, :], packed[ds(j * 2 + par, 1), :, :].rearrange("a p c -> (a p) c"))\
                                    .then_inc(sem[f"raw{par}"], 16)
                        if store is not None:
                            sp.wait_ge(sem["fma"], UNITS + 4)
                            sp.dma_start(store, xres[:, :, :]).then_inc(sem["out"], 16)
                            sp.wait_ge(sem["out"], 16)

                    @block.gpsimd
                    def _(pool):
                        pool.sem_inc(sem["wlo"], 2)
                        with pool.Fori(0, chunks // 2) as j:
                            for par in range(2):
                                pool.wait_ge(sem["whi"], j * 2 + (par + 1))
                                nc.gpsimd.tensor_tensor(w_lo[:, par, :], raw[:, par, :], w_hi[:, par, :], ALU.subtract)\
                                    .then_inc(sem["wlo"], 1)

                    @block.scalar
                    def _(act):
                        def split(j, c):
                            act.wait_ge(sem[f"raw{c % 2}"], j * 16 + 16 * (c // 2 + 1))
                            nc.scalar.activation(w_hi[:, c % 2, :], raw[:, c % 2, :], ACT.Copy).then_inc(sem["whi"], 1)

                        def unit(j, u):
                            k = j * ROUND
                            if u % BLK == 2 and not (isinstance(j, int) and j == ROUNDS - 1 and u == ROUND - 2):
                                c = u // BLK + 1
                                act.wait_ge(sem["down"], k + BLK * c)
                                split(j, c)
                            act.wait_ge(sem["gu"], k + (u + 1))
                            act.wait_ge(sem["mul"], k + (u + 1))
                            nc.scalar.activation(act_g[:, u % 2, :], bank(u % 2), ACT.Silu).then_inc(sem["silu"], 1)
                            act.wait_ge(sem["mul"], k + (u + 3))
                            act.wait_ge(sem["down"], k + (u + 1))
                            nc.scalar.activation(hid_hi[:, u % 4, :], hid[:, u % 2, :], ACT.Copy).then_inc(sem["hhi"], 1)

                        split(0, 0)
                        run(act, unit)

                    @block.vector
                    def _(dve):
                        dve.sem_inc(sem["mul"], 2)
                        dve.sem_inc(sem["fma"], 4)

                        def add(j, u):
                            k = j * ROUND
                            dve.wait_ge(sem["down"], k + (u + 5))
                            dve.wait_ge(sem["fma"], k + (u + 1))
                            for n in range(TB):
                                t = (u % BLK) * TB + n
                                acc = xres[:, t, :]
                                last = nc.vector.scalar_tensor_tensor(
                                    acc, bank(4 + 2 * (u % 2) + n // 2)[:, (n % 2) * DIM:(n % 2 + 1) * DIM],
                                    weights_of[:, ds(j * (2 * NT) + ((u // BLK) * NT + t), 1)], acc, ALU.mult, ALU.add)
                            last.then_inc(sem["fma"], 1)

                        def unit(j, u):
                            k = j * ROUND
                            dve.wait_ge(sem["silu"], k + (u + 1))
                            nc.vector.tensor_tensor(hid[:, u % 2, :], bank(2 + u % 2), act_g[:, u % 2, :], ALU.mult)\
                                .then_inc(sem["mul"], 1)
                            if u >= 2:
                                add(j, u - 2)
                            dve.wait_ge(sem["hhi"], k + (u + 1))
                            nc.vector.tensor_tensor(hid_lo[:, u % 4, :], hid[:, u % 2, :], hid_hi[:, u % 4, :], ALU.subtract)\
                                .then_inc(sem["hlo"], 1)

                        run(dve, unit)
                        add(ROUNDS - 1, ROUND - 2)
                        add(ROUNDS - 1, ROUND - 1)

                    @block.tensor
                    def _(pe):
                        pe.sem_inc(sem["down"], 4)

                        def gate_up(j, u):
                            k, par = j * ROUND, (u // BLK) % 2
                            rows = slice((u % BLK) * BANK, (u % BLK + 1) * BANK)
                            if u % BLK == 0:
                                pe.wait_ge(sem["wlo"], j * 2 + (u // BLK + 3))
                            pe.wait_ge(sem["mul"], k + (u + 1))
                            for g in range(2):
                                n = 0
                                for kd in range(KD):
                                    w = slice((g * KD + kd) * P, (g * KD + kd + 1) * P)
                                    for a, m in ((w_hi, xnT_hi), (w_hi, xnT_lo), (w_lo, xnT_hi)):
                                        last = nc.tensor.matmul(bank(2 * g + u % 2), a[:, par, w], m[:, kd, rows],
                                                                start=n == 0, stop=n == 3 * KD - 1)
                                        n += 1
                            last.then_inc(sem["gu"], 1)

                        def down(j, u):
                            k, par = j * ROUND, (u // BLK) % 2
                            w = slice(2 * KD * P, MCOL)
                            pe.wait_ge(sem["hlo"], k + (u + 1))
                            pe.wait_ge(sem["fma"], k + (u + 3))
                            for n in range(TB):
                                dst = bank(4 + 2 * (u % 2) + n // 2)[:, (n % 2) * DIM:(n % 2 + 1) * DIM]
                                rows = slice(n * P, (n + 1) * P)
                                for m, (a, b) in enumerate(((hid_hi, w_hi), (hid_hi, w_lo), (hid_lo, w_hi))):
                                    last = nc.tensor.matmul(dst, a[:, u % 4, rows], b[:, par, w], start=m == 0, stop=m == 2)
                            last.then_inc(sem["down"], 1)

                        def unit(j, u):
                            gate_up(j, u)
                            if u >= 2:
                                down(j, u - 2)

                        run(pe, unit)
                        down(ROUNDS - 1, ROUND - 2)
                        down(ROUNDS - 1, ROUND - 1)

        with scope() as s:
            xres = sb(s, "x_first", [P, NT, DIM])
            norm_phase("n0_", xres, x_tiles, None)
        for layer, cfg in enumerate(LAYERS):
            w = layer_in[layer]
            tag = f"L{layer}"
            attention_phase(tag + "a_", w["attention"])
            with scope() as s:
                xres = sb(s, tag + "xres", [P, NT, DIM])
                chunks = cfg["experts"] * cfg["per"] + cfg["shared"]
                weights_of = sb(s, tag + "weights_of", [P, chunks * NT])
                norm_phase(tag + "n_", xres, x_tiles if layer == 0 else mid_tiles, (w["out"], w["out_bias"]))
                route_phase(tag + "r_", cfg, w["router"], w["router_bias"], weights_of)
                expert_phase(tag + "e_", chunks, w["experts"], weights_of, xres, mid_tiles if layer == 0 else out_tiles)
                if layer == 0:
                    norm_phase("n1_", xres, None, None)


def kernel(**inputs):
    import numpy as np
    import concourse.bacc as bacc
    from concourse.bass_utils import run_bass_kernel_spmd

    a = {k: np.asarray(v) for k, v in inputs.items()}

    def pairs(wq, wk, wv):
        out = []
        for hp in range(HP):
            c = slice(hp * P, (hp + 1) * P)
            cols = [wq[k * P:(k + 1) * P, c] for k in range(KD)]
            for w in (wk, wv):
                cols += [w[:P, c], np.concatenate([w[P:, c], w[P:, c]], axis=0)]
            out.append(np.concatenate(cols, axis=1))
        return np.ascontiguousarray(np.stack(out))

    def chunk(gate, up, down):
        cols = [m[:, k * P:(k + 1) * P].T for m in (gate, up) for k in range(KD)]
        return np.concatenate(cols + [down.T], axis=1)

    def router(w):
        return np.ascontiguousarray(w.T.reshape(KD, P, w.shape[0]).transpose(1, 0, 2))

    H = P
    packed0 = [chunk(a["L0_ffn_shared_gate_w"][c * H:(c + 1) * H], a["L0_ffn_shared_up_w"][c * H:(c + 1) * H],
                     a["L0_ffn_shared_down_w"][:, c * H:(c + 1) * H]) for c in range(LAYERS[0]["shared"])]
    packed0 += [chunk(gu[:H], gu[H:], dn) for gu, dn in zip(a["L0_ffn_experts_gate_up"], a["L0_ffn_experts_down"])]
    packed1 = [chunk(a["L1_ffn_w_gate_s"][c * H:(c + 1) * H], a["L1_ffn_w_up_s"][c * H:(c + 1) * H],
                     a["L1_ffn_w_down_s"][:, c * H:(c + 1) * H]) for c in range(LAYERS[1]["shared"])]
    packed1 += [chunk(g[c * H:(c + 1) * H], u[c * H:(c + 1) * H], d[:, c * H:(c + 1) * H])
                for g, u, d in zip(a["L1_ffn_gate"], a["L1_ffn_up"], a["L1_ffn_down"]) for c in range(LAYERS[1]["per"])]

    ctxT = a["ctx_768"].reshape(BATCH * SKV, CTXD).T

    def wo(w):
        return np.ascontiguousarray(w.reshape(HP, P, DIM).transpose(1, 0, 2))

    arrays = {
        "x": np.ascontiguousarray(a["x"].reshape(TOK, DIM)),
        "ctx_top": np.ascontiguousarray(ctxT[:P]),
        "ctx_bot": np.ascontiguousarray(np.concatenate([ctxT[P:], ctxT[P:]], axis=0)),
        "attention0": pairs(a["L0_xattn_w_q"], a["L0_xattn_w_k"], a["L0_xattn_w_v"]),
        "out0": wo(a["L0_xattn_w_o"]), "out_bias0": np.ascontiguousarray(a["L0_xattn_b_o"]),
        "router0": router(a["L0_ffn_gate_weight"]), "router_bias0": np.ascontiguousarray(a["L0_ffn_e_score_correction_bias"]),
        "experts0": np.ascontiguousarray(np.stack(packed0)),
        "attention1": pairs(a["L1_xattn_Wq"], a["L1_xattn_Wk"], a["L1_xattn_Wv"]),
        "out1": wo(a["L1_xattn_Wo"]), "out_bias1": np.ascontiguousarray(a["L1_xattn_bo"]),
        "router1": router(a["L1_ffn_router"]),
        "experts1": np.ascontiguousarray(np.stack(packed1)),
    }
    nc = bacc.Bacc("TRN2", target_bir_lowering=False, num_devices=1)
    d = {n: nc.dram_tensor(f"in_{n}", v.shape, mybir.dt.from_np(v.dtype), kind="ExternalInput").ap() for n, v in arrays.items()}
    out = nc.dram_tensor("out", (TOK, DIM), F32, kind="ExternalOutput").ap()
    layers = [{n: d.get(f"{n}{i}") for n in ("attention", "out", "out_bias", "router", "router_bias", "experts")} for i in range(2)]
    build(nc, d["x"], d["ctx_top"], d["ctx_bot"], layers, out)
    r = run_bass_kernel_spmd(nc, [{f"in_{n}": v for n, v in arrays.items()}], core_ids=[0])
    return r.results[0]["out"].reshape(BATCH, SEQ, DIM)
```

```python
import concourse.bass as bass
from concourse import mybir
from contextlib import ExitStack

F32 = mybir.dt.float32
F32R = mybir.dt.float32r
I32 = mybir.dt.int32
ALU = mybir.AluOpType
ACT = mybir.ActivationFunctionType
AX = mybir.AxisListType
ds = bass.ds

P = 128
BATCH, SEQ, DIM = 4, 512, 256
SKV, CTXD = 1024, 192
HEADS, DH = 16, 64
TOK = BATCH * SEQ
NT = TOK // P
KD = DIM // P
HP = HEADS // 2
QT = SEQ // P
KVT = SKV // P
WCOL = (KD + 4) * P
MCOL = 2 * KD * P + DIM
BANK = 512
BLK = TOK // BANK
SCALE = DH ** -0.5
ORDER = ["K0", "P6", 0, 1, "K1", 2, "P7", 3, "V0", 4, "Q", 5, "V1", 6, 7, "V2", "V3"]
LATE = 2
EPS = 1e-5

LAYERS = [
    dict(experts=32, per=1, shared=2, groups=8, top_groups=4, top=6, scale=2.5),
    dict(experts=8, per=4, shared=4, groups=0, top_groups=0, top=1, scale=1.0),
]
SORTED = LAYERS[1]
TILES = NT + SORTED["experts"] - 1
HID = SORTED["per"] * P
ECOL = 2 * KD * HID + SORTED["per"] * DIM


def build(nc, x, ctx_top, ctx_bot, layer_in, out):
    stack = ExitStack()

    def scope():
        return ExitStack()

    with stack:
        def sb(where, name, shape, dt=F32):
            return where.enter_context(nc.sbuf_tensor(name, shape, dt))

        def sems(where, prefix, names):
            return {n: where.enter_context(nc.semaphore(f"{prefix}_{n}")) for n in names.split()}

        ident = sb(stack, "ident", [P, P])
        ones = sb(stack, "ones", [P, DH])
        xnT_hi = sb(stack, "xnT_hi", [P, KD, TOK], F32R)
        xnT_lo = sb(stack, "xnT_lo", [P, KD, TOK], F32R)
        xres = sb(stack, "xres", [P, NT, DIM])
        ctx_scope = stack.enter_context(scope())
        ctx_hi = sb(ctx_scope, "ctx_hi", [P, BATCH * SKV], F32R)
        ctx_lo = sb(ctx_scope, "ctx_lo", [P, BATCH * SKV], F32R)
        ctx_hl = sb(ctx_scope, "ctx_hl", [P, BATCH * SKV], F32R)
        sorted_x = nc.dram_tensor("sorted_x", (TILES * P, DIM), F32, kind="Internal").ap()
        sorted_y = nc.dram_tensor("sorted_y", (TILES * P, DIM), F32, kind="Internal").ap()
        psum = stack.enter_context(nc.psum_tensor("psum", [P, 8 * BANK], F32))
        x_tiles = x.rearrange("(t p) d -> p t d", p=P)
        out_tiles = out.rearrange("(t p) d -> p t d", p=P)

        def bank(n, width=BANK):
            return psum[:, n * BANK:n * BANK + width]

        def norm_phase(tag, xres, source=None, keep=None, wipe=None, clear=(), prefetch=None):
            NG = NT // 2
            STAGES = BATCH
            NCH = 2 * BATCH
            with scope() as s:
                stats = sb(s, tag + "stats", [P, NT, 6])
                mean = sb(s, tag + "mean", [P, NT])
                var = sb(s, tag + "var", [P, NT])
                dif = sb(s, tag + "dif", [P, NT])
                std = sb(s, tag + "std", [P, NT])
                rstd = sb(s, tag + "rstd", [P, NT])
                if keep is None:
                    xn, xn_groups = sb(s, tag + "xn", [P, 2, 2, DIM]), 2
                else:
                    xn, xn_groups = keep[:, :, :].rearrange("p (g i) d -> p g i d", i=2), NG
                if source is not None:
                    stage = sb(s, tag + "stage", [P, STAGES, SKV])
                if wipe is not None:
                    zeros = sb(s, tag + "zeros", [P, DIM])
                sem = sems(s, tag, "stat batch sqrt xn tr hi lo"
                           + (" x0 x1 id chi clo_top clo_rest " + " ".join(f"staged{n}" for n in range(STAGES)) if source is not None else "")
                           + (" zero wiped" if wipe is not None else ""))
                with nc.Block() as block:

                    def chunk(n):
                        return slice((n % BATCH) * SKV, (n % BATCH + 1) * SKV)

                    def group_bank(g):
                        return bank(g % 2).rearrange("p (k t) -> p k t", k=KD)

                    @block.sync
                    def _(sp):
                        if source is not None:
                            for half in range(2):
                                tiles = slice(half * NG, (half + 1) * NG)
                                sp.dma_start(xres[:, tiles, :], source[:, tiles, :]).then_inc(sem[f"x{half}"], 16)
                            for n in range(NCH):
                                if n >= STAGES:
                                    sp.wait_ge(sem["clo_top"], n - STAGES + 1)
                                src = ctx_top if n < BATCH else ctx_bot
                                sp.dma_start(stage[:, n % STAGES, :], src[:, chunk(n)]).then_inc(sem[f"staged{n % STAGES}"], 16)
                        if prefetch is not None:
                            prefetch(sp)
                        if wipe is not None:
                            sp.wait_ge(sem["zero"], 1)
                            sp.dma_start(wipe.rearrange("(t p) d -> p t d", p=P),
                                         zeros[:, :].unsqueeze(1).broadcast_to([P, wipe.shape[0] // P, DIM])).then_inc(sem["wiped"], 16)
                            sp.wait_ge(sem["wiped"], 16)

                    @block.gpsimd
                    def _(pool):
                        for used in clear:
                            pool.sem_clear(used)
                        if wipe is not None:
                            nc.gpsimd.memset(zeros[:, :], 0.0).then_inc(sem["zero"], 1)
                        if source is not None:
                            nc.gpsimd.memset(ident[:, :], 0.0).then_inc(sem["id"], 1)
                            nc.gpsimd.memset(ones[:, :], 1.0).then_inc(sem["id"], 1)
                            pool.wait_ge(sem["id"], 2)
                            nc.gpsimd.affine_select(out=ident[:, :], in_=ident[:, :], compare_op=ALU.not_equal, fill=1.0, base=0,
                                                    pattern=[[-1, P]], channel_multiplier=1).then_inc(sem["id"], 1)
                            for n in range(BATCH):
                                pool.wait_ge(sem["chi"], n + 1)
                                nc.gpsimd.tensor_tensor(ctx_lo[:, chunk(n)], stage[:, n, :], ctx_hi[:, chunk(n)], ALU.subtract)\
                                    .then_inc(sem["clo_top"], 1)

                    @block.scalar
                    def _(act):
                        def context(n):
                            act.wait_ge(sem[f"staged{n % STAGES}"], 16 * (n // STAGES + 1))
                            dst = ctx_hi if n < BATCH else ctx_hl
                            nc.scalar.activation(dst[:, chunk(n)], stage[:, n % STAGES, :], ACT.Copy).then_inc(sem["chi"], 1)

                        for n in range(BATCH if source is not None else 0):
                            context(n)
                        act.wait_ge(sem["batch"], 8)
                        nc.scalar.activation(std[:, :], var[:, :], ACT.Sqrt).then_inc(sem["sqrt"], 1)
                        for g in range(NG):
                            act.wait_ge(sem["tr"], g + 1)
                            nc.scalar.activation(xnT_hi[:, :, 2 * g * P:2 * (g + 1) * P], group_bank(g), ACT.Copy)\
                                .then_inc(sem["hi"], 1)
                        for n in range(BATCH, NCH if source is not None else BATCH):
                            context(n)

                    @block.tensor
                    def _(pe):
                        if source is not None:
                            pe.wait_ge(sem["id"], 3)
                        for g in range(NG):
                            pe.wait_ge(sem["xn"], g + 1)
                            if g >= 2:
                                pe.wait_ge(sem["lo"], g - 1)
                            for t in range(2):
                                for k in range(KD):
                                    last = nc.tensor.transpose(group_bank(g)[:, k, t * P:(t + 1) * P],
                                                               xn[:, g % xn_groups, t, k * P:(k + 1) * P], ident[:, :])
                            last.then_inc(sem["tr"], 1)

                    @block.vector
                    def _(dve):
                        for t in range(NT):
                            if source is not None and t % NG == 0:
                                dve.wait_ge(sem[f"x{t // NG}"], 16)
                            nc.vector.bn_stats(stats[:, t, :], xres[:, t, :]).then_inc(sem["stat"], 1)
                        dve.wait_ge(sem["stat"], NT)
                        n = 0

                        def link(ins):
                            nonlocal n
                            n += 1
                            ins.then_inc(sem["batch"], 1)
                            dve.wait_ge(sem["batch"], n)

                        me, se, mo, so = (stats[:, :, i] for i in (1, 2, 4, 5))
                        link(nc.vector.tensor_tensor(mean[:, :], me, mo, ALU.add))
                        link(nc.vector.tensor_scalar(mean[:, :], mean[:, :], 0.5, None, ALU.mult))
                        link(nc.vector.tensor_tensor(dif[:, :], me, mo, ALU.subtract))
                        link(nc.vector.tensor_tensor(dif[:, :], dif[:, :], dif[:, :], ALU.mult))
                        link(nc.vector.tensor_scalar(dif[:, :], dif[:, :], DIM / 4.0, None, ALU.mult))
                        link(nc.vector.tensor_tensor(var[:, :], se, so, ALU.add))
                        link(nc.vector.tensor_tensor(var[:, :], var[:, :], dif[:, :], ALU.add))
                        link(nc.vector.tensor_scalar(var[:, :], var[:, :], 1.0 / DIM, EPS, ALU.mult, ALU.add))
                        dve.wait_ge(sem["sqrt"], 1)
                        link(nc.vector.reciprocal(rstd[:, :], std[:, :]))
                        link(nc.vector.tensor_tensor(dif[:, :], var[:, :], rstd[:, :], ALU.mult))
                        link(nc.vector.tensor_tensor(dif[:, :], dif[:, :], rstd[:, :], ALU.mult))
                        link(nc.vector.tensor_scalar(dif[:, :], dif[:, :], -0.5, 1.5, ALU.mult, ALU.add))
                        link(nc.vector.tensor_tensor(rstd[:, :], rstd[:, :], dif[:, :], ALU.mult))

                        def normalise(g):
                            if g >= xn_groups:
                                dve.wait_ge(sem["tr"], g - 1)
                            for i in range(2):
                                t = 2 * g + i
                                last = nc.vector.tensor_scalar(xn[:, g % xn_groups, i, :], xres[:, t, :], mean[:, t:t + 1],
                                                               rstd[:, t:t + 1], ALU.subtract, ALU.mult)
                            last.then_inc(sem["xn"], 1)

                        normalise(0)
                        for g in range(NG):
                            if g + 1 < NG:
                                normalise(g + 1)
                            dve.wait_ge(sem["hi"], g + 1)
                            cols = slice(2 * g * P, 2 * (g + 1) * P)
                            nc.vector.tensor_tensor(xnT_lo[:, :, cols], group_bank(g), xnT_hi[:, :, cols], ALU.subtract)\
                                .then_inc(sem["lo"], 1)
                        if source is not None:
                            for n in range(BATCH, NCH):
                                dve.wait_ge(sem["chi"], n + 1)
                                nc.vector.tensor_tensor(ctx_hl[DH:P, chunk(n)], stage[DH:P, n % STAGES, :], ctx_hl[DH:P, chunk(n)],
                                                        ALU.subtract).then_inc(sem["clo_rest"], 1)

        attention_sems = sems(stack, "a", "raw wo bias biased whi wlo one proj hi lo vh v score max mt mrow qk exp acc "
                                          "total inv pv norm out ocopy added")

        def attention_phase(tag, weights, wo, bias, xres):
            with scope() as s:
                raw = sb(s, tag + "raw", [P, WCOL])
                w_split = sb(s, tag + "w_split", [P, 2, WCOL], F32R)
                w_hi, w_lo = w_split[:, 0, :], w_split[:, 1, :]
                wo_sb = sb(s, tag + "wo", [P, DIM])
                k_hl = sb(s, tag + "k_hl", [P, 2, 2, SKV], F32R)
                k_hs = sb(s, tag + "k_hs", [P, 2, 2, SKV], F32R)
                q_hh = sb(s, tag + "q_hh", [P, 2, 2, SEQ], F32R)
                q_lm = sb(s, tag + "q_lm", [P, 2, 2, SEQ], F32R)
                v = sb(s, tag + "v", [P, 2, KVT, P])
                probs = sb(s, tag + "probs", [P, 2, KVT, SEQ])
                psums = sb(s, tag + "psums", [P, 2, SEQ])
                row_max = sb(s, tag + "row_max", [P, QT, P])
                inv = sb(s, tag + "inv", [P, SEQ])
                o_sb = inv
                out_sb = sb(s, tag + "out_sb", [P, 2, 2 * DIM])
                bias_sb = inv[:, 0:DIM]
                sem = attention_sems
                with nc.Block() as block:
                    O, TOTAL = bank(4), bank(5)
                    PIECES = ["K0", "K1", "V0", "Q", "V1", "V2", "V3"]
                    RING = dict(K0=7, K1=6, V0=7, Q=6, V1=7, V2=6, V3=7, OUT0=6, OUT1=7, MT=6)
                    NP = len(PIECES)
                    VALUES = ["V0", "V1", "V2", "V3"]
                    NV = len(VALUES)
                    LOWS = ["K0", "K1", "Q"]
                    HEAD = [slice(0, DH), slice(DH, P)]

                    def slot(n):
                        return psum[:, (n % 2) * 2 * BANK:(n % 2) * 2 * BANK + 2 * BANK]

                    def halves(piece):
                        return bank(RING[piece]).rearrange("p (n w d) -> p n w d", n=2, w=2)

                    WQ = [slice(k * P, (k + 1) * P) for k in range(KD)]
                    WK = [slice((KD + k) * P, (KD + k + 1) * P) for k in range(2)]
                    WV = [slice((KD + 2 + k) * P, (KD + 3 + k) * P) for k in range(2)]

                    def half_of(piece):
                        n = int(piece[1])
                        return slice(n * BANK, (n + 1) * BANK)

                    def run(eng, segment):
                        segment(0, 0, first=True)
                        with eng.Fori(0, HP - 1) as hp:
                            for b in range(1, BATCH + 1):
                                segment(hp, b)
                        for b in range(1, BATCH):
                            segment(HP - 1, b, ahead=b < BATCH - 1)

                    @block.sync
                    def _(sp):
                        sp.dma_start(raw[:, :], weights[0, :, :]).then_inc(sem["raw"], 16)
                        sp.dma_start(bias_sb, bias.partition_broadcast(P)).then_inc(sem["bias"], 16)
                        sp.dma_start(wo_sb[:, :], wo[0, :, :]).then_inc(sem["wo"], 16)
                        with sp.Fori(0, HP - 1) as hp:
                            sp.wait_ge(sem["wlo"], hp + 1)
                            sp.dma_start(raw[:, :], weights[ds(hp + 1, 1), :, :].rearrange("a p c -> (a p) c"))\
                                .then_inc(sem["raw"], 16)
                            sp.wait_ge(sem["out"], hp * (2 * BATCH) + 2 * BATCH)
                            sp.dma_start(wo_sb[:, :], wo[ds(hp + 1, 1), :, :].rearrange("a p c -> (a p) c"))\
                                .then_inc(sem["wo"], 16)

                    @block.gpsimd
                    def _(pool):
                        for par in range(2):
                            for h in range(2):
                                nc.gpsimd.memset(k_hs[DH:DH + 1, par, h, :].bitcast(F32), 1.0).then_inc(sem["one"], 1)
                        pool.wait_ge(sem["one"], 4)
                        nc.gpsimd.memset(row_max[:, :, :], 0.0).then_inc(sem["one"], 1)
                        pool.wait_ge(sem["one"], 5)
                        pool.wait_ge(sem["bias"], 16)
                        for t in range(NT):
                            nc.gpsimd.tensor_tensor(xres[:, t, :], xres[:, t, :], bias_sb, ALU.add).then_inc(sem["biased"], 1)

                        def accumulate(hp, b):
                            i = hp * BATCH
                            n = 0
                            for kv in range(1, KVT):
                                for h in range(2):
                                    pool.wait_ge(sem["exp"], i * 8 + (8 * b + 2 * (kv // 2) + h + 1))
                                    if kv > 1:
                                        pool.wait_ge(sem["acc"], i * (2 * KVT - 2) + ((2 * KVT - 2) * b + n - 1))
                                    a = probs[:, h, 0, :] if kv == 1 else psums[:, h, :]
                                    nc.gpsimd.tensor_tensor(psums[:, h, :], a, probs[:, h, kv, :], ALU.add).then_inc(sem["acc"], 1)
                                    n += 1

                        def add_output(hp, b):
                            o = hp * (2 * BATCH)
                            for half in range(2):
                                t = (b % BATCH) * QT + 2 * half
                                rows = xres[:, t:t + 2, :].rearrange("p t d -> p (t d)")
                                pool.wait_ge(sem["ocopy"], o + (2 * b + half + 3))
                                pool.wait_ge(sem["added"], o + (2 * b + half + 3))
                                nc.gpsimd.tensor_tensor(rows, out_sb[:, half, :], rows, ALU.add).then_inc(sem["added"], 1)

                        def segment(hp, b, first=False, ahead=True):
                            accumulate(hp, b)
                            if not first:
                                add_output(hp, b - 1)

                        pool.wait_ge(sem["biased"], NT)
                        pool.sem_inc(sem["added"], 2 * BATCH + 2)
                        run(pool, segment)
                        add_output(HP - 1, BATCH - 1)

                    @block.scalar
                    def _(act):
                        def split_weights(hp):
                            act.wait_ge(sem["raw"], hp * 16 + 16)
                            nc.scalar.activation(w_hi, raw[:, :], ACT.Copy).then_inc(sem["whi"], 1)

                        def evacuate(piece, hp, b):
                            i, par = hp * BATCH, b % 2
                            src = bank(RING[piece])
                            act.wait_ge(sem["proj"], i * NP + (NP * b + PIECES.index(piece) + 1))
                            if piece in VALUES:
                                n = VALUES.index(piece)
                                nc.scalar.activation(v[:, par, 2 * n:2 * n + 2, :], halves(piece)[:, :, 0, :], ACT.Copy)\
                                    .then_inc(sem["vh"], 1)
                                return
                            if piece in ("K0", "K1"):
                                for h in range(2):
                                    last = nc.scalar.activation(k_hl[0:DH, par, h, half_of(piece)], src[HEAD[h], :], ACT.Copy)
                            else:
                                for h in range(2):
                                    last = nc.scalar.activation(q_hh[0:DH, par, h, :], src[HEAD[h], :], ACT.Copy)
                            last.then_inc(sem["hi"], 1)

                        def max_rows(hp, b):
                            i, par = hp * BATCH, b % 2
                            act.wait_ge(sem["mt"], i + (b + 1))
                            for h in range(2):
                                nc.scalar.activation(q_lm[DH:DH + 1, par, h, :], bank(RING["MT"])[32 * h:32 * h + 1, :],
                                                     ACT.Copy, scale=-1.0).then_inc(sem["mrow"], 1)

                        def exps(hp, b, p):
                            i, h, kp = hp * BATCH, p % 2, p // 2
                            act.wait_ge(sem["qk"], i * 8 + (8 * b + p + 1))
                            nc.scalar.activation(probs[:, h, 2 * kp:2 * kp + 2, :],
                                                 slot(p).rearrange("p (n q) -> p n q", n=2), ACT.Exp, scale=SCALE)\
                                .then_inc(sem["exp"], 1)

                        def copy_output(hp, b):
                            o = hp * (2 * BATCH)
                            for half in range(2):
                                act.wait_ge(sem["out"], o + (2 * b + half + 1))
                                act.wait_ge(sem["added"], o + (2 * b + half + 1 + 2 * BATCH))
                                nc.scalar.activation(out_sb[:, half, :], bank(RING[f"OUT{half}"]), ACT.Copy).then_inc(sem["ocopy"], 1)

                        def segment(hp, b, first=False, ahead=True):
                            for what in ORDER:
                                if isinstance(what, int):
                                    exps(hp, b, what)
                                elif ahead and what in PIECES:
                                    evacuate(what, hp, b + 1)
                            if b == BATCH - 2 and not isinstance(hp, int):
                                act.wait_ge(sem["proj"], hp * (NP * BATCH) + NP * BATCH)
                                split_weights(hp + 1)
                            if not first:
                                copy_output(hp, b - 1)
                            if ahead:
                                max_rows(hp, b + 1)

                        act.sem_inc(sem["ocopy"], 2)
                        split_weights(0)
                        for piece in PIECES:
                            evacuate(piece, 0, 0)
                        max_rows(0, 0)
                        run(act, segment)
                        copy_output(HP - 1, BATCH - 1)

                    @block.vector
                    def _(dve):
                        dve.sem_inc(sem["norm"], 1)
                        dve.sem_inc(sem["inv"], 1)

                        def split_weights(hp):
                            dve.wait_ge(sem["whi"], hp + 1)
                            nc.vector.tensor_tensor(w_lo, raw[:, :], w_hi, ALU.subtract).then_inc(sem["wlo"], 1)

                        def low_parts(piece, hp, b):
                            i, par = hp * BATCH, b % 2
                            src = bank(RING[piece])
                            dve.wait_ge(sem["hi"], i * 3 + (3 * b + LOWS.index(piece) + 1))
                            for h in range(2):
                                if piece == "Q":
                                    nc.vector.tensor_tensor(q_lm[0:DH, par, h, :], src[HEAD[h], :],
                                                            q_hh[0:DH, par, h, :], ALU.subtract)
                                    last = nc.vector.tensor_copy(q_hh[DH:P, par, h, :], q_hh[0:DH, par, h, :])
                                else:
                                    cols = half_of(piece)
                                    nc.vector.tensor_tensor(k_hl[DH:P, par, h, cols], src[HEAD[h], :],
                                                            k_hl[0:DH, par, h, cols], ALU.subtract)
                                    last = nc.vector.tensor_copy(k_hs[0:DH, par, h, cols], k_hl[0:DH, par, h, cols])
                            last.then_inc(sem["lo"], 1)

                        def values(piece, hp, b):
                            i, par, n = hp * BATCH, b % 2, VALUES.index(piece)
                            dst = v[:, par, 2 * n:2 * n + 2, :]
                            dve.wait_ge(sem["vh"], i * NV + (NV * b + n + 1))
                            nc.vector.tensor_tensor(dst, halves(piece)[:, :, 1, :], dst, ALU.add).then_inc(sem["v"], 1)

                        def maximum(hp, b, t):
                            i = hp * BATCH
                            dve.wait_ge(sem["score"], i * 8 + (8 * b + t + 1))
                            col = 32 * (t % 2)
                            nc.vector.reduce_max(row_max[:, t // 2, col:col + 1], slot(t), axis=AX.X).then_inc(sem["max"], 1)

                        def invert(hp, b):
                            i = hp * BATCH
                            dve.wait_ge(sem["total"], i + (b + 1))
                            nc.vector.reciprocal(inv[:, :], TOTAL).then_inc(sem["inv"], 1)

                        def normalise(hp, b):
                            i = hp * BATCH
                            dve.wait_ge(sem["inv"], i + (b + 2))
                            dve.wait_ge(sem["pv"], i + (b + 1))
                            nc.vector.tensor_tensor(o_sb[:, :], O, inv[:, :], ALU.mult).then_inc(sem["norm"], 1)

                        def leave(piece, hp, b):
                            (values if piece in VALUES else low_parts)(piece, hp, b)

                        def segment(hp, b, first=False, ahead=True):
                            if not first:
                                invert(hp, b - 1)
                            for piece in PIECES:
                                if ahead:
                                    leave(piece, hp, b + 1)
                                if piece == "Q" and not first:
                                    normalise(hp, b - 1)
                            if b == BATCH - 2 and not isinstance(hp, int):
                                split_weights(hp + 1)
                            for t in range(8):
                                if ahead:
                                    maximum(hp, b + 1, t)

                        split_weights(0)
                        for piece in PIECES:
                            leave(piece, 0, 0)
                        for t in range(8):
                            maximum(0, 0, t)
                        run(dve, segment)
                        invert(HP - 1, BATCH - 1)
                        normalise(HP - 1, BATCH - 1)

                    @block.tensor
                    def _(pe):
                        def split_product(dst, terms):
                            for n, (w, m) in enumerate(terms):
                                last = nc.tensor.matmul(dst, w, m, start=n == 0, stop=n == len(terms) - 1)
                            return last

                        def project(piece, hp, b, first=False):
                            i, batch = hp * BATCH, b % BATCH
                            dst = bank(RING[piece])
                            if piece in ("K0", "K1"):
                                if piece == "K0":
                                    if batch == 0:
                                        pe.wait_ge(sem["wlo"], hp + (b // BATCH + 1))
                                    if not first:
                                        pe.wait_ge(sem["v"], i * NV + NV * b)
                                        if b > 1:
                                            pe.wait_ge(sem["ocopy"], i * 2 + 2 * (b - 1))
                                elif not first:
                                    pe.wait_ge(sem["mrow"], i * 2 + 2 * b)
                                cols = slice(batch * SKV + half_of(piece).start, batch * SKV + half_of(piece).stop)
                                last = split_product(dst, [(w_hi[:, WK[0]], ctx_hi[:, cols]), (w_hi[:, WK[0]], ctx_lo[:, cols]),
                                                           (w_lo[:, WK[0]], ctx_hi[:, cols]), (w_hi[:, WK[1]], ctx_hl[:, cols]),
                                                           (w_lo[:, WK[1]], ctx_hl[:, cols])])
                            elif piece == "Q":
                                pe.wait_ge(sem["lo"], i * 3 + (3 * b + 2))
                                rows = slice(batch * SEQ, (batch + 1) * SEQ)
                                terms = []
                                for k in range(KD):
                                    terms += [(w_hi[:, WQ[k]], xnT_hi[:, k, rows]), (w_hi[:, WQ[k]], xnT_lo[:, k, rows]),
                                              (w_lo[:, WQ[k]], xnT_hi[:, k, rows])]
                                last = split_product(dst, terms)
                            else:
                                if piece == "V0":
                                    pe.wait_ge(sem["lo"], i * 3 + (3 * b + 1))
                                elif piece == "V2":
                                    pe.wait_ge(sem["lo"], i * 3 + (3 * b + 3))
                                else:
                                    pe.wait_ge(sem["v"], i * NV + (NV * b + (1 if piece == "V1" else 2)))
                                for n in range(2):
                                    col = batch * SKV + (2 * VALUES.index(piece) + n) * P
                                    keys = slice(col, col + P)
                                    both = dst[:, n * 2 * P:(n + 1) * 2 * P].rearrange("p (w d) -> p w d", w=2)
                                    nc.tensor.matmul(both, ctx_hi[:, keys], w_split[:, :, WV[0]], start=True, stop=False)
                                    nc.tensor.matmul(both, ctx_hl[:, keys], w_split[:, :, WV[1]], start=False, stop=False)
                                    last = nc.tensor.matmul(both[:, 0, :], ctx_lo[:, keys], w_hi[:, WV[0]], start=False, stop=True)
                            last.then_inc(sem["proj"], 1)

                        def score(hp, b, t, first=False):
                            i, par, h, qt = hp * BATCH, b % 2, t % 2, t // 2
                            if t == 0:
                                pe.wait_ge(sem["lo"], i * 3 + (3 * b + 3))
                            if t >= 2:
                                pe.wait_ge(sem["max"], i * 8 + (8 * b + t - 1))
                            elif not first:
                                pe.wait_ge(sem["exp"], i * 8 + (8 * b + t - 1))
                            for half in range(2):
                                last = nc.tensor.matmul(slot(t)[:, half * BANK:(half + 1) * BANK],
                                                        q_hh[:, par, h, qt * P:(qt + 1) * P],
                                                        k_hl[:, par, h, half * BANK:(half + 1) * BANK], start=True, stop=True)
                            last.then_inc(sem["score"], 1)

                        def transpose_max(hp, b):
                            i = hp * BATCH
                            pe.wait_ge(sem["max"], i * 8 + (8 * b + 8))
                            for qt in range(QT):
                                last = nc.tensor.transpose(bank(RING["MT"])[:, qt * P:(qt + 1) * P], row_max[:, qt, :], ident[:, :])
                            last.then_inc(sem["mt"], 1)

                        def qk(hp, b, p):
                            i, par, h, kp = hp * BATCH, b % 2, p % 2, p // 2
                            if p == 0:
                                pe.wait_ge(sem["mrow"], i * 2 + (2 * b + 2))
                            if p < 2:
                                pe.wait_ge(sem["max"], i * 8 + (8 * b + 7 + p))
                            else:
                                pe.wait_ge(sem["exp"], i * 8 + (8 * b + p - 1))
                            for n in range(2):
                                keys = slice((2 * kp + n) * P, (2 * kp + n + 1) * P)
                                dst = slot(p)[:, n * BANK:(n + 1) * BANK]
                                nc.tensor.matmul(dst, k_hl[:, par, h, keys], q_hh[:, par, h, :], start=True, stop=False)
                                last = nc.tensor.matmul(dst, k_hs[0:DH + 1, par, h, keys], q_lm[0:DH + 1, par, h, :],
                                                        start=False, stop=True)
                            last.then_inc(sem["qk"], 1)

                        def pv(hp, b, kv):
                            i, par = hp * BATCH, b % 2
                            if kv == 0:
                                pe.wait_ge(sem["norm"], i + (b + 1))
                            if kv % 2 == 0:
                                pe.wait_ge(sem["v"], i * NV + (NV * b + kv // 2 + 1))
                                pe.wait_ge(sem["exp"], i * 8 + (8 * b + kv + 2))
                            for h in range(2):
                                last = nc.tensor.matmul(O[HEAD[h], :], v[:, par, kv, HEAD[h]], probs[:, h, kv, :],
                                                        start=kv == 0, stop=kv == KVT - 1)
                            if kv == KVT - 1:
                                last.then_inc(sem["pv"], 1)

                        def total(hp, b):
                            i = hp * BATCH
                            pe.wait_ge(sem["acc"], i * (2 * KVT - 2) + (2 * KVT - 2) * (b + 1))
                            pe.wait_ge(sem["inv"], i + (b + 1))
                            for h in range(2):
                                last = nc.tensor.matmul(TOTAL[HEAD[h], :], ones[:, :], psums[:, h, :], start=True, stop=True)
                            last.then_inc(sem["total"], 1)

                        def output(hp, b, half, ahead=True):
                            i = hp * BATCH
                            if half == 0:
                                pe.wait_ge(sem["norm"], i + (b + 2))
                                pe.wait_ge(sem["wo"], (hp + b // BATCH) * 16 + 16)
                                if ahead:
                                    pe.wait_ge(sem["v"], i * NV + (NV * (b + 3) - 1))
                            elif ahead:
                                pe.wait_ge(sem["v"], i * NV + NV * (b + 3))
                            if not ahead:
                                pe.wait_ge(sem["ocopy"], i * 2 + (2 * b + half + 1))
                            for n in range(2):
                                t = 2 * half + n
                                last = nc.tensor.matmul(bank(RING[f"OUT{half}"])[:, n * DIM:(n + 1) * DIM],
                                                        o_sb[:, t * P:(t + 1) * P], wo_sb[:, :], start=True, stop=True)
                            last.then_inc(sem["out"], 1)

                        def segment(hp, b, first=False, ahead=True):
                            for what in ORDER:
                                if isinstance(what, int):
                                    qk(hp, b, what)
                                elif what in PIECES:
                                    if ahead:
                                        project(what, hp, b + 1)
                                elif not first:
                                    pv(hp, b - 1, int(what[1]))
                            for t in range(8):
                                if ahead:
                                    score(hp, b + 1, t)
                                if not first and t >= 6:
                                    output(hp, b - 1, t - 6, ahead)
                                if t < KVT - LATE:
                                    pv(hp, b, t)
                            total(hp, b)
                            if ahead:
                                if not first:
                                    pe.wait_ge(sem["ocopy"], hp * (2 * BATCH) + (2 * b + 1))
                                transpose_max(hp, b + 1)

                        pe.wait_ge(sem["one"], 5)
                        for piece in PIECES:
                            project(piece, 0, 0, first=True)
                        for t in range(8):
                            score(0, 0, t, first=True)
                        transpose_max(0, 0)
                        run(pe, segment)
                        for kv in range(KVT - LATE, KVT):
                            pv(HP - 1, BATCH - 1, kv)
                        for half in range(2):
                            output(HP - 1, BATCH - 1, half, ahead=False)

        def route_phase(tag, cfg, router, bias, weights_of, place=None, prefetch=None):
            E, per = cfg["experts"], cfg["per"]
            G = cfg["groups"]
            with scope() as s:
                rt = sb(s, tag + "rt", [P, KD, E])
                rt_hi = sb(s, tag + "rt_hi", [P, KD, P], F32R)
                rt_lo = sb(s, tag + "rt_lo", [P, KD, P], F32R)
                logits_T = sb(s, tag + "logits_T", [E, BLK, BANK])
                scores = sb(s, tag + "scores", [P, NT, E])
                choice = sb(s, tag + "choice", [P, NT, E])
                eq, gt, sel, start = (sb(s, tag + n, [P, NT, E]) for n in ("eq", "gt", "sel", "start"))
                top = sb(s, tag + "top", [P, NT, 8])
                need = sb(s, tag + "need", [P, NT])
                if G:
                    bias_sb = sb(s, tag + "rbias", [P, E])
                    gmax, geq, ggt, gsel, gstart = (sb(s, tag + n, [P, NT, G]) for n in ("gmax", "geq", "ggt", "gsel", "gstart"))
                if place is not None:
                    slot_of, expert_of = place
                    earlier = sb(s, tag + "earlier", [P, P])
                    every = sb(s, tag + "every", [P, P])
                    index, slots, tile_expert = (sb(s, tag + n, [P, n_]) for n, n_ in
                                                 (("index", TILES), ("slots", NT), ("tile_expert", TILES)))
                    held, upto, over = (sb(s, tag + n, [P, E, NT]) for n in ("held", "upto", "over"))
                    tiles, end = (sb(s, tag + n, [P, E]) for n in ("tiles", "end"))
                    past = sb(s, tag + "past", [P, TILES, E])
                sem = sems(s, tag, "rt pad hi lo logits copied turned scores step" + (" bias" if G else "") + (" const picked counted" if place else ""))
                with nc.Block() as block:

                    @block.sync
                    def _(sp):
                        sp.dma_start(rt[:, :, :], router).then_inc(sem["rt"], 16)
                        if prefetch is not None:
                            prefetch(sp)
                        if G:
                            sp.dma_start(bias_sb[:, :], bias.partition_broadcast(P)).then_inc(sem["bias"], 16)

                    @block.gpsimd
                    def _(pool):
                        for part in (rt_hi, rt_lo):
                            nc.gpsimd.memset(part[:, :, :].bitcast(F32), 0.0).then_inc(sem["pad"], 1)
                        if place is not None:
                            nc.gpsimd.memset(every[:, :], 1.0).then_inc(sem["const"], 1)
                            pool.wait_ge(sem["const"], 1)
                            nc.gpsimd.affine_select(out=earlier[:, :], in_=every[:, :], compare_op=ALU.is_gt, fill=0.0, base=0,
                                                    pattern=[[1, P]], channel_multiplier=-1).then_inc(sem["const"], 1)

                    @block.scalar
                    def _(act):
                        act.wait_ge(sem["rt"], 16)
                        act.wait_ge(sem["pad"], 2)
                        nc.scalar.activation(rt_hi[:, :, 0:E], rt[:, :, :], ACT.Copy).then_inc(sem["hi"], 1)
                        for blk in range(BLK):
                            act.wait_ge(sem["logits"], blk + 1)
                            nc.scalar.activation(logits_T[:, blk, :], bank(blk)[0:E, :], ACT.Copy).then_inc(sem["copied"], 1)
                        act.wait_ge(sem["turned"], 1)
                        nc.scalar.activation(scores[:, :, :], bank(BLK, NT * E).rearrange("p (t e) -> p t e", e=E),
                                             ACT.Sigmoid if G else ACT.Copy).then_inc(sem["scores"], 1)

                    @block.tensor
                    def _(pe):
                        pe.wait_ge(sem["lo"], 1)
                        for blk in range(BLK):
                            rows = slice(blk * BANK, (blk + 1) * BANK)
                            n = 0
                            for k in range(KD):
                                for w, a in ((rt_hi, xnT_hi), (rt_hi, xnT_lo), (rt_lo, xnT_hi)):
                                    last = nc.tensor.matmul(bank(blk), w[:, k, :], a[:, k, rows], start=n == 0, stop=n == 3 * KD - 1)
                                    n += 1
                            last.then_inc(sem["logits"], 1)
                        for t in range(NT):
                            blk, n = divmod(t, NT // BLK)
                            pe.wait_ge(sem["copied"], blk + 1)
                            last = nc.tensor.transpose(bank(BLK)[:, t * E:(t + 1) * E], logits_T[:, blk, n * P:(n + 1) * P],
                                                       ident[0:E, 0:E])
                        last.then_inc(sem["turned"], 1)
                        if place is not None:
                            pe.wait_ge(sem["const"], 2)
                            pe.wait_ge(sem["picked"], 1)
                            picked = sel[:, :, :].rearrange("p t e -> p (t e)")
                            nc.tensor.matmul(bank(BLK + 1, NT * E), earlier[:, :], picked, start=True, stop=True)
                            nc.tensor.matmul(bank(BLK + 2, NT * E), every[:, :], picked, start=True, stop=True)\
                                .then_inc(sem["counted"], 1)

                    @block.vector
                    def _(dve):
                        dve.wait_ge(sem["hi"], 1)
                        nc.vector.tensor_tensor(rt_lo[:, :, 0:E], rt[:, :, :], rt_hi[:, :, 0:E], ALU.subtract).then_inc(sem["lo"], 1)
                        n = 0

                        def link(ins):
                            nonlocal n
                            n += 1
                            ins.then_inc(sem["step"], 1)
                            dve.wait_ge(sem["step"], n)

                        def flat(a):
                            return a.rearrange("p t n -> p (t n)")

                        def wide(a, n):
                            return a.unsqueeze(2).broadcast_to([P, NT, n])

                        def pick(v, k, n, eq, gt, sel, start):
                            link(nc.vector.memset(start[:, :, :], 1.0))
                            link(nc.vector.memset(start[:, :, 0:1], 0.0))
                            for t in range(NT):
                                last = nc.vector.max(top[:, t, :], v[:, t, :])
                            link(last)
                            kth = top[:, :, k - 1:k].broadcast_to([P, NT, n])
                            link(nc.vector.tensor_tensor(gt[:, :, :], v[:, :, :], kth, ALU.is_gt))
                            link(nc.vector.tensor_tensor(eq[:, :, :], v[:, :, :], kth, ALU.is_equal))
                            link(nc.vector.reduce_sum(need[:, :], gt[:, :, :], axis=AX.X))
                            link(nc.vector.tensor_scalar(need[:, :], need[:, :], -1.0, float(k), ALU.mult, ALU.add))
                            link(nc.vector.tensor_tensor_scan(flat(sel[:, :, :]), flat(start[:, :, :]), flat(eq[:, :, :]), 0.0,
                                                              ALU.mult, ALU.add))
                            link(nc.vector.tensor_tensor(sel[:, :, :], sel[:, :, :], wide(need[:, :], n), ALU.is_le))
                            link(nc.vector.tensor_tensor(eq[:, :, :], eq[:, :, :], sel[:, :, :], ALU.mult))
                            link(nc.vector.tensor_tensor(sel[:, :, :], gt[:, :, :], eq[:, :, :], ALU.add))

                        def sort_tokens():
                            nc.vector.memset(start[:, :, 0:1], 0.0).then_inc(sem["picked"], 1)
                            link(nc.vector.memset(index[:, :], 1.0))
                            link(nc.vector.tensor_tensor_scan(tile_expert[:, :], index[:, :], index[:, :], 0.0, ALU.mult, ALU.add))
                            link(nc.vector.tensor_scalar(index[:, :], tile_expert[:, :], -1.0, None, ALU.add))
                            link(nc.vector.memset(over[:, :, :], 1.0))
                            link(nc.vector.memset(over[:, :, 0:1], 0.0))
                            dve.wait_ge(sem["counted"], 1)
                            link(nc.vector.tensor_copy(held[:, :, :], bank(BLK + 2, NT * E).rearrange("p (t e) -> p e t", e=E)))
                            link(nc.vector.tensor_tensor_scan(upto[:, :, :].rearrange("p e t -> p (e t)"),
                                                              over[:, :, :].rearrange("p e t -> p (e t)"),
                                                              held[:, :, :].rearrange("p e t -> p (e t)"), 0.0, ALU.mult, ALU.add))
                            link(nc.vector.tensor_scalar(tiles[:, :], upto[:, :, NT - 1], 1.0 / P, None, ALU.mult))
                            link(nc.vector.tensor_tensor(over[:, :, :], tiles[:, :].unsqueeze(2).broadcast_to([P, E, NT]),
                                                         index[:, 0:NT].unsqueeze(1).broadcast_to([P, E, NT]), ALU.is_gt))
                            link(nc.vector.reduce_sum(tiles[:, :], over[:, :, :], axis=AX.X))
                            link(nc.vector.memset(need[:, 0:E], 1.0))
                            link(nc.vector.tensor_tensor_scan(end[:, :], need[:, 0:E], tiles[:, :], 0.0, ALU.mult, ALU.add))
                            link(nc.vector.tensor_tensor(past[:, :, :], end[:, :].unsqueeze(1).broadcast_to([P, TILES, E]),
                                                         index[:, :].unsqueeze(2).broadcast_to([P, TILES, E]), ALU.is_le))
                            link(nc.vector.reduce_sum(tile_expert[:, :], past[:, :, :], axis=AX.X))
                            link(nc.vector.tensor_scalar(expert_of[:, :], tile_expert[:, :], E - 1.0, None, ALU.min))
                            link(nc.vector.tensor_tensor(tiles[:, :], end[:, :], tiles[:, :], ALU.subtract))
                            link(nc.vector.tensor_scalar(tiles[:, :], tiles[:, :], float(P), None, ALU.mult))
                            link(nc.vector.tensor_tensor(upto[:, :, :], upto[:, :, :], held[:, :, :], ALU.subtract))
                            link(nc.vector.tensor_tensor(upto[:, :, :], upto[:, :, :],
                                                         tiles[:, :].unsqueeze(2).broadcast_to([P, E, NT]), ALU.add))
                            link(nc.vector.tensor_tensor(gt[:, :, :], bank(BLK + 1, NT * E).rearrange("p (t e) -> p t e", e=E),
                                                         upto[:, :, :].rearrange("p e t -> p t e"), ALU.add))
                            link(nc.vector.tensor_tensor(gt[:, :, :], gt[:, :, :], sel[:, :, :], ALU.mult))
                            link(nc.vector.reduce_sum(slots[:, :], gt[:, :, :], axis=AX.X))
                            link(nc.vector.tensor_copy(slot_of[:, :], slots[:, :]))

                        dve.wait_ge(sem["scores"], 1)
                        if G:
                            dve.wait_ge(sem["bias"], 16)
                            link(nc.vector.tensor_tensor(choice[:, :, :], scores[:, :, :],
                                                         bias_sb[:, :].unsqueeze(1).broadcast_to([P, NT, E]), ALU.add))
                            link(nc.vector.reduce_max(flat(gmax[:, :, :]), flat(choice[:, :, :])
                                                      .rearrange("p (g m) -> p g m", m=E // G), axis=AX.X))
                            pick(gmax, cfg["top_groups"], G, geq, ggt, gsel, gstart)
                            link(nc.vector.tensor_tensor(
                                flat(choice[:, :, :]).rearrange("p (g m) -> p g m", m=E // G),
                                flat(choice[:, :, :]).rearrange("p (g m) -> p g m", m=E // G),
                                flat(gsel[:, :, :]).unsqueeze(2).broadcast_to([P, NT * G, E // G]), ALU.mult))
                            pick(choice, cfg["top"], E, eq, gt, sel, start)
                            link(nc.vector.tensor_tensor(sel[:, :, :], sel[:, :, :], scores[:, :, :], ALU.mult))
                            link(nc.vector.reduce_sum(need[:, :], sel[:, :, :], axis=AX.X))
                            link(nc.vector.tensor_scalar(need[:, :], need[:, :], 1e-20, None, ALU.add))
                            link(nc.vector.reciprocal(need[:, :], need[:, :]))
                            link(nc.vector.tensor_scalar(need[:, :], need[:, :], cfg["scale"], None, ALU.mult))
                            link(nc.vector.tensor_tensor(sel[:, :, :], sel[:, :, :], wide(need[:, :], E), ALU.mult))
                        else:
                            pick(scores, cfg["top"], E, eq, gt, sel, start)
                        first = cfg["shared"] * NT
                        link(nc.vector.memset(weights_of[:, 0:first], 1.0))
                        if place is not None:
                            sort_tokens()
                        for c in range(per if place is None else 0):
                            link(nc.vector.tensor_copy(
                                weights_of[:, first:].rearrange("p (e c t) -> p c t e", c=per, t=NT)[:, c, :, :], sel[:, :, :]))

        expert_sems = sems(stack, "e", "raw0 raw1 whi wlo gu silu mul hhi hlo down fma")

        def expert_phase(tag, chunks, packed, weights_of, xres, dispatch=None):
            with scope() as s:
                raw = sb(s, tag + "raw", [P, 2, MCOL])
                w_hi = sb(s, tag + "w_hi", [P, 2, MCOL], F32R)
                w_lo = sb(s, tag + "w_lo", [P, 2, MCOL], F32R)
                act_g = sb(s, tag + "act_g", [P, 2, BANK])
                hid = sb(s, tag + "hid", [P, 2, BANK])
                hid_hi = sb(s, tag + "hid_hi", [P, 4, BANK], F32R)
                hid_lo = sb(s, tag + "hid_lo", [P, 4, BANK], F32R)
                sem = expert_sems
                sent = [s.enter_context(nc.semaphore(f"{tag}sent{n}")) for n in range(NT)] if dispatch else []
                UNITS = chunks * BLK
                ROUND = 2 * BLK
                ROUNDS = UNITS // ROUND
                TB = NT // BLK
                with nc.Block() as block:

                    def run(eng, unit):
                        unit(0, 0)
                        unit(0, 1)
                        with eng.Fori(0, ROUNDS - 1) as j:
                            for u in range(2, ROUND + 2):
                                unit(j, u)
                        for u in range(2, ROUND):
                            unit(ROUNDS - 1, u)

                    @block.sync
                    def _(sp):
                        with sp.Fori(0, chunks // 2) as j:
                            for par in range(2):
                                sp.wait_ge(sem["wlo"], j * 2 + (par + 1))
                                sp.dma_start(raw[:, par, :], packed[ds(j * 2 + par, 1), :, :].rearrange("a p c -> (a p) c"))\
                                    .then_inc(sem[f"raw{par}"], 16)
                    @block.gpsimd
                    def _(pool):
                        pool.sem_inc(sem["wlo"], 2)
                        with pool.Fori(0, chunks // 2) as j:
                            for par in range(2):
                                pool.wait_ge(sem["whi"], j * 2 + (par + 1))
                                nc.gpsimd.tensor_tensor(w_lo[:, par, :], raw[:, par, :], w_hi[:, par, :], ALU.subtract)\
                                    .then_inc(sem["wlo"], 1)
                        if dispatch is not None:
                            rows, slot_of = dispatch
                            for t in range(NT):
                                nc.gpsimd.indirect_dma_start(sorted_x, bass.IndirectOffsetOnAxis(ap=slot_of[:, t:t + 1], axis=0),
                                                             rows[:, t, :], None).then_inc(sent[t], 16)
                            for done in sent:
                                pool.wait_ge(done, 16)

                    @block.scalar
                    def _(act):
                        def split(j, c):
                            act.wait_ge(sem[f"raw{c % 2}"], j * 16 + 16 * (c // 2 + 1))
                            nc.scalar.activation(w_hi[:, c % 2, :], raw[:, c % 2, :], ACT.Copy).then_inc(sem["whi"], 1)

                        def unit(j, u):
                            k = j * ROUND
                            if u % BLK == 2 and not (isinstance(j, int) and j == ROUNDS - 1 and u == ROUND - 2):
                                c = u // BLK + 1
                                act.wait_ge(sem["down"], k + BLK * c)
                                split(j, c)
                            act.wait_ge(sem["gu"], k + (u + 1))
                            act.wait_ge(sem["mul"], k + (u + 1))
                            nc.scalar.activation(act_g[:, u % 2, :], bank(u % 2), ACT.Silu).then_inc(sem["silu"], 1)
                            act.wait_ge(sem["mul"], k + (u + 3))
                            act.wait_ge(sem["down"], k + (u + 1))
                            nc.scalar.activation(hid_hi[:, u % 4, :], hid[:, u % 2, :], ACT.Copy).then_inc(sem["hhi"], 1)

                        split(0, 0)
                        run(act, unit)

                    @block.vector
                    def _(dve):
                        dve.sem_inc(sem["mul"], 2)
                        dve.sem_inc(sem["fma"], 4)

                        def add(j, u):
                            k = j * ROUND
                            dve.wait_ge(sem["down"], k + (u + 5))
                            dve.wait_ge(sem["fma"], k + (u + 1))
                            for n in range(TB):
                                t = (u % BLK) * TB + n
                                acc = xres[:, t, :]
                                last = nc.vector.scalar_tensor_tensor(
                                    acc, bank(4 + 2 * (u % 2) + n // 2)[:, (n % 2) * DIM:(n % 2 + 1) * DIM],
                                    weights_of[:, ds(j * (2 * NT) + ((u // BLK) * NT + t), 1)], acc, ALU.mult, ALU.add)
                            last.then_inc(sem["fma"], 1)

                        def unit(j, u):
                            k = j * ROUND
                            dve.wait_ge(sem["silu"], k + (u + 1))
                            nc.vector.tensor_tensor(hid[:, u % 2, :], bank(2 + u % 2), act_g[:, u % 2, :], ALU.mult)\
                                .then_inc(sem["mul"], 1)
                            if u >= 2:
                                add(j, u - 2)
                            dve.wait_ge(sem["hhi"], k + (u + 1))
                            nc.vector.tensor_tensor(hid_lo[:, u % 4, :], hid[:, u % 2, :], hid_hi[:, u % 4, :], ALU.subtract)\
                                .then_inc(sem["hlo"], 1)

                        run(dve, unit)
                        add(ROUNDS - 1, ROUND - 2)
                        add(ROUNDS - 1, ROUND - 1)

                    @block.tensor
                    def _(pe):
                        pe.sem_inc(sem["down"], 4)

                        def gate_up(j, u):
                            k, par = j * ROUND, (u // BLK) % 2
                            rows = slice((u % BLK) * BANK, (u % BLK + 1) * BANK)
                            if u % BLK == 0:
                                pe.wait_ge(sem["wlo"], j * 2 + (u // BLK + 3))
                            pe.wait_ge(sem["mul"], k + (u + 1))
                            for g in range(2):
                                n = 0
                                for kd in range(KD):
                                    w = slice((g * KD + kd) * P, (g * KD + kd + 1) * P)
                                    for a, m in ((w_hi, xnT_hi), (w_hi, xnT_lo), (w_lo, xnT_hi)):
                                        last = nc.tensor.matmul(bank(2 * g + u % 2), a[:, par, w], m[:, kd, rows],
                                                                start=n == 0, stop=n == 3 * KD - 1)
                                        n += 1
                            last.then_inc(sem["gu"], 1)

                        def down(j, u):
                            k, par = j * ROUND, (u // BLK) % 2
                            w = slice(2 * KD * P, MCOL)
                            pe.wait_ge(sem["hlo"], k + (u + 1))
                            pe.wait_ge(sem["fma"], k + (u + 3))
                            for n in range(TB):
                                dst = bank(4 + 2 * (u % 2) + n // 2)[:, (n % 2) * DIM:(n % 2 + 1) * DIM]
                                rows = slice(n * P, (n + 1) * P)
                                for m, (a, b) in enumerate(((hid_hi, w_hi), (hid_hi, w_lo), (hid_lo, w_hi))):
                                    last = nc.tensor.matmul(dst, a[:, u % 4, rows], b[:, par, w], start=m == 0, stop=m == 2)
                            last.then_inc(sem["down"], 1)

                        def unit(j, u):
                            gate_up(j, u)
                            if u >= 2:
                                down(j, u - 2)

                        run(pe, unit)
                        down(ROUNDS - 1, ROUND - 2)
                        down(ROUNDS - 1, ROUND - 1)

        def sorted_phase(tag, weights, loaded, place, rows, xres, store):
            slot_of, expert_of = place
            per = HID // P
            x_slots = sorted_x.rearrange("(t p) d -> t p d", p=P)
            y_slots = sorted_y.rearrange("(t p) d -> t p d", p=P)
            with scope() as s:
                xs = sb(s, tag + "xs", [P, 2, DIM])
                xsT = sb(s, tag + "xsT", [P, 2, KD * P])
                gated = sb(s, tag + "gated", [P, 2, HID])
                hid = sb(s, tag + "hid", [P, 2, HID])
                hidT = sb(s, tag + "hidT", [P, 2, HID])
                y = sb(s, tag + "y", [P, 2, DIM])
                sem = sems(s, tag, "xs0 xs1 xt xcopy gu silu mul ht hcopy down ycopy y0 y1 sum out")
                back = [s.enter_context(nc.semaphore(f"{tag}back{n}")) for n in range(NT)]
                OUTS = 4
                LOOP = (TILES - 4) // 2
                with nc.Block() as block:

                    def there(r, u):
                        return not isinstance(r, int) or 0 <= 2 * r + u < TILES

                    def run(eng, step):
                        for u in (-1, 0, 1, 2):
                            step(0, u)
                        with eng.Fori(0, LOOP) as r:
                            for u in (3, 4):
                                step(r, u)
                        for u in range(3, TILES + 3 - 2 * LOOP):
                            step(LOOP, u)

                    def tile(a, r, u):
                        return a[ds(r * 2 + u, 1), :, :].rearrange("a p d -> (a p) d")

                    @block.sync
                    def _(sp):
                        def load(r, u):
                            sp.wait_ge(sem["xt"], r * 2 + (u + 1))
                            sp.dma_start(xs[:, u % 2, :], tile(x_slots, r, u)).then_inc(sem[f"xs{u % 2}"], 16)

                        with sp.Fori(0, TILES // 2) as r:
                            for u in range(2):
                                load(r, u)
                        for u in range(TILES % 2):
                            load(TILES // 2, u)
                        n = NT // OUTS
                        for part in range(OUTS):
                            sp.wait_ge(sem["sum"], n * (part + 1))
                            sp.dma_start(store[:, part * n:(part + 1) * n, :], xres[:, part * n:(part + 1) * n, :])\
                                .then_inc(sem["out"], 16)
                            sp.wait_ge(sem["out"], 16 * (part + 1))

                    @block.gpsimd
                    def _(pool):
                        for par in range(2):
                            pool.wait_ge(sem[f"y{par}"], 16 * ((TILES + 1 - par) // 2 + 1))
                        for t in range(NT):
                            nc.gpsimd.indirect_dma_start(rows[:, t, :], None, sorted_y,
                                                         bass.IndirectOffsetOnAxis(ap=slot_of[:, t:t + 1], axis=0))\
                                .then_inc(back[t], 16)

                    @block.scalar
                    def _(act):
                        act.sem_inc(sem["hcopy"], 1)
                        for par in range(2):
                            act.sem_inc(sem[f"y{par}"], 16)

                        def step(r, u):
                            k = r * 2
                            if there(r, u + 1):
                                act.wait_ge(sem["xt"], k + (u + 4))
                                act.wait_ge(sem["gu"], k + (u + 2))
                                nc.scalar.activation(xsT[:, (u + 1) % 2, :], bank(5, KD * P), ACT.Copy).then_inc(sem["xcopy"], 1)
                            if there(r, u):
                                act.wait_ge(sem["gu"], k + (u + 3))
                                act.wait_ge(sem["mul"], k + (u + 1))
                                nc.scalar.activation(gated[:, u % 2, :], bank(u % 2), ACT.Silu).then_inc(sem["silu"], 1)
                            if there(r, u - 1):
                                act.wait_ge(sem["ht"], k + (u + 2))
                                act.wait_ge(sem["down"], k + u)
                                nc.scalar.activation(hidT[:, (u - 1) % 2, :], bank(4), ACT.Copy).then_inc(sem["hcopy"], 1)
                            if there(r, u - 3):
                                act.wait_ge(sem["ycopy"], k + u)
                                act.dma_start(tile(y_slots, r, u - 3), y[:, (u - 3) % 2, :]).then_inc(sem[f"y{(u - 3) % 2}"], 16)

                        run(act, step)

                    @block.vector
                    def _(dve):
                        dve.sem_inc(sem["mul"], 2)
                        dve.sem_inc(sem["ycopy"], 2)

                        def step(r, u):
                            k = r * 2
                            if there(r, u):
                                dve.wait_ge(sem["silu"], k + (u + 1))
                                dve.wait_ge(sem["ht"], k + (u + 1))
                                nc.vector.tensor_tensor(hid[:, u % 2, :], bank(2 + u % 2), gated[:, u % 2, :], ALU.mult)\
                                    .then_inc(sem["mul"], 1)
                            if there(r, u - 2):
                                dve.wait_ge(sem["down"], k + (u + 1))
                                dve.wait_ge(sem[f"y{u % 2}"], r * 16 + 16 * (u // 2))
                                nc.vector.tensor_copy(y[:, u % 2, :], bank(6 + u % 2, DIM)).then_inc(sem["ycopy"], 1)

                        run(dve, step)
                        for t in range(NT):
                            dve.wait_ge(back[t], 16)
                            nc.vector.tensor_tensor(xres[:, t, :], xres[:, t, :], rows[:, t, :], ALU.add).then_inc(sem["sum"], 1)

                    @block.tensor
                    def _(pe):
                        for n in ("xt", "gu", "ht", "down"):
                            pe.sem_inc(sem[n], 2)
                        for part in loaded:
                            pe.wait_ge(part, 16)

                        def expert(r, u):
                            e = nc.tensor.value_load(expert_of[0:1, ds(r * 2 + u, 1)], min_val=0, max_val=SORTED["experts"] - 1)
                            return lambda first, n: weights[:, ds(e, 1), first:first + n].rearrange("p a c -> p (a c)")

                        def step(r, u):
                            k = r * 2
                            if there(r, u + 1):
                                pe.wait_ge(sem[f"xs{(u + 1) % 2}"], r * 16 + 16 * ((u + 1) // 2 + 1))
                                if there(r, u):
                                    pe.wait_ge(sem["xcopy"], k + (u + 1))
                                for kd in range(KD):
                                    cols = slice(kd * P, (kd + 1) * P)
                                    last = nc.tensor.transpose(bank(5)[:, cols], xs[:, (u + 1) % 2, cols], ident[:, :])
                                last.then_inc(sem["xt"], 1)
                            if there(r, u):
                                w = expert(r, u)
                                pe.wait_ge(sem["xcopy"], k + (u + 1))
                                pe.wait_ge(sem["mul"], k + (u + 1))
                                for g in range(2):
                                    for kd in range(KD):
                                        last = nc.tensor.matmul(bank(2 * g + u % 2), xsT[:, u % 2, kd * P:(kd + 1) * P],
                                                                w((g * KD + kd) * HID, HID), start=kd == 0, stop=kd == KD - 1)
                                last.then_inc(sem["gu"], 1)
                            if there(r, u - 1):
                                pe.wait_ge(sem["mul"], k + (u + 2))
                                pe.wait_ge(sem["hcopy"], k + u)
                                for c in range(per):
                                    cols = slice(c * P, (c + 1) * P)
                                    last = nc.tensor.transpose(bank(4)[:, cols], hid[:, (u - 1) % 2, cols], ident[:, :])
                                last.then_inc(sem["ht"], 1)
                            if there(r, u - 2):
                                w = expert(r, u - 2)
                                pe.wait_ge(sem["hcopy"], k + u)
                                pe.wait_ge(sem["ycopy"], k + (u - 1))
                                for c in range(per):
                                    last = nc.tensor.matmul(bank(6 + u % 2, DIM), hidT[:, u % 2, c * P:(c + 1) * P],
                                                            w(2 * KD * HID + c * DIM, DIM), start=c == 0, stop=c == per - 1)
                                last.then_inc(sem["down"], 1)

                        run(pe, step)

        w = layer_in[0]
        cfg = LAYERS[0]
        norm_phase("n_", xres, x_tiles)
        attention_phase("L0a_", w["attention"], w["out"], w["out_bias"], xres)
        norm_phase("L0n_", xres, wipe=sorted_x, clear=attention_sems.values())
        with scope() as s:
            chunks = cfg["experts"] * cfg["per"] + cfg["shared"]
            weights_of = sb(s, "L0weights_of", [P, chunks * NT])
            route_phase("L0r_", cfg, w["router"], w["router_bias"], weights_of)
            expert_phase("L0e_", chunks, w["experts"], weights_of, xres)
        w = layer_in[1]
        cfg = LAYERS[1]
        norm_phase("L1i_", xres, clear=expert_sems.values())
        attention_phase("L1a_", w["attention"], w["out"], w["out_bias"], xres)
        ctx_scope.close()
        with scope() as s:
            weights_of = sb(s, "L1weights_of", [P, cfg["shared"] * NT])
            place = sb(s, "L1slot_of", [P, NT], I32), sb(s, "L1expert_of", [P, TILES], I32)
            rows = sb(s, "L1rows", [P, NT, DIM])
            weights = sb(s, "L1weights", [P, cfg["experts"], ECOL])
            loaded = [s.enter_context(nc.semaphore(f"L1loaded{n}")) for n in range(2)]
            parts = slice(0, 5), slice(5, cfg["experts"])

            def load(n):
                return lambda sp: sp.dma_start(weights[:, parts[n], :], w["sorted"][parts[n], :, :].rearrange("e p c -> p e c"))\
                    .then_inc(loaded[n], 16)

            norm_phase("L1n_", xres, keep=rows, prefetch=load(0))
            route_phase("L1r_", cfg, w["router"], None, weights_of, place, prefetch=load(1))
            expert_phase("L1e_", cfg["shared"], w["experts"], weights_of, xres, (rows, place[0]))
            sorted_phase("L1s_", weights, loaded, place, rows, xres, out_tiles)


def kernel(**inputs):
    import numpy as np
    import concourse.bacc as bacc
    from concourse.bass_utils import run_bass_kernel_spmd

    a = {k: np.asarray(v) for k, v in inputs.items()}

    def pairs(wq, wk, wv):
        out = []
        for hp in range(HP):
            c = slice(hp * P, (hp + 1) * P)
            cols = [wq[k * P:(k + 1) * P, c] for k in range(KD)]
            for w in (wk, wv):
                cols += [w[:P, c], np.concatenate([w[P:, c], w[P:, c]], axis=0)]
            out.append(np.concatenate(cols, axis=1))
        return np.ascontiguousarray(np.stack(out))

    def chunk(gate, up, down):
        cols = [m[:, k * P:(k + 1) * P].T for m in (gate, up) for k in range(KD)]
        return np.concatenate(cols + [down.T], axis=1)

    def router(w):
        return np.ascontiguousarray(w.T.reshape(KD, P, w.shape[0]).transpose(1, 0, 2))

    H = P
    packed0 = [chunk(a["L0_ffn_shared_gate_w"][c * H:(c + 1) * H], a["L0_ffn_shared_up_w"][c * H:(c + 1) * H],
                     a["L0_ffn_shared_down_w"][:, c * H:(c + 1) * H]) for c in range(LAYERS[0]["shared"])]
    packed0 += [chunk(gu[:H], gu[H:], dn) for gu, dn in zip(a["L0_ffn_experts_gate_up"], a["L0_ffn_experts_down"])]
    packed1 = [chunk(a["L1_ffn_w_gate_s"][c * H:(c + 1) * H], a["L1_ffn_w_up_s"][c * H:(c + 1) * H],
                     a["L1_ffn_w_down_s"][:, c * H:(c + 1) * H]) for c in range(LAYERS[1]["shared"])]

    def sorted_expert(gate, up, down):
        cols = [m[:, k * P:(k + 1) * P].T for m in (gate, up) for k in range(KD)]
        return np.concatenate(cols + [down[:, c * P:(c + 1) * P].T for c in range(HID // P)], axis=1)

    ctxT = a["ctx_768"].reshape(BATCH * SKV, CTXD).T

    def wo(w):
        return np.ascontiguousarray(w.reshape(HP, P, DIM))

    arrays = {
        "x": np.ascontiguousarray(a["x"].reshape(TOK, DIM)),
        "ctx_top": np.ascontiguousarray(ctxT[:P]),
        "ctx_bot": np.ascontiguousarray(np.concatenate([ctxT[P:], ctxT[P:]], axis=0)),
        "attention0": pairs(a["L0_xattn_w_q"], a["L0_xattn_w_k"], a["L0_xattn_w_v"]),
        "out0": wo(a["L0_xattn_w_o"]), "out_bias0": np.ascontiguousarray(a["L0_xattn_b_o"]),
        "router0": router(a["L0_ffn_gate_weight"]), "router_bias0": np.ascontiguousarray(a["L0_ffn_e_score_correction_bias"]),
        "experts0": np.ascontiguousarray(np.stack(packed0)),
        "attention1": pairs(a["L1_xattn_Wq"], a["L1_xattn_Wk"], a["L1_xattn_Wv"]),
        "out1": wo(a["L1_xattn_Wo"]), "out_bias1": np.ascontiguousarray(a["L1_xattn_bo"]),
        "router1": router(a["L1_ffn_router"]),
        "sorted1": np.ascontiguousarray(np.stack([sorted_expert(g, u, d) for g, u, d in
                                                  zip(a["L1_ffn_gate"], a["L1_ffn_up"], a["L1_ffn_down"])])),
        "experts1": np.ascontiguousarray(np.stack(packed1)),
    }
    nc = bacc.Bacc("TRN2", target_bir_lowering=False, num_devices=1)
    d = {n: nc.dram_tensor(f"in_{n}", v.shape, mybir.dt.from_np(v.dtype), kind="ExternalInput").ap() for n, v in arrays.items()}
    out = nc.dram_tensor("out", (TOK, DIM), F32, kind="ExternalOutput").ap()
    layers = [{n: d.get(f"{n}{i}") for n in ("attention", "out", "out_bias", "router", "router_bias", "experts", "sorted")} for i in range(2)]
    build(nc, d["x"], d["ctx_top"], d["ctx_bot"], layers, out)
    r = run_bass_kernel_spmd(nc, [{f"in_{n}": v for n, v in arrays.items()}], core_ids=[0])
    return r.results[0]["out"].reshape(BATCH, SEQ, DIM)
```

```python
import concourse.bass as bass
from concourse import mybir
from contextlib import ExitStack

F32 = mybir.dt.float32
F32R = mybir.dt.float32r
I32 = mybir.dt.int32
ALU = mybir.AluOpType
ACT = mybir.ActivationFunctionType
AX = mybir.AxisListType
ds = bass.ds

P = 128
BATCH, SEQ, DIM = 4, 512, 256
SKV, CTXD = 1024, 192
HEADS, DH = 16, 64
TOK = BATCH * SEQ
NT = TOK // P
KD = DIM // P
HP = HEADS // 2
QT = SEQ // P
KVT = SKV // P
WCOL = (KD + 4) * P
MCOL = 2 * KD * P + DIM
BANK = 512
BLK = TOK // BANK
SCALE = DH ** -0.5
ORDER = ["K0", "P6", 0, 1, "K1", 2, "P7", 3, "V0", 4, "Q", 5, "V1", 6, 7, "V2", "V3"]
LATE = 2
EPS = 1e-5

LAYERS = [
    dict(experts=32, per=1, shared=2, groups=8, top_groups=4, top=6, scale=2.5),
    dict(experts=8, per=4, shared=4, groups=0, top_groups=0, top=1, scale=1.0),
]
SORTED = LAYERS[1]
TILES = NT + SORTED["experts"] - 1
HID = SORTED["per"] * P
ECOL = 2 * KD * HID + SORTED["per"] * DIM


def build(nc, x, ctx_top, ctx_bot, layer_in, out):
    stack = ExitStack()

    def scope():
        return ExitStack()

    with stack:
        def sb(where, name, shape, dt=F32):
            return where.enter_context(nc.sbuf_tensor(name, shape, dt))

        def sems(where, prefix, names):
            return {n: where.enter_context(nc.semaphore(f"{prefix}_{n}")) for n in names.split()}

        ident = sb(stack, "ident", [P, P])
        ones = sb(stack, "ones", [P, DH])
        xnT_hi = sb(stack, "xnT_hi", [P, KD, TOK], F32R)
        xnT_lo = sb(stack, "xnT_lo", [P, KD, TOK], F32R)
        xres = sb(stack, "xres", [P, NT, DIM])
        ctx_scope = stack.enter_context(scope())
        ctx_hi = sb(ctx_scope, "ctx_hi", [P, BATCH * SKV], F32R)
        ctx_lo = sb(ctx_scope, "ctx_lo", [P, BATCH * SKV], F32R)
        ctx_hl = sb(ctx_scope, "ctx_hl", [P, BATCH * SKV], F32R)
        sorted_x = nc.dram_tensor("sorted_x", (TILES * P, DIM), F32, kind="Internal").ap()
        sorted_y = nc.dram_tensor("sorted_y", (TILES * P, DIM), F32, kind="Internal").ap()
        psum = stack.enter_context(nc.psum_tensor("psum", [P, 8 * BANK], F32))
        x_tiles = x.rearrange("(t p) d -> p t d", p=P)
        out_tiles = out.rearrange("(t p) d -> p t d", p=P)

        def bank(n, width=BANK):
            return psum[:, n * BANK:n * BANK + width]

        def norm_phase(tag, xres, source=None, keep=None, wipe=None, clear=(), prefetch=None):
            NG = NT // 2
            NCH = 2 * BATCH
            with scope() as s:
                stats = sb(s, tag + "stats", [P, NT, 6])
                mean = sb(s, tag + "mean", [P, NT])
                var = sb(s, tag + "var", [P, NT])
                dif = sb(s, tag + "dif", [P, NT])
                std = sb(s, tag + "std", [P, NT])
                rstd = sb(s, tag + "rstd", [P, NT])
                shift = sb(s, tag + "shift", [P, NT])
                if keep is None:
                    xn, xn_groups = sb(s, tag + "xn", [P, 2, 2, DIM]), 2
                else:
                    xn, xn_groups = keep[:, :, :].rearrange("p (g i) d -> p g i d", i=2), NG
                if source is not None:
                    stage = sb(s, tag + "stage", [P, NCH, SKV])
                if wipe is not None:
                    zeros = sb(s, tag + "zeros", [P, DIM])
                sem = sems(s, tag, "stat batch sqrt xn_even xn_odd tr hi lo"
                           + (" x0 x1 id chi clo " + " ".join(f"staged{n}" for n in range(NCH)) if source is not None else "")
                           + (" zero wiped" if wipe is not None else ""))
                with nc.Block() as block:

                    def chunk(n):
                        return slice((n % BATCH) * SKV, (n % BATCH + 1) * SKV)

                    def group_bank(g):
                        return bank(g % 2).rearrange("p (k t) -> p k t", k=KD)

                    @block.sync
                    def _(sp):
                        if source is not None:
                            for half in range(2):
                                tiles = slice(half * NG, (half + 1) * NG)
                                sp.dma_start(xres[:, tiles, :], source[:, tiles, :]).then_inc(sem[f"x{half}"], 16)
                            for n in range(NCH):
                                src = ctx_top if n < BATCH else ctx_bot
                                sp.dma_start(stage[:, n, :], src[:, chunk(n)]).then_inc(sem[f"staged{n}"], 16)
                        if prefetch is not None:
                            prefetch(sp)
                        if wipe is not None:
                            sp.wait_ge(sem["zero"], 1)
                            sp.dma_start(wipe.rearrange("(t p) d -> p t d", p=P),
                                         zeros[:, :].unsqueeze(1).broadcast_to([P, wipe.shape[0] // P, DIM])).then_inc(sem["wiped"], 16)
                            sp.wait_ge(sem["wiped"], 16)

                    @block.gpsimd
                    def _(pool):
                        for used in clear:
                            pool.sem_clear(used)
                        if wipe is not None:
                            nc.gpsimd.memset(zeros[:, :], 0.0).then_inc(sem["zero"], 1)
                        if source is not None:
                            nc.gpsimd.memset(ident[:, :], 0.0).then_inc(sem["id"], 1)
                            nc.gpsimd.memset(ones[:, :], 1.0).then_inc(sem["id"], 1)
                            pool.wait_ge(sem["id"], 2)
                            nc.gpsimd.affine_select(out=ident[:, :], in_=ident[:, :], compare_op=ALU.not_equal, fill=1.0, base=0,
                                                    pattern=[[-1, P]], channel_multiplier=1).then_inc(sem["id"], 1)
                            for n in range(NCH):
                                pool.wait_ge(sem["chi"], n + 1)
                                if n == BATCH:
                                    pool.wait_ge(sem["clo"], n)
                                part, hi, lo = (slice(0, P), ctx_hi, ctx_lo) if n < BATCH else (slice(DH, P), ctx_hl, ctx_hl)
                                nc.gpsimd.tensor_tensor(lo[part, chunk(n)], stage[part, n, :], hi[part, chunk(n)], ALU.subtract)\
                                    .then_inc(sem["clo"], 1)

                    @block.scalar
                    def _(act):
                        def context(n):
                            act.wait_ge(sem[f"staged{n}"], 16)
                            dst = ctx_hi if n < BATCH else ctx_hl
                            nc.scalar.activation(dst[:, chunk(n)], stage[:, n, :], ACT.Copy).then_inc(sem["chi"], 1)

                        def normalise(g):
                            t = 2 * g + 1
                            if g >= xn_groups:
                                act.wait_ge(sem["tr"], g - 1)
                            nc.scalar.activation(xn[:, g % xn_groups, 1, :], xres[:, t, :], ACT.Identity,
                                                 bias=shift[:, t:t + 1], scale=rstd[:, t:t + 1]).then_inc(sem["xn_odd"], 1)

                        early = 2 if source is not None else 0
                        for n in range(early):
                            context(n)
                        act.wait_ge(sem["batch"], 8)
                        nc.scalar.activation(std[:, :], var[:, :], ACT.Sqrt).then_inc(sem["sqrt"], 1)
                        act.wait_ge(sem["batch"], 14)
                        normalise(0)
                        for g in range(NG):
                            if g + 1 < NG:
                                normalise(g + 1)
                            act.wait_ge(sem["tr"], g + 1)
                            nc.scalar.activation(xnT_hi[:, :, 2 * g * P:2 * (g + 1) * P], group_bank(g), ACT.Copy)\
                                .then_inc(sem["hi"], 1)
                            if source is not None and early + g < NCH:
                                context(early + g)

                    @block.tensor
                    def _(pe):
                        if source is not None:
                            pe.wait_ge(sem["id"], 3)
                        for g in range(NG):
                            pe.wait_ge(sem["xn_even"], g + 1)
                            pe.wait_ge(sem["xn_odd"], g + 1)
                            if g >= 2:
                                pe.wait_ge(sem["lo"], g - 1)
                            for t in range(2):
                                for k in range(KD):
                                    last = nc.tensor.transpose(group_bank(g)[:, k, t * P:(t + 1) * P],
                                                               xn[:, g % xn_groups, t, k * P:(k + 1) * P], ident[:, :])
                            last.then_inc(sem["tr"], 1)

                    @block.vector
                    def _(dve):
                        for t in range(NT):
                            if source is not None and t % NG == 0:
                                dve.wait_ge(sem[f"x{t // NG}"], 16)
                            nc.vector.bn_stats(stats[:, t, :], xres[:, t, :]).then_inc(sem["stat"], 1)
                        dve.wait_ge(sem["stat"], NT)
                        n = 0

                        def link(ins):
                            nonlocal n
                            n += 1
                            ins.then_inc(sem["batch"], 1)
                            dve.wait_ge(sem["batch"], n)

                        me, se, mo, so = (stats[:, :, i] for i in (1, 2, 4, 5))
                        link(nc.vector.tensor_tensor(mean[:, :], me, mo, ALU.add))
                        link(nc.vector.tensor_scalar(mean[:, :], mean[:, :], 0.5, None, ALU.mult))
                        link(nc.vector.tensor_tensor(dif[:, :], me, mo, ALU.subtract))
                        link(nc.vector.tensor_tensor(dif[:, :], dif[:, :], dif[:, :], ALU.mult))
                        link(nc.vector.tensor_scalar(dif[:, :], dif[:, :], DIM / 4.0, None, ALU.mult))
                        link(nc.vector.tensor_tensor(var[:, :], se, so, ALU.add))
                        link(nc.vector.tensor_tensor(var[:, :], var[:, :], dif[:, :], ALU.add))
                        link(nc.vector.tensor_scalar(var[:, :], var[:, :], 1.0 / DIM, EPS, ALU.mult, ALU.add))
                        dve.wait_ge(sem["sqrt"], 1)
                        link(nc.vector.reciprocal(rstd[:, :], std[:, :]))
                        link(nc.vector.tensor_tensor(dif[:, :], var[:, :], rstd[:, :], ALU.mult))
                        link(nc.vector.tensor_tensor(dif[:, :], dif[:, :], rstd[:, :], ALU.mult))
                        link(nc.vector.tensor_scalar(dif[:, :], dif[:, :], -0.5, 1.5, ALU.mult, ALU.add))
                        link(nc.vector.tensor_tensor(rstd[:, :], rstd[:, :], dif[:, :], ALU.mult))
                        link(nc.vector.scalar_tensor_tensor(shift[:, :], mean[:, :], -1.0, rstd[:, :], ALU.mult, ALU.mult))

                        def normalise(g):
                            if g >= xn_groups:
                                dve.wait_ge(sem["tr"], g - 1)
                            t = 2 * g
                            nc.vector.tensor_scalar(xn[:, g % xn_groups, 0, :], xres[:, t, :], mean[:, t:t + 1],
                                                    rstd[:, t:t + 1], ALU.subtract, ALU.mult).then_inc(sem["xn_even"], 1)

                        normalise(0)
                        for g in range(NG):
                            if g + 1 < NG:
                                normalise(g + 1)
                            dve.wait_ge(sem["hi"], g + 1)
                            cols = slice(2 * g * P, 2 * (g + 1) * P)
                            nc.vector.tensor_tensor(xnT_lo[:, :, cols], group_bank(g), xnT_hi[:, :, cols], ALU.subtract)\
                                .then_inc(sem["lo"], 1)

        attention_sems = sems(stack, "a", "raw wo bias biased whi wlo one proj hi lo vh v score max mt mrow qk exp acc "
                                          "total inv pv norm out ocopy added")

        def attention_phase(tag, weights, wo, bias, xres):
            with scope() as s:
                raw = sb(s, tag + "raw", [P, WCOL])
                w_split = sb(s, tag + "w_split", [P, 2, WCOL], F32R)
                w_hi, w_lo = w_split[:, 0, :], w_split[:, 1, :]
                wo_sb = sb(s, tag + "wo", [P, DIM])
                k_hl = sb(s, tag + "k_hl", [P, 2, 2, SKV], F32R)
                k_hs = sb(s, tag + "k_hs", [P, 2, 2, SKV], F32R)
                q_hh = sb(s, tag + "q_hh", [P, 2, 2, SEQ], F32R)
                q_lm = sb(s, tag + "q_lm", [P, 2, 2, SEQ], F32R)
                v = sb(s, tag + "v", [P, 2, KVT, P])
                probs = sb(s, tag + "probs", [P, 2, KVT, SEQ])
                psums = sb(s, tag + "psums", [P, 2, SEQ])
                row_max = sb(s, tag + "row_max", [P, QT, P])
                inv = sb(s, tag + "inv", [P, SEQ])
                o_sb = inv
                out_sb = sb(s, tag + "out_sb", [P, 2, 2 * DIM])
                bias_sb = inv[:, 0:DIM]
                sem = attention_sems
                with nc.Block() as block:
                    O, TOTAL = bank(4), bank(5)
                    PIECES = ["K0", "K1", "V0", "Q", "V1", "V2", "V3"]
                    RING = dict(K0=7, K1=6, V0=7, Q=6, V1=7, V2=6, V3=7, OUT0=6, OUT1=7, MT=6)
                    NP = len(PIECES)
                    VALUES = ["V0", "V1", "V2", "V3"]
                    NV = len(VALUES)
                    LOWS = ["K0", "K1", "Q"]
                    HEAD = [slice(0, DH), slice(DH, P)]

                    def slot(n):
                        return psum[:, (n % 2) * 2 * BANK:(n % 2) * 2 * BANK + 2 * BANK]

                    def halves(piece):
                        return bank(RING[piece]).rearrange("p (n w d) -> p n w d", n=2, w=2)

                    WQ = [slice(k * P, (k + 1) * P) for k in range(KD)]
                    WK = [slice((KD + k) * P, (KD + k + 1) * P) for k in range(2)]
                    WV = [slice((KD + 2 + k) * P, (KD + 3 + k) * P) for k in range(2)]

                    def half_of(piece):
                        n = int(piece[1])
                        return slice(n * BANK, (n + 1) * BANK)

                    def run(eng, segment):
                        segment(0, 0, first=True)
                        with eng.Fori(0, HP - 1) as hp:
                            for b in range(1, BATCH + 1):
                                segment(hp, b)
                        for b in range(1, BATCH):
                            segment(HP - 1, b, ahead=b < BATCH - 1)

                    @block.sync
                    def _(sp):
                        sp.dma_start(raw[:, :], weights[0, :, :]).then_inc(sem["raw"], 16)
                        sp.dma_start(bias_sb, bias.partition_broadcast(P)).then_inc(sem["bias"], 16)
                        sp.dma_start(wo_sb[:, :], wo[0, :, :]).then_inc(sem["wo"], 16)
                        with sp.Fori(0, HP - 1) as hp:
                            sp.wait_ge(sem["wlo"], hp + 1)
                            sp.dma_start(raw[:, :], weights[ds(hp + 1, 1), :, :].rearrange("a p c -> (a p) c"))\
                                .then_inc(sem["raw"], 16)
                            sp.wait_ge(sem["out"], hp * (2 * BATCH) + 2 * BATCH)
                            sp.dma_start(wo_sb[:, :], wo[ds(hp + 1, 1), :, :].rearrange("a p c -> (a p) c"))\
                                .then_inc(sem["wo"], 16)

                    @block.gpsimd
                    def _(pool):
                        for par in range(2):
                            for h in range(2):
                                nc.gpsimd.memset(k_hs[DH:DH + 1, par, h, :].bitcast(F32), 1.0).then_inc(sem["one"], 1)
                        pool.wait_ge(sem["one"], 4)
                        nc.gpsimd.memset(row_max[:, :, :], 0.0).then_inc(sem["one"], 1)
                        pool.wait_ge(sem["one"], 5)
                        pool.wait_ge(sem["bias"], 16)
                        for t in range(NT):
                            nc.gpsimd.tensor_tensor(xres[:, t, :], xres[:, t, :], bias_sb, ALU.add).then_inc(sem["biased"], 1)

                        def accumulate(hp, b):
                            i = hp * BATCH
                            n = 0
                            for kv in range(1, KVT):
                                for h in range(2):
                                    pool.wait_ge(sem["exp"], i * 8 + (8 * b + 2 * (kv // 2) + h + 1))
                                    if kv > 1:
                                        pool.wait_ge(sem["acc"], i * (2 * KVT - 2) + ((2 * KVT - 2) * b + n - 1))
                                    a = probs[:, h, 0, :] if kv == 1 else psums[:, h, :]
                                    nc.gpsimd.tensor_tensor(psums[:, h, :], a, probs[:, h, kv, :], ALU.add).then_inc(sem["acc"], 1)
                                    n += 1

                        def add_output(hp, b):
                            o = hp * (2 * BATCH)
                            for half in range(2):
                                t = (b % BATCH) * QT + 2 * half
                                rows = xres[:, t:t + 2, :].rearrange("p t d -> p (t d)")
                                pool.wait_ge(sem["ocopy"], o + (2 * b + half + 3))
                                pool.wait_ge(sem["added"], o + (2 * b + half + 3))
                                nc.gpsimd.tensor_tensor(rows, out_sb[:, half, :], rows, ALU.add).then_inc(sem["added"], 1)

                        def segment(hp, b, first=False, ahead=True):
                            accumulate(hp, b)
                            if not first:
                                add_output(hp, b - 1)

                        pool.wait_ge(sem["biased"], NT)
                        pool.sem_inc(sem["added"], 2 * BATCH + 2)
                        run(pool, segment)
                        add_output(HP - 1, BATCH - 1)

                    @block.scalar
                    def _(act):
                        def split_weights(hp):
                            act.wait_ge(sem["raw"], hp * 16 + 16)
                            nc.scalar.activation(w_hi, raw[:, :], ACT.Copy).then_inc(sem["whi"], 1)

                        def evacuate(piece, hp, b):
                            i, par = hp * BATCH, b % 2
                            src = bank(RING[piece])
                            act.wait_ge(sem["proj"], i * NP + (NP * b + PIECES.index(piece) + 1))
                            if piece in VALUES:
                                n = VALUES.index(piece)
                                nc.scalar.activation(v[:, par, 2 * n:2 * n + 2, :], halves(piece)[:, :, 0, :], ACT.Copy)\
                                    .then_inc(sem["vh"], 1)
                                return
                            if piece in ("K0", "K1"):
                                for h in range(2):
                                    last = nc.scalar.activation(k_hl[0:DH, par, h, half_of(piece)], src[HEAD[h], :], ACT.Copy)
                            else:
                                for h in range(2):
                                    last = nc.scalar.activation(q_hh[0:DH, par, h, :], src[HEAD[h], :], ACT.Copy)
                            last.then_inc(sem["hi"], 1)

                        def max_rows(hp, b):
                            i, par = hp * BATCH, b % 2
                            act.wait_ge(sem["mt"], i + (b + 1))
                            for h in range(2):
                                nc.scalar.activation(q_lm[DH:DH + 1, par, h, :], bank(RING["MT"])[32 * h:32 * h + 1, :],
                                                     ACT.Copy, scale=-1.0).then_inc(sem["mrow"], 1)

                        def exps(hp, b, p):
                            i, h, kp = hp * BATCH, p % 2, p // 2
                            act.wait_ge(sem["qk"], i * 8 + (8 * b + p + 1))
                            nc.scalar.activation(probs[:, h, 2 * kp:2 * kp + 2, :],
                                                 slot(p).rearrange("p (n q) -> p n q", n=2), ACT.Exp, scale=SCALE)\
                                .then_inc(sem["exp"], 1)

                        def copy_output(hp, b):
                            o = hp * (2 * BATCH)
                            for half in range(2):
                                act.wait_ge(sem["out"], o + (2 * b + half + 1))
                                act.wait_ge(sem["added"], o + (2 * b + half + 1 + 2 * BATCH))
                                nc.scalar.activation(out_sb[:, half, :], bank(RING[f"OUT{half}"]), ACT.Copy).then_inc(sem["ocopy"], 1)

                        def segment(hp, b, first=False, ahead=True):
                            for what in ORDER:
                                if isinstance(what, int):
                                    exps(hp, b, what)
                                elif ahead and what in PIECES:
                                    evacuate(what, hp, b + 1)
                            if b == BATCH - 2 and not isinstance(hp, int):
                                act.wait_ge(sem["proj"], hp * (NP * BATCH) + NP * BATCH)
                                split_weights(hp + 1)
                            if not first:
                                copy_output(hp, b - 1)
                            if ahead:
                                max_rows(hp, b + 1)

                        act.sem_inc(sem["ocopy"], 2)
                        split_weights(0)
                        for piece in PIECES:
                            evacuate(piece, 0, 0)
                        max_rows(0, 0)
                        run(act, segment)
                        copy_output(HP - 1, BATCH - 1)

                    @block.vector
                    def _(dve):
                        dve.sem_inc(sem["norm"], 1)
                        dve.sem_inc(sem["inv"], 1)

                        def split_weights(hp):
                            dve.wait_ge(sem["whi"], hp + 1)
                            nc.vector.tensor_tensor(w_lo, raw[:, :], w_hi, ALU.subtract).then_inc(sem["wlo"], 1)

                        def low_parts(piece, hp, b):
                            i, par = hp * BATCH, b % 2
                            src = bank(RING[piece])
                            dve.wait_ge(sem["hi"], i * 3 + (3 * b + LOWS.index(piece) + 1))
                            for h in range(2):
                                if piece == "Q":
                                    nc.vector.tensor_tensor(q_lm[0:DH, par, h, :], src[HEAD[h], :],
                                                            q_hh[0:DH, par, h, :], ALU.subtract)
                                    last = nc.vector.tensor_copy(q_hh[DH:P, par, h, :], q_hh[0:DH, par, h, :])
                                else:
                                    cols = half_of(piece)
                                    nc.vector.tensor_tensor(k_hl[DH:P, par, h, cols], src[HEAD[h], :],
                                                            k_hl[0:DH, par, h, cols], ALU.subtract)
                                    last = nc.vector.tensor_copy(k_hs[0:DH, par, h, cols], k_hl[0:DH, par, h, cols])
                            last.then_inc(sem["lo"], 1)

                        def values(piece, hp, b):
                            i, par, n = hp * BATCH, b % 2, VALUES.index(piece)
                            dst = v[:, par, 2 * n:2 * n + 2, :]
                            dve.wait_ge(sem["vh"], i * NV + (NV * b + n + 1))
                            nc.vector.tensor_tensor(dst, halves(piece)[:, :, 1, :], dst, ALU.add).then_inc(sem["v"], 1)

                        def maximum(hp, b, t):
                            i = hp * BATCH
                            dve.wait_ge(sem["score"], i * 8 + (8 * b + t + 1))
                            col = 32 * (t % 2)
                            nc.vector.reduce_max(row_max[:, t // 2, col:col + 1], slot(t), axis=AX.X).then_inc(sem["max"], 1)

                        def invert(hp, b):
                            i = hp * BATCH
                            dve.wait_ge(sem["total"], i + (b + 1))
                            nc.vector.reciprocal(inv[:, :], TOTAL).then_inc(sem["inv"], 1)

                        def normalise(hp, b):
                            i = hp * BATCH
                            dve.wait_ge(sem["inv"], i + (b + 2))
                            dve.wait_ge(sem["pv"], i + (b + 1))
                            nc.vector.tensor_tensor(o_sb[:, :], O, inv[:, :], ALU.mult).then_inc(sem["norm"], 1)

                        def leave(piece, hp, b):
                            (values if piece in VALUES else low_parts)(piece, hp, b)

                        def segment(hp, b, first=False, ahead=True):
                            if not first:
                                invert(hp, b - 1)
                            for piece in PIECES:
                                if ahead:
                                    leave(piece, hp, b + 1)
                                if piece == "Q" and not first:
                                    normalise(hp, b - 1)
                            if b == BATCH - 2 and not isinstance(hp, int):
                                split_weights(hp + 1)
                            for t in range(8):
                                if ahead:
                                    maximum(hp, b + 1, t)

                        split_weights(0)
                        for piece in PIECES:
                            leave(piece, 0, 0)
                        for t in range(8):
                            maximum(0, 0, t)
                        run(dve, segment)
                        invert(HP - 1, BATCH - 1)
                        normalise(HP - 1, BATCH - 1)

                    @block.tensor
                    def _(pe):
                        def split_product(dst, terms):
                            for n, (w, m) in enumerate(terms):
                                last = nc.tensor.matmul(dst, w, m, start=n == 0, stop=n == len(terms) - 1)
                            return last

                        def project(piece, hp, b, first=False):
                            i, batch = hp * BATCH, b % BATCH
                            dst = bank(RING[piece])
                            if piece in ("K0", "K1"):
                                if piece == "K0":
                                    if batch == 0:
                                        pe.wait_ge(sem["wlo"], hp + (b // BATCH + 1))
                                    if not first:
                                        pe.wait_ge(sem["v"], i * NV + NV * b)
                                        if b > 1:
                                            pe.wait_ge(sem["ocopy"], i * 2 + 2 * (b - 1))
                                elif not first:
                                    pe.wait_ge(sem["mrow"], i * 2 + 2 * b)
                                cols = slice(batch * SKV + half_of(piece).start, batch * SKV + half_of(piece).stop)
                                last = split_product(dst, [(w_hi[:, WK[0]], ctx_hi[:, cols]), (w_hi[:, WK[0]], ctx_lo[:, cols]),
                                                           (w_lo[:, WK[0]], ctx_hi[:, cols]), (w_hi[:, WK[1]], ctx_hl[:, cols]),
                                                           (w_lo[:, WK[1]], ctx_hl[:, cols])])
                            elif piece == "Q":
                                pe.wait_ge(sem["lo"], i * 3 + (3 * b + 2))
                                rows = slice(batch * SEQ, (batch + 1) * SEQ)
                                terms = []
                                for k in range(KD):
                                    terms += [(w_hi[:, WQ[k]], xnT_hi[:, k, rows]), (w_hi[:, WQ[k]], xnT_lo[:, k, rows]),
                                              (w_lo[:, WQ[k]], xnT_hi[:, k, rows])]
                                last = split_product(dst, terms)
                            else:
                                if piece == "V0":
                                    pe.wait_ge(sem["lo"], i * 3 + (3 * b + 1))
                                elif piece == "V2":
                                    pe.wait_ge(sem["lo"], i * 3 + (3 * b + 3))
                                else:
                                    pe.wait_ge(sem["v"], i * NV + (NV * b + (1 if piece == "V1" else 2)))
                                for n in range(2):
                                    col = batch * SKV + (2 * VALUES.index(piece) + n) * P
                                    keys = slice(col, col + P)
                                    both = dst[:, n * 2 * P:(n + 1) * 2 * P].rearrange("p (w d) -> p w d", w=2)
                                    nc.tensor.matmul(both, ctx_hi[:, keys], w_split[:, :, WV[0]], start=True, stop=False)
                                    nc.tensor.matmul(both, ctx_hl[:, keys], w_split[:, :, WV[1]], start=False, stop=False)
                                    last = nc.tensor.matmul(both[:, 0, :], ctx_lo[:, keys], w_hi[:, WV[0]], start=False, stop=True)
                            last.then_inc(sem["proj"], 1)

                        def score(hp, b, t, first=False):
                            i, par, h, qt = hp * BATCH, b % 2, t % 2, t // 2
                            if t == 0:
                                pe.wait_ge(sem["lo"], i * 3 + (3 * b + 3))
                            if t >= 2:
                                pe.wait_ge(sem["max"], i * 8 + (8 * b + t - 1))
                            elif not first:
                                pe.wait_ge(sem["exp"], i * 8 + (8 * b + t - 1))
                            for half in range(2):
                                last = nc.tensor.matmul(slot(t)[:, half * BANK:(half + 1) * BANK],
                                                        q_hh[:, par, h, qt * P:(qt + 1) * P],
                                                        k_hl[:, par, h, half * BANK:(half + 1) * BANK], start=True, stop=True)
                            last.then_inc(sem["score"], 1)

                        def transpose_max(hp, b):
                            i = hp * BATCH
                            pe.wait_ge(sem["max"], i * 8 + (8 * b + 8))
                            for qt in range(QT):
                                last = nc.tensor.transpose(bank(RING["MT"])[:, qt * P:(qt + 1) * P], row_max[:, qt, :], ident[:, :])
                            last.then_inc(sem["mt"], 1)

                        def qk(hp, b, p):
                            i, par, h, kp = hp * BATCH, b % 2, p % 2, p // 2
                            if p == 0:
                                pe.wait_ge(sem["mrow"], i * 2 + (2 * b + 2))
                            if p < 2:
                                pe.wait_ge(sem["max"], i * 8 + (8 * b + 7 + p))
                            else:
                                pe.wait_ge(sem["exp"], i * 8 + (8 * b + p - 1))
                            for n in range(2):
                                keys = slice((2 * kp + n) * P, (2 * kp + n + 1) * P)
                                dst = slot(p)[:, n * BANK:(n + 1) * BANK]
                                nc.tensor.matmul(dst, k_hl[:, par, h, keys], q_hh[:, par, h, :], start=True, stop=False)
                                last = nc.tensor.matmul(dst, k_hs[0:DH + 1, par, h, keys], q_lm[0:DH + 1, par, h, :],
                                                        start=False, stop=True)
                            last.then_inc(sem["qk"], 1)

                        def pv(hp, b, kv):
                            i, par = hp * BATCH, b % 2
                            if kv == 0:
                                pe.wait_ge(sem["norm"], i + (b + 1))
                            if kv % 2 == 0:
                                pe.wait_ge(sem["v"], i * NV + (NV * b + kv // 2 + 1))
                                pe.wait_ge(sem["exp"], i * 8 + (8 * b + kv + 2))
                            for h in range(2):
                                last = nc.tensor.matmul(O[HEAD[h], :], v[:, par, kv, HEAD[h]], probs[:, h, kv, :],
                                                        start=kv == 0, stop=kv == KVT - 1)
                            if kv == KVT - 1:
                                last.then_inc(sem["pv"], 1)

                        def total(hp, b):
                            i = hp * BATCH
                            pe.wait_ge(sem["acc"], i * (2 * KVT - 2) + (2 * KVT - 2) * (b + 1))
                            pe.wait_ge(sem["inv"], i + (b + 1))
                            for h in range(2):
                                last = nc.tensor.matmul(TOTAL[HEAD[h], :], ones[:, :], psums[:, h, :], start=True, stop=True)
                            last.then_inc(sem["total"], 1)

                        def output(hp, b, half, ahead=True):
                            i = hp * BATCH
                            if half == 0:
                                pe.wait_ge(sem["norm"], i + (b + 2))
                                pe.wait_ge(sem["wo"], (hp + b // BATCH) * 16 + 16)
                                if ahead:
                                    pe.wait_ge(sem["v"], i * NV + (NV * (b + 3) - 1))
                            elif ahead:
                                pe.wait_ge(sem["v"], i * NV + NV * (b + 3))
                            if not ahead:
                                pe.wait_ge(sem["ocopy"], i * 2 + (2 * b + half + 1))
                            for n in range(2):
                                t = 2 * half + n
                                last = nc.tensor.matmul(bank(RING[f"OUT{half}"])[:, n * DIM:(n + 1) * DIM],
                                                        o_sb[:, t * P:(t + 1) * P], wo_sb[:, :], start=True, stop=True)
                            last.then_inc(sem["out"], 1)

                        def segment(hp, b, first=False, ahead=True):
                            for what in ORDER:
                                if isinstance(what, int):
                                    qk(hp, b, what)
                                elif what in PIECES:
                                    if ahead:
                                        project(what, hp, b + 1)
                                elif not first:
                                    pv(hp, b - 1, int(what[1]))
                            for t in range(8):
                                if ahead:
                                    score(hp, b + 1, t)
                                if not first and t >= 6:
                                    output(hp, b - 1, t - 6, ahead)
                                if t < KVT - LATE:
                                    pv(hp, b, t)
                            total(hp, b)
                            if ahead:
                                if not first:
                                    pe.wait_ge(sem["ocopy"], hp * (2 * BATCH) + (2 * b + 1))
                                transpose_max(hp, b + 1)

                        pe.wait_ge(sem["one"], 5)
                        for piece in PIECES:
                            project(piece, 0, 0, first=True)
                        for t in range(8):
                            score(0, 0, t, first=True)
                        transpose_max(0, 0)
                        run(pe, segment)
                        for kv in range(KVT - LATE, KVT):
                            pv(HP - 1, BATCH - 1, kv)
                        for half in range(2):
                            output(HP - 1, BATCH - 1, half, ahead=False)

        expert_sems = sems(stack, "e", "rt pad ready rhi rlo logits copied turned scores step bias const picked counted taken placed "
                                       "raw0 raw1 whi wlo gu silu mul hhi hlo down fma")

        def expert_phase(tag, cfg, router, bias, packed, xres, dispatch=None, prefetch=None):
            E, per, G = cfg["experts"], cfg["per"], cfg["groups"]
            chunks = cfg["shared"] + (E * per if dispatch is None else 0)
            with scope() as s:
                raw = sb(s, tag + "raw", [P, 2, MCOL])
                w_hi = sb(s, tag + "w_hi", [P, 2, MCOL], F32R)
                w_lo = sb(s, tag + "w_lo", [P, 2, MCOL], F32R)
                act_g = sb(s, tag + "act_g", [P, 2, BANK])
                hid = sb(s, tag + "hid", [P, 2, BANK])
                hid_hi = sb(s, tag + "hid_hi", [P, 4, BANK], F32R)
                hid_lo = sb(s, tag + "hid_lo", [P, 4, BANK], F32R)
                rt = sb(s, tag + "rt", [P, KD, E])
                rt_hi, rt_lo = (hid_lo[:, n, 0:KD * P].rearrange("p (k e) -> p k e", k=KD) for n in (0, 1))
                logits_T = [buffer[0:E, n, :] for buffer in (act_g, hid) for n in range(2)]
                weights_of = sb(s, tag + "weights_of", [P, chunks * NT])
                scores, eq, gt, sel, start = (sb(s, tag + n, [P, NT, E]) for n in ("scores", "eq", "gt", "sel", "start"))
                top = sb(s, tag + "top", [P, NT, 8])
                need = sb(s, tag + "need", [P, NT])
                if G:
                    choice = sb(s, tag + "choice", [P, NT, E])
                    bias_sb = sb(s, tag + "rbias", [P, E])
                    gmax, geq, ggt, gsel, gstart = (sb(s, tag + n, [P, NT, G]) for n in ("gmax", "geq", "ggt", "gsel", "gstart"))
                if dispatch is not None:
                    rows, slot_of, expert_of = dispatch
                    index, slots, tile_expert = (sb(s, tag + n, [P, n_]) for n, n_ in
                                                 (("index", TILES), ("slots", NT), ("tile_expert", TILES)))
                    held, upto, over = (a[:, :, :].rearrange("p t e -> p (t e)").rearrange("p (e t) -> p e t", e=E)
                                        for a in (eq, scores, start))
                    tiles, end = (sb(s, tag + n, [P, E]) for n in ("tiles", "end"))
                    past = sb(s, tag + "past", [P, TILES, E])
                    earlier = sb(s, tag + "earlier", [P, P])
                    every = past[:, 0:P // E, :].rearrange("p t e -> p (t e)")
                sem = expert_sems
                sent = [s.enter_context(nc.semaphore(f"{tag}sent{n}")) for n in range(NT)] if dispatch else []
                UNITS = chunks * BLK
                ROUND = 2 * BLK
                ROUNDS = UNITS // ROUND
                TB = NT // BLK
                with nc.Block() as block:

                    def run(eng, unit, done=0):
                        for u in range(done, 2):
                            unit(0, u)
                        with eng.Fori(0, ROUNDS - 1) as j:
                            for u in range(2, ROUND + 2):
                                unit(j, u)
                        for u in range(2, ROUND):
                            unit(ROUNDS - 1, u)

                    def rest(eng, unit):
                        done = cfg["shared"] * BLK
                        first = -(-(done - 2) // ROUND)
                        for u in range(done, min(first * ROUND + 2, UNITS)):
                            unit((u - 2) // ROUND, (u - 2) % ROUND + 2)
                        if first < ROUNDS - 1:
                            with eng.Fori(first, ROUNDS - 1) as j:
                                for u in range(2, ROUND + 2):
                                    unit(j, u)
                        if done < UNITS:
                            for u in range(2, ROUND):
                                unit(ROUNDS - 1, u)

                    @block.sync
                    def _(sp):
                        sp.dma_start(rt[:, :, :], router).then_inc(sem["rt"], 16)
                        if G:
                            sp.dma_start(bias_sb[:, :], bias.partition_broadcast(P)).then_inc(sem["bias"], 16)
                        with sp.Fori(0, chunks // 2) as j:
                            for par in range(2):
                                sp.wait_ge(sem["wlo"], j * 2 + (par + 1))
                                sp.dma_start(raw[:, par, :], packed[ds(j * 2 + par, 1), :, :].rearrange("a p c -> (a p) c"))\
                                    .then_inc(sem[f"raw{par}"], 16)
                        if prefetch is not None:
                            prefetch(sp)

                    @block.gpsimd
                    def _(pool):
                        pool.sem_inc(sem["wlo"], 2)
                        for part in (rt_hi, rt_lo):
                            nc.gpsimd.memset(part.bitcast(F32), 0.0).then_inc(sem["pad"], 1)
                        if dispatch is not None:
                            nc.gpsimd.memset(every, 1.0).then_inc(sem["const"], 1)
                            pool.wait_ge(sem["const"], 1)
                            nc.gpsimd.affine_select(out=earlier[:, :], in_=every, compare_op=ALU.is_gt, fill=0.0, base=0,
                                                    pattern=[[1, P]], channel_multiplier=-1).then_inc(sem["const"], 1)
                        with pool.Fori(0, chunks // 2) as j:
                            for par in range(2):
                                pool.wait_ge(sem["whi"], j * 2 + (par + 1))
                                nc.gpsimd.tensor_tensor(w_lo[:, par, :], raw[:, par, :], w_hi[:, par, :], ALU.subtract)\
                                    .then_inc(sem["wlo"], 1)
                        if dispatch is not None:
                            pool.wait_ge(sem["placed"], 1)
                            for t in range(NT):
                                nc.gpsimd.indirect_dma_start(sorted_x, bass.IndirectOffsetOnAxis(ap=slot_of[:, t:t + 1], axis=0),
                                                             rows[:, t, :], None).then_inc(sent[t], 16)
                            for done in sent:
                                pool.wait_ge(done, 16)

                    @block.scalar
                    def _(act):
                        def split(j, c):
                            act.wait_ge(sem[f"raw{c % 2}"], j * 16 + 16 * (c // 2 + 1))
                            nc.scalar.activation(w_hi[:, c % 2, :], raw[:, c % 2, :], ACT.Copy).then_inc(sem["whi"], 1)

                        def unit(j, u):
                            k = j * ROUND
                            if u % BLK == 2 and not (isinstance(j, int) and j == ROUNDS - 1 and u == ROUND - 2):
                                c = u // BLK + 1
                                act.wait_ge(sem["down"], k + BLK * c)
                                split(j, c)
                            act.wait_ge(sem["gu"], k + (u + 1))
                            act.wait_ge(sem["mul"], k + (u + 1))
                            nc.scalar.activation(act_g[:, u % 2, :], bank(u % 2), ACT.Silu).then_inc(sem["silu"], 1)
                            act.wait_ge(sem["mul"], k + (u + 3))
                            act.wait_ge(sem["down"], k + (u + 1))
                            nc.scalar.activation(hid_hi[:, u % 4, :], hid[:, u % 2, :], ACT.Copy).then_inc(sem["hhi"], 1)

                        act.wait_ge(sem["rt"], 16)
                        act.wait_ge(sem["pad"], 2)
                        nc.scalar.activation(rt_hi[:, :, 0:E], rt[:, :, :], ACT.Copy).then_inc(sem["rhi"], 1)
                        split(0, 0)
                        for blk in range(BLK):
                            act.wait_ge(sem["logits"], blk + 1)
                            nc.scalar.activation(logits_T[blk], bank(blk)[0:E, :], ACT.Copy).then_inc(sem["copied"], 1)
                        act.wait_ge(sem["turned"], 1)
                        nc.scalar.activation(scores[:, :, :], bank(BLK, NT * E).rearrange("p (t e) -> p t e", e=E),
                                             ACT.Sigmoid if G else ACT.Copy).then_inc(sem["scores"], 1)
                        run(act, unit)

                    @block.vector
                    def _(dve):
                        dve.sem_inc(sem["mul"], 2)
                        dve.sem_inc(sem["fma"], 4)

                        def add(j, u):
                            k = j * ROUND
                            dve.wait_ge(sem["down"], k + (u + 5))
                            dve.wait_ge(sem["fma"], k + (u + 1))
                            for n in range(TB):
                                t = (u % BLK) * TB + n
                                acc = xres[:, t, :]
                                last = nc.vector.scalar_tensor_tensor(
                                    acc, bank(4 + 2 * (u % 2) + n // 2)[:, (n % 2) * DIM:(n % 2 + 1) * DIM],
                                    weights_of[:, ds(j * (2 * NT) + ((u // BLK) * NT + t), 1)], acc, ALU.mult, ALU.add)
                            last.then_inc(sem["fma"], 1)

                        def unit(j, u):
                            k = j * ROUND
                            dve.wait_ge(sem["silu"], k + (u + 1))
                            nc.vector.tensor_tensor(hid[:, u % 2, :], bank(2 + u % 2), act_g[:, u % 2, :], ALU.mult)\
                                .then_inc(sem["mul"], 1)
                            if u >= 2:
                                add(j, u - 2)
                            dve.wait_ge(sem["hhi"], k + (u + 1))
                            nc.vector.tensor_tensor(hid_lo[:, u % 4, :], hid[:, u % 2, :], hid_hi[:, u % 4, :], ALU.subtract)\
                                .then_inc(sem["hlo"], 1)

                        steps = 0

                        def link(ins):
                            nonlocal steps
                            steps += 1
                            ins.then_inc(sem["step"], 1)
                            dve.wait_ge(sem["step"], steps)

                        def flat(a):
                            return a.rearrange("p t n -> p (t n)")

                        def wide(a, n):
                            return a.unsqueeze(2).broadcast_to([P, NT, n])

                        def pick(v, k, n, eq, gt, sel, start):
                            link(nc.vector.memset(start[:, :, :], 1.0))
                            link(nc.vector.memset(start[:, :, 0:1], 0.0))
                            for t in range(NT):
                                last = nc.vector.max(top[:, t, :], v[:, t, :])
                            link(last)
                            if G:
                                yield
                            kth = top[:, :, k - 1:k].broadcast_to([P, NT, n])
                            link(nc.vector.tensor_tensor(gt[:, :, :], v[:, :, :], kth, ALU.is_gt))
                            link(nc.vector.tensor_tensor(eq[:, :, :], v[:, :, :], kth, ALU.is_equal))
                            link(nc.vector.reduce_sum(need[:, :], gt[:, :, :], axis=AX.X))
                            link(nc.vector.tensor_scalar(need[:, :], need[:, :], -1.0, float(k), ALU.mult, ALU.add))
                            if G:
                                yield
                            link(nc.vector.tensor_tensor_scan(flat(sel[:, :, :]), flat(start[:, :, :]), flat(eq[:, :, :]), 0.0,
                                                              ALU.mult, ALU.add))
                            link(nc.vector.tensor_tensor(sel[:, :, :], sel[:, :, :], wide(need[:, :], n), ALU.is_le))
                            link(nc.vector.tensor_tensor(eq[:, :, :], eq[:, :, :], sel[:, :, :], ALU.mult))
                            link(nc.vector.tensor_tensor(sel[:, :, :], gt[:, :, :], eq[:, :, :], ALU.add))

                        def sort_tokens():
                            nc.vector.memset(start[:, :, 0:1], 0.0).then_inc(sem["picked"], 1)
                            link(nc.vector.memset(index[:, :], 1.0))
                            link(nc.vector.tensor_tensor_scan(tile_expert[:, :], index[:, :], index[:, :], 0.0, ALU.mult, ALU.add))
                            link(nc.vector.tensor_scalar(index[:, :], tile_expert[:, :], -1.0, None, ALU.add))
                            link(nc.vector.memset(over[:, :, :], 1.0))
                            link(nc.vector.memset(over[:, :, 0:1], 0.0))
                            yield
                            dve.wait_ge(sem["counted"], 1)
                            link(nc.vector.tensor_copy(held[:, :, :], bank(0)[:, NT * E:2 * NT * E].rearrange("p (t e) -> p e t", e=E)))
                            nc.vector.tensor_copy(gt[:, :, :], bank(0, NT * E).rearrange("p (t e) -> p t e", e=E))\
                                .then_inc(sem["taken"], 1)
                            dve.wait_ge(sem["taken"], 1)
                            yield
                            link(nc.vector.tensor_tensor_scan(upto[:, :, :].rearrange("p e t -> p (e t)"),
                                                              over[:, :, :].rearrange("p e t -> p (e t)"),
                                                              held[:, :, :].rearrange("p e t -> p (e t)"), 0.0, ALU.mult, ALU.add))
                            link(nc.vector.tensor_scalar(tiles[:, :], upto[:, :, NT - 1], 1.0 / P, None, ALU.mult))
                            link(nc.vector.tensor_tensor(over[:, :, :], tiles[:, :].unsqueeze(2).broadcast_to([P, E, NT]),
                                                         index[:, 0:NT].unsqueeze(1).broadcast_to([P, E, NT]), ALU.is_gt))
                            link(nc.vector.reduce_sum(tiles[:, :], over[:, :, :], axis=AX.X))
                            link(nc.vector.memset(need[:, 0:E], 1.0))
                            link(nc.vector.tensor_tensor_scan(end[:, :], need[:, 0:E], tiles[:, :], 0.0, ALU.mult, ALU.add))
                            yield
                            link(nc.vector.tensor_tensor(past[:, :, :], end[:, :].unsqueeze(1).broadcast_to([P, TILES, E]),
                                                         index[:, :].unsqueeze(2).broadcast_to([P, TILES, E]), ALU.is_le))
                            link(nc.vector.reduce_sum(tile_expert[:, :], past[:, :, :], axis=AX.X))
                            link(nc.vector.tensor_scalar(expert_of[:, :], tile_expert[:, :], E - 1.0, None, ALU.min))
                            yield
                            link(nc.vector.tensor_tensor(tiles[:, :], end[:, :], tiles[:, :], ALU.subtract))
                            link(nc.vector.tensor_scalar(tiles[:, :], tiles[:, :], float(P), None, ALU.mult))
                            link(nc.vector.tensor_tensor(upto[:, :, :], upto[:, :, :], held[:, :, :], ALU.subtract))
                            link(nc.vector.tensor_tensor(upto[:, :, :], upto[:, :, :],
                                                         tiles[:, :].unsqueeze(2).broadcast_to([P, E, NT]), ALU.add))
                            link(nc.vector.tensor_tensor(gt[:, :, :], gt[:, :, :],
                                                         upto[:, :, :].rearrange("p e t -> p t e"), ALU.add))
                            link(nc.vector.tensor_tensor(gt[:, :, :], gt[:, :, :], sel[:, :, :], ALU.mult))
                            link(nc.vector.reduce_sum(slots[:, :], gt[:, :, :], axis=AX.X))
                            nc.vector.tensor_copy(slot_of[:, :], slots[:, :]).then_inc(sem["placed"], 1)

                        def choose():
                            dve.wait_ge(sem["scores"], 1)
                            if G:
                                dve.wait_ge(sem["bias"], 16)
                                link(nc.vector.tensor_tensor(choice[:, :, :], scores[:, :, :],
                                                             bias_sb[:, :].unsqueeze(1).broadcast_to([P, NT, E]), ALU.add))
                                link(nc.vector.reduce_max(flat(gmax[:, :, :]), flat(choice[:, :, :])
                                                          .rearrange("p (g m) -> p g m", m=E // G), axis=AX.X))
                                yield from pick(gmax, cfg["top_groups"], G, geq, ggt, gsel, gstart)
                                link(nc.vector.tensor_tensor(
                                    flat(choice[:, :, :]).rearrange("p (g m) -> p g m", m=E // G),
                                    flat(choice[:, :, :]).rearrange("p (g m) -> p g m", m=E // G),
                                    flat(gsel[:, :, :]).unsqueeze(2).broadcast_to([P, NT * G, E // G]), ALU.mult))
                                yield
                                yield from pick(choice, cfg["top"], E, eq, gt, sel, start)
                                yield
                                link(nc.vector.tensor_tensor(sel[:, :, :], sel[:, :, :], scores[:, :, :], ALU.mult))
                                link(nc.vector.reduce_sum(need[:, :], sel[:, :, :], axis=AX.X))
                                yield
                                link(nc.vector.tensor_scalar(need[:, :], need[:, :], 1e-20, None, ALU.add))
                                link(nc.vector.reciprocal(need[:, :], need[:, :]))
                                link(nc.vector.tensor_scalar(need[:, :], need[:, :], cfg["scale"], None, ALU.mult))
                                link(nc.vector.tensor_tensor(sel[:, :, :], sel[:, :, :], wide(need[:, :], E), ALU.mult))
                            else:
                                yield from pick(scores, cfg["top"], E, eq, gt, sel, start)
                            first = cfg["shared"] * NT
                            if dispatch is not None:
                                yield from sort_tokens()
                            for c in range(per if dispatch is None else 0):
                                link(nc.vector.tensor_copy(
                                    weights_of[:, first:].rearrange("p (e c t) -> p c t e", c=per, t=NT)[:, c, :, :], sel[:, :, :]))

                        dve.wait_ge(sem["rhi"], 1)
                        nc.vector.tensor_tensor(rt_lo[:, :, 0:E], rt[:, :, :], rt_hi[:, :, 0:E], ALU.subtract).then_inc(sem["rlo"], 1)
                        link(nc.vector.memset(weights_of[:, 0:cfg["shared"] * NT], 1.0))
                        choosing = choose()
                        for u in range(cfg["shared"] * BLK):
                            next(choosing, None)
                            unit(u // ROUND, u % ROUND) if u < 2 else unit((u - 2) // ROUND, (u - 2) % ROUND + 2)
                        for _ in choosing:
                            pass
                        rest(dve, unit)
                        add(ROUNDS - 1, ROUND - 2)
                        add(ROUNDS - 1, ROUND - 1)

                    @block.tensor
                    def _(pe):
                        pe.sem_inc(sem["down"], 4)

                        def gate_up(j, u):
                            k, par = j * ROUND, (u // BLK) % 2
                            rows = slice((u % BLK) * BANK, (u % BLK + 1) * BANK)
                            if u % BLK == 0:
                                pe.wait_ge(sem["wlo"], j * 2 + (u // BLK + 3))
                            pe.wait_ge(sem["mul"], k + (u + 1))
                            for g in range(2):
                                n = 0
                                for kd in range(KD):
                                    w = slice((g * KD + kd) * P, (g * KD + kd + 1) * P)
                                    for a, m in ((w_hi, xnT_hi), (w_hi, xnT_lo), (w_lo, xnT_hi)):
                                        last = nc.tensor.matmul(bank(2 * g + u % 2), a[:, par, w], m[:, kd, rows],
                                                                start=n == 0, stop=n == 3 * KD - 1)
                                        n += 1
                            last.then_inc(sem["gu"], 1)

                        def down(j, u):
                            k, par = j * ROUND, (u // BLK) % 2
                            w = slice(2 * KD * P, MCOL)
                            pe.wait_ge(sem["hlo"], k + (u + 1))
                            pe.wait_ge(sem["fma"], k + (u + 3))
                            for n in range(TB):
                                dst = bank(4 + 2 * (u % 2) + n // 2)[:, (n % 2) * DIM:(n % 2 + 1) * DIM]
                                rows = slice(n * P, (n + 1) * P)
                                for m, (a, b) in enumerate(((hid_hi, w_hi), (hid_hi, w_lo), (hid_lo, w_hi))):
                                    last = nc.tensor.matmul(dst, a[:, u % 4, rows], b[:, par, w], start=m == 0, stop=m == 2)
                            last.then_inc(sem["down"], 1)

                        def unit(j, u):
                            gate_up(j, u)
                            if u >= 2:
                                down(j, u - 2)

                        def count():
                            pe.wait_ge(sem["const"], 2)
                            pe.wait_ge(sem["mul"], 3)
                            pe.wait_ge(sem["picked"], 1)
                            picked = sel[:, :, :].rearrange("p t e -> p (t e)")
                            nc.tensor.matmul(bank(0)[:, 0:NT * E], earlier[:, :], picked, start=True, stop=True)
                            nc.tensor.matmul(bank(0)[:, NT * E:2 * NT * E], every, picked, start=True, stop=True)\
                                .then_inc(sem["counted"], 1)
                            pe.wait_ge(sem["taken"], 1)

                        pe.wait_ge(sem["rlo"], 1)
                        for blk in range(BLK):
                            block_rows = slice(blk * BANK, (blk + 1) * BANK)
                            n = 0
                            for k in range(KD):
                                for w, a in ((rt_hi, xnT_hi), (rt_hi, xnT_lo), (rt_lo, xnT_hi)):
                                    last = nc.tensor.matmul(bank(blk), w[:, k, :], a[:, k, block_rows], start=n == 0, stop=n == 3 * KD - 1)
                                    n += 1
                            last.then_inc(sem["logits"], 1)
                        for t in range(NT):
                            blk, n = divmod(t, NT // BLK)
                            pe.wait_ge(sem["copied"], blk + 1)
                            last = nc.tensor.transpose(bank(BLK)[:, t * E:(t + 1) * E], logits_T[blk][:, n * P:(n + 1) * P],
                                                       ident[0:E, 0:E])
                        last.then_inc(sem["turned"], 1)
                        unit(0, 0)
                        unit(0, 1)
                        if dispatch is not None:
                            count()
                        pe.wait_ge(sem["scores"], 1)
                        run(pe, unit, 2)
                        down(ROUNDS - 1, ROUND - 2)
                        down(ROUNDS - 1, ROUND - 1)

        def sorted_phase(tag, weights, loaded, place, rows, xres, store):
            slot_of, expert_of = place
            per = HID // P
            assert 2 * KD * HID == TOK and KD == 2
            x_slots = sorted_x.rearrange("(t p) d -> t p d", p=P)
            y_slots = sorted_y.rearrange("(t p) d -> t p d", p=P)
            with scope() as s:
                xs = sb(s, tag + "xs", [P, 2, DIM])
                xsT_hi = sb(s, tag + "xsT_hi", [P, 2, KD * P], F32R)
                xsT_lo = sb(s, tag + "xsT_lo", [P, 2, KD * P], F32R)
                gated = sb(s, tag + "gated", [P, 2, HID])
                hid = sb(s, tag + "hid", [P, 2, HID])
                hidT_hi = sb(s, tag + "hidT_hi", [P, 2, HID], F32R)
                hidT_lo = sb(s, tag + "hidT_lo", [P, 2, HID], F32R)
                GATE_UP, DOWN = 2 * KD * HID, per * DIM
                gu_hi, gu_lo = xnT_hi, xnT_lo
                down_hi = sb(s, tag + "down_hi", [P, 2, DOWN], F32R)
                down_lo = sb(s, tag + "down_lo", [P, 2, DOWN], F32R)
                y = sb(s, tag + "y", [P, 2, DIM])
                sem = sems(s, tag, "xs0 xs1 xt xhi xlo ghi glo dhi dlo gu silu mul ht hhi hlo down ycopy y0 y1 sum out")
                back = [s.enter_context(nc.semaphore(f"{tag}back{n}")) for n in range(NT)]
                OUTS = 4
                LOOP = (TILES - 4) // 2
                with nc.Block() as block:

                    def there(r, u):
                        return not isinstance(r, int) or 0 <= 2 * r + u < TILES

                    def run(eng, step):
                        for u in (-1, 0, 1, 2):
                            step(0, u)
                        with eng.Fori(0, LOOP) as r:
                            for u in (3, 4):
                                step(r, u)
                        for u in range(3, TILES + 3 - 2 * LOOP):
                            step(LOOP, u)

                    def expert(eng, r, u):
                        e = eng.value_load(expert_of[0:1, ds(r * 2 + u, 1)], min_val=0, max_val=SORTED["experts"] - 1)
                        return lambda cols: weights[:, ds(e, 1), cols].rearrange("p a c -> p (a c)")

                    GATE_UP_HALVES = slice(0, GATE_UP // 2), slice(GATE_UP // 2, GATE_UP)
                    DOWN_COLS = slice(GATE_UP, ECOL)

                    def tile(a, r, u):
                        return a[ds(r * 2 + u, 1), :, :].rearrange("a p d -> (a p) d")

                    @block.sync
                    def _(sp):
                        def load(r, u):
                            sp.wait_ge(sem["xt"], r * 2 + (u + 1))
                            sp.dma_start(xs[:, u % 2, :], tile(x_slots, r, u)).then_inc(sem[f"xs{u % 2}"], 16)

                        with sp.Fori(0, TILES // 2) as r:
                            for u in range(2):
                                load(r, u)
                        for u in range(TILES % 2):
                            load(TILES // 2, u)
                        n = NT // OUTS
                        for part in range(OUTS):
                            sp.wait_ge(sem["sum"], n * (part + 1))
                            sp.dma_start(store[:, part * n:(part + 1) * n, :], xres[:, part * n:(part + 1) * n, :])\
                                .then_inc(sem["out"], 16)
                            sp.wait_ge(sem["out"], 16 * (part + 1))

                    @block.gpsimd
                    def _(pool):
                        def step(r, u):
                            if there(r, u - 1):
                                w = expert(nc.gpsimd, r, u - 1)
                                pool.wait_ge(sem["dhi"], r * 2 + u)
                                nc.gpsimd.tensor_tensor(down_lo[:, (u - 1) % 2, :], w(DOWN_COLS), down_hi[:, (u - 1) % 2, :],
                                                        ALU.subtract).then_inc(sem["dlo"], 1)

                        run(pool, step)
                        for par in range(2):
                            pool.wait_ge(sem[f"y{par}"], 16 * ((TILES + 1 - par) // 2 + 1))
                        for t in range(NT):
                            nc.gpsimd.indirect_dma_start(rows[:, t, :], None, sorted_y,
                                                         bass.IndirectOffsetOnAxis(ap=slot_of[:, t:t + 1], axis=0))\
                                .then_inc(back[t], 16)

                    @block.scalar
                    def _(act):
                        for par in range(2):
                            act.sem_inc(sem[f"y{par}"], 16)
                        for part in loaded:
                            act.wait_ge(part, 16)

                        def step(r, u):
                            k = r * 2
                            if there(r, u + 1):
                                par = (u + 1) % 2
                                act.wait_ge(sem["xt"], k + (u + 4))
                                act.wait_ge(sem["gu"], k + (u + 2))
                                nc.scalar.activation(xsT_hi[:, par, :], bank(5, KD * P), ACT.Copy).then_inc(sem["xhi"], 1)
                                w = expert(nc.scalar, r, u + 1)
                                for cols in GATE_UP_HALVES:
                                    nc.scalar.activation(gu_hi[:, par, cols], w(cols), ACT.Copy).then_inc(sem["ghi"], 1)
                            if there(r, u):
                                act.wait_ge(sem["gu"], k + (u + 3))
                                act.wait_ge(sem["mul"], k + (u + 1))
                                nc.scalar.activation(gated[:, u % 2, :], bank(u % 2), ACT.Silu).then_inc(sem["silu"], 1)
                            if there(r, u - 1):
                                par = (u - 1) % 2
                                w = expert(nc.scalar, r, u - 1)
                                act.wait_ge(sem["down"], k + u)
                                nc.scalar.activation(down_hi[:, par, :], w(DOWN_COLS), ACT.Copy).then_inc(sem["dhi"], 1)
                                act.wait_ge(sem["ht"], k + (u + 2))
                                nc.scalar.activation(hidT_hi[:, par, :], bank(4), ACT.Copy).then_inc(sem["hhi"], 1)
                            if there(r, u - 3):
                                act.wait_ge(sem["ycopy"], k + u)
                                act.dma_start(tile(y_slots, r, u - 3), y[:, (u - 3) % 2, :]).then_inc(sem[f"y{(u - 3) % 2}"], 16)

                        run(act, step)

                    @block.vector
                    def _(dve):
                        dve.sem_inc(sem["mul"], 2)
                        dve.sem_inc(sem["ycopy"], 2)
                        dve.sem_inc(sem["hlo"], 1)

                        def step(r, u):
                            k = r * 2
                            if there(r, u + 1):
                                par = (u + 1) % 2
                                dve.wait_ge(sem["xhi"], k + (u + 2))
                                nc.vector.tensor_tensor(xsT_lo[:, par, :], bank(5, KD * P), xsT_hi[:, par, :], ALU.subtract)\
                                    .then_inc(sem["xlo"], 1)
                                w = expert(nc.vector, r, u + 1)
                                for n, cols in enumerate(GATE_UP_HALVES):
                                    dve.wait_ge(sem["ghi"], r * 4 + (2 * u + 3 + n))
                                    nc.vector.tensor_tensor(gu_lo[:, par, cols], w(cols), gu_hi[:, par, cols], ALU.subtract)\
                                        .then_inc(sem["glo"], 1)
                            if there(r, u):
                                dve.wait_ge(sem["silu"], k + (u + 1))
                                dve.wait_ge(sem["ht"], k + (u + 1))
                                nc.vector.tensor_tensor(hid[:, u % 2, :], bank(2 + u % 2), gated[:, u % 2, :], ALU.mult)\
                                    .then_inc(sem["mul"], 1)
                            if there(r, u - 1):
                                par = (u - 1) % 2
                                dve.wait_ge(sem["hhi"], k + u)
                                nc.vector.tensor_tensor(hidT_lo[:, par, :], bank(4), hidT_hi[:, par, :], ALU.subtract)\
                                    .then_inc(sem["hlo"], 1)
                            if there(r, u - 2):
                                dve.wait_ge(sem["down"], k + (u + 1))
                                dve.wait_ge(sem[f"y{u % 2}"], r * 16 + 16 * (u // 2))
                                nc.vector.tensor_copy(y[:, u % 2, :], bank(6 + u % 2, DIM)).then_inc(sem["ycopy"], 1)

                        run(dve, step)
                        for t in range(NT):
                            dve.wait_ge(back[t], 16)
                            nc.vector.tensor_tensor(xres[:, t, :], xres[:, t, :], rows[:, t, :], ALU.add).then_inc(sem["sum"], 1)

                    @block.tensor
                    def _(pe):
                        for n in ("xt", "gu", "ht", "down"):
                            pe.sem_inc(sem[n], 2)

                        def step(r, u):
                            k = r * 2
                            if there(r, u + 1):
                                pe.wait_ge(sem[f"xs{(u + 1) % 2}"], r * 16 + 16 * ((u + 1) // 2 + 1))
                                if there(r, u):
                                    pe.wait_ge(sem["xlo"], k + (u + 1))
                                for kd in range(KD):
                                    cols = slice(kd * P, (kd + 1) * P)
                                    last = nc.tensor.transpose(bank(5)[:, cols], xs[:, (u + 1) % 2, cols], ident[:, :])
                                last.then_inc(sem["xt"], 1)
                            if there(r, u):
                                par = u % 2
                                pe.wait_ge(sem["xlo"], k + (u + 1))
                                pe.wait_ge(sem["glo"], r * 4 + (2 * u + 2))
                                pe.wait_ge(sem["mul"], k + (u + 1))
                                for g in range(2):
                                    n = 0
                                    for kd in range(KD):
                                        part = slice(kd * P, (kd + 1) * P)
                                        cols = slice((g * KD + kd) * HID, (g * KD + kd + 1) * HID)
                                        for a, w in ((xsT_hi, gu_hi), (xsT_hi, gu_lo), (xsT_lo, gu_hi)):
                                            last = nc.tensor.matmul(bank(2 * g + par), a[:, par, part], w[:, par, cols],
                                                                    start=n == 0, stop=n == 3 * KD - 1)
                                            n += 1
                                last.then_inc(sem["gu"], 1)
                            if there(r, u - 1):
                                pe.wait_ge(sem["mul"], k + (u + 2))
                                pe.wait_ge(sem["hlo"], k + u)
                                for c in range(per):
                                    cols = slice(c * P, (c + 1) * P)
                                    last = nc.tensor.transpose(bank(4)[:, cols], hid[:, (u - 1) % 2, cols], ident[:, :])
                                last.then_inc(sem["ht"], 1)
                            if there(r, u - 2):
                                par = u % 2
                                pe.wait_ge(sem["hlo"], k + u)
                                pe.wait_ge(sem["dlo"], k + (u - 1))
                                pe.wait_ge(sem["ycopy"], k + (u - 1))
                                n = 0
                                for c in range(per):
                                    part, cols = slice(c * P, (c + 1) * P), slice(c * DIM, (c + 1) * DIM)
                                    for a, w in ((hidT_hi, down_hi), (hidT_hi, down_lo), (hidT_lo, down_hi)):
                                        last = nc.tensor.matmul(bank(6 + par, DIM), a[:, par, part], w[:, par, cols],
                                                                start=n == 0, stop=n == 3 * per - 1)
                                        n += 1
                                last.then_inc(sem["down"], 1)

                        run(pe, step)

        w = layer_in[0]
        cfg = LAYERS[0]
        norm_phase("n_", xres, x_tiles)
        attention_phase("L0a_", w["attention"], w["out"], w["out_bias"], xres)
        norm_phase("L0n_", xres, wipe=sorted_x, clear=attention_sems.values())
        expert_phase("L0e_", cfg, w["router"], w["router_bias"], w["experts"], xres)
        w = layer_in[1]
        cfg = LAYERS[1]
        norm_phase("L1i_", xres, clear=expert_sems.values())
        attention_phase("L1a_", w["attention"], w["out"], w["out_bias"], xres)
        ctx_scope.close()
        with scope() as s:
            place = sb(s, "L1slot_of", [P, NT], I32), sb(s, "L1expert_of", [P, TILES], I32)
            rows = sb(s, "L1rows", [P, NT, DIM])
            weights = sb(s, "L1weights", [P, cfg["experts"], ECOL])
            loaded = [s.enter_context(nc.semaphore(f"L1loaded{n}")) for n in range(2)]
            parts = slice(0, 4), slice(4, cfg["experts"])

            def load(n):
                return lambda sp: sp.dma_start(weights[:, parts[n], :], w["sorted"][parts[n], :, :].rearrange("e p c -> p e c"))\
                    .then_inc(loaded[n], 16)

            norm_phase("L1n_", xres, keep=rows, prefetch=load(0))
            expert_phase("L1e_", cfg, w["router"], None, w["experts"], xres, (rows, *place), load(1))
            sorted_phase("L1s_", weights, loaded, place, rows, xres, out_tiles)


def kernel(**inputs):
    import numpy as np
    import concourse.bacc as bacc
    from concourse.bass_utils import run_bass_kernel_spmd

    a = {k: np.asarray(v) for k, v in inputs.items()}

    def pairs(wq, wk, wv):
        out = []
        for hp in range(HP):
            c = slice(hp * P, (hp + 1) * P)
            cols = [wq[k * P:(k + 1) * P, c] for k in range(KD)]
            for w in (wk, wv):
                cols += [w[:P, c], np.concatenate([w[P:, c], w[P:, c]], axis=0)]
            out.append(np.concatenate(cols, axis=1))
        return np.ascontiguousarray(np.stack(out))

    def chunk(gate, up, down):
        cols = [m[:, k * P:(k + 1) * P].T for m in (gate, up) for k in range(KD)]
        return np.concatenate(cols + [down.T], axis=1)

    def router(w):
        return np.ascontiguousarray(w.T.reshape(KD, P, w.shape[0]).transpose(1, 0, 2))

    H = P
    packed0 = [chunk(a["L0_ffn_shared_gate_w"][c * H:(c + 1) * H], a["L0_ffn_shared_up_w"][c * H:(c + 1) * H],
                     a["L0_ffn_shared_down_w"][:, c * H:(c + 1) * H]) for c in range(LAYERS[0]["shared"])]
    packed0 += [chunk(gu[:H], gu[H:], dn) for gu, dn in zip(a["L0_ffn_experts_gate_up"], a["L0_ffn_experts_down"])]
    packed1 = [chunk(a["L1_ffn_w_gate_s"][c * H:(c + 1) * H], a["L1_ffn_w_up_s"][c * H:(c + 1) * H],
                     a["L1_ffn_w_down_s"][:, c * H:(c + 1) * H]) for c in range(LAYERS[1]["shared"])]

    def sorted_expert(gate, up, down):
        cols = [m[:, k * P:(k + 1) * P].T for m in (gate, up) for k in range(KD)]
        return np.concatenate(cols + [down[:, c * P:(c + 1) * P].T for c in range(HID // P)], axis=1)

    ctxT = a["ctx_768"].reshape(BATCH * SKV, CTXD).T

    def wo(w):
        return np.ascontiguousarray(w.reshape(HP, P, DIM))

    arrays = {
        "x": np.ascontiguousarray(a["x"].reshape(TOK, DIM)),
        "ctx_top": np.ascontiguousarray(ctxT[:P]),
        "ctx_bot": np.ascontiguousarray(np.concatenate([ctxT[P:], ctxT[P:]], axis=0)),
        "attention0": pairs(a["L0_xattn_w_q"], a["L0_xattn_w_k"], a["L0_xattn_w_v"]),
        "out0": wo(a["L0_xattn_w_o"]), "out_bias0": np.ascontiguousarray(a["L0_xattn_b_o"]),
        "router0": router(a["L0_ffn_gate_weight"]), "router_bias0": np.ascontiguousarray(a["L0_ffn_e_score_correction_bias"]),
        "experts0": np.ascontiguousarray(np.stack(packed0)),
        "attention1": pairs(a["L1_xattn_Wq"], a["L1_xattn_Wk"], a["L1_xattn_Wv"]),
        "out1": wo(a["L1_xattn_Wo"]), "out_bias1": np.ascontiguousarray(a["L1_xattn_bo"]),
        "router1": router(a["L1_ffn_router"]),
        "sorted1": np.ascontiguousarray(np.stack([sorted_expert(g, u, d) for g, u, d in
                                                  zip(a["L1_ffn_gate"], a["L1_ffn_up"], a["L1_ffn_down"])])),
        "experts1": np.ascontiguousarray(np.stack(packed1)),
    }
    nc = bacc.Bacc("TRN2", target_bir_lowering=False, num_devices=1)
    d = {n: nc.dram_tensor(f"in_{n}", v.shape, mybir.dt.from_np(v.dtype), kind="ExternalInput").ap() for n, v in arrays.items()}
    out = nc.dram_tensor("out", (TOK, DIM), F32, kind="ExternalOutput").ap()
    layers = [{n: d.get(f"{n}{i}") for n in ("attention", "out", "out_bias", "router", "router_bias", "experts", "sorted")} for i in range(2)]
    build(nc, d["x"], d["ctx_top"], d["ctx_bot"], layers, out)
    r = run_bass_kernel_spmd(nc, [{f"in_{n}": v for n, v in arrays.items()}], core_ids=[0])
    return r.results[0]["out"].reshape(BATCH, SEQ, DIM)
```
